# Optimizing a Trainium2 kernel written in Bass

```python
import numpy as np
import jax
import jax.numpy as jnp

def _softmax(x, axis=-1):
    return jax.nn.softmax(x, axis=axis)

def _gelu(x):
    return jax.nn.gelu(x, approximate=True)

def _silu(x):
    return jax.nn.silu(x)

def _sigmoid(x):
    return jax.nn.sigmoid(x)

def _layernorm(x, axis=-1, eps=1e-05):
    m = jnp.mean(x, axis=axis, keepdims=True)
    v = jnp.var(x, axis=axis, keepdims=True)
    return (x - m) / jnp.sqrt(v + eps)

def _scatter_add(tgt, idx, src, axis=0):
    return tgt.at[idx].add(src)

def _segment_sum(src, seg, n):
    return jax.ops.segment_sum(src, seg, n)
kernel_name = 'mk_decoder_preln_d2_seqx_r8_137bc7'

def setup_inputs(seed: int=0):
    np.random.seed(seed)
    _w = jnp.asarray

    def _rec_inputs():
        import jax
        import jax.numpy as jnp
        _rk = jax.random.key(seed)
        x = 7.22e-05 + 1 * jax.random.normal(jax.random.fold_in(_rk, 1), (2, 256, 128), jnp.float32)
        _lenS = 256 - jax.random.randint(jax.random.fold_in(_rk, 7), (2,), 0, max(1, 256 // 4) + 1, jnp.int32)
        _lenS2 = 512 - jax.random.randint(jax.random.fold_in(_rk, 8), (2,), 0, max(1, 512 // 4) + 1, jnp.int32)
        _ctx_768P = jax.random.normal(jax.random.fold_in(_rk, 11), (2, 16, 96), jnp.float32)
        _ctx_768c = jax.random.dirichlet(jax.random.fold_in(_rk, 511), 0.3 * jnp.ones((16,), jnp.float32), (2, 512))
        _ctx_768t = jnp.einsum('bsk,bkd->bsd', _ctx_768c, _ctx_768P)
        _ctx_768t = _ctx_768t * jax.lax.rsqrt(jnp.mean(jnp.square(_ctx_768t)) + 1e-12) * 0.953939
        ctx_768 = 2.09791e-05 + 1.00001 * (_ctx_768t + 0.3 * jax.random.normal(jax.random.fold_in(_rk, 611), (2, 512, 96), jnp.float32))
        return (x, ctx_768)
    x, ctx_768 = _rec_inputs()

    def _L0_attn_setup():
        import jax, jax.numpy as jnp
        import numpy as np
        B, S, D, H = (4, 256, 128, 16)
        DH = D // H
        key = jax.random.key(seed)
        ks = jax.random.split(key, 5)
        std = 1.0 / np.sqrt(D)
        return {'x': jax.random.normal(ks[0], (B, S, D), dtype=jnp.float32), 'mask': jnp.ones((S, S), dtype=bool), 'Wq': jax.random.normal(ks[1], (D, D), dtype=jnp.float32) * std, 'Wk': jax.random.normal(ks[2], (D, D), dtype=jnp.float32) * std, 'Wv': jax.random.normal(ks[3], (D, D), dtype=jnp.float32) * std, 'Wout': jax.random.normal(ks[4], (D, D), dtype=jnp.float32) * std}
    _L0_attn_all = _L0_attn_setup()
    _L0_attn_in = {k: v for k, v in _L0_attn_all.items() if k in ('mask', 'Wq', 'Wk', 'Wv', 'Wout')}
    del _L0_attn_all

    def _L0_xattn_setup():
        import jax, jax.numpy as jnp
        import numpy as np
        HEADS = 8
        DIM_HEAD = 64
        SCALE = DIM_HEAD ** (-0.5)
        key = jax.random.key(seed)
        ks = jax.random.split(key, 7)
        b, n, m = (4, 256, 128)
        qd, cd, inner = (128, 96, HEADS * DIM_HEAD)
        s = lambda fan_in: 1.0 / np.sqrt(fan_in)
        return {'x': jax.random.normal(ks[0], (b, n, qd), jnp.float32), 'context': jax.random.normal(ks[1], (b, m, cd), jnp.float32), 'Wq': jax.random.normal(ks[2], (qd, inner), jnp.float32) * s(qd), 'Wk': jax.random.normal(ks[3], (cd, inner), jnp.float32) * s(cd), 'Wv': jax.random.normal(ks[4], (cd, inner), jnp.float32) * s(cd), 'Wout': jax.random.normal(ks[5], (inner, qd), jnp.float32) * s(inner), 'bout': jax.random.normal(ks[6], (qd,), jnp.float32) * 0.01}
    _L0_xattn_all = _L0_xattn_setup()
    _L0_xattn_in = {k: v for k, v in _L0_xattn_all.items() if k in ('Wq', 'Wk', 'Wv', 'Wout', 'bout')}
    del _L0_xattn_all

    def _L0_ffn_setup():
        import jax, jax.numpy as jnp
        import numpy as np
        B, N, C, H, REG = (1, 2309, 128, 16, 5)
        D = C // H
        key = jax.random.key(seed)
        k0, k1, k2, k3 = jax.random.split(key, 4)
        x = jax.random.normal(k0, (B, N, C), dtype=jnp.float32)
        g_info = jax.random.normal(k1, (12, 2, C), dtype=jnp.float32)
        W_qkv = jax.random.normal(k2, (C, 3 * C), dtype=jnp.float32) * 0.02
        W_proj = jax.random.normal(k3, (C, C), dtype=jnp.float32) * 0.02
        b_proj = jnp.zeros((C,), dtype=jnp.float32)
        return {'x': x, 'g_info': g_info, 'W_qkv': W_qkv, 'W_proj': W_proj, 'b_proj': b_proj}
    _L0_ffn_all = _L0_ffn_setup()
    _L0_ffn_in = {k: v for k, v in _L0_ffn_all.items() if k in ('g_info', 'W_qkv', 'W_proj', 'b_proj')}
    del _L0_ffn_all

    def _L1_attn_setup():
        import jax, jax.numpy as jnp
        import numpy as np
        B, S, HID, NH = (8, 512, 128, 16)
        D = HID // NH
        LN_EPS = 1e-05

        def _l2norm(a):
            n = jnp.sqrt(jnp.sum(a * a, axis=-1, keepdims=True))
            return a / jnp.maximum(n, 1e-12)
        key = jax.random.key(seed)
        ks = jax.random.split(key, 8)
        s = 0.02
        x = jax.random.normal(ks[0], (B, S, HID), jnp.float32)
        Wq = jax.random.normal(ks[1], (HID, NH * D), jnp.float32) * s
        Wk = jax.random.normal(ks[2], (HID, NH * D), jnp.float32) * s
        Wv = jax.random.normal(ks[3], (HID, NH * D), jnp.float32) * s
        Wbeta = jax.random.normal(ks[4], (HID, NH), jnp.float32) * s
        Wg = jax.random.normal(ks[5], (HID, NH * D), jnp.float32) * s
        Wout = jax.random.normal(ks[6], (NH * D, HID), jnp.float32) * s
        ln_g = jnp.ones((NH * D,), jnp.float32)
        ln_b = jnp.zeros((NH * D,), jnp.float32)
        return {'x': x, 'Wq': Wq, 'Wk': Wk, 'Wv': Wv, 'Wbeta': Wbeta, 'Wg': Wg, 'Wout': Wout, 'ln_g': ln_g, 'ln_b': ln_b}
    _L1_attn_all = _L1_attn_setup()
    _L1_attn_in = {k: v for k, v in _L1_attn_all.items() if k in ('Wq', 'Wk', 'Wv', 'Wbeta', 'Wg', 'Wout', 'ln_g', 'ln_b')}
    del _L1_attn_all

    def _L1_xattn_setup():
        import jax, jax.numpy as jnp
        import numpy as np
        HEADS = 16
        DIM_HEAD = 64
        key = jax.random.key(seed)
        ks = jax.random.split(key, 8)
        B, S, D = (16, 512, 128)
        K, DE = (77, 96)
        inner = HEADS * DIM_HEAD
        hidden_states = jax.random.normal(ks[0], (B, S, D), dtype=jnp.float32)
        encoder_hidden_states = jax.random.normal(ks[1], (B, K, DE), dtype=jnp.float32)
        sc_q = 1.0 / np.sqrt(D)
        sc_kv = 1.0 / np.sqrt(DE)
        sc_o = 1.0 / np.sqrt(inner)
        Wq = jax.random.normal(ks[2], (D, inner), dtype=jnp.float32) * sc_q
        Wk = jax.random.normal(ks[3], (DE, inner), dtype=jnp.float32) * sc_kv
        Wv = jax.random.normal(ks[4], (DE, inner), dtype=jnp.float32) * sc_kv
        Wo = jax.random.normal(ks[5], (inner, D), dtype=jnp.float32) * sc_o
        bo = jax.random.normal(ks[6], (D,), dtype=jnp.float32) * 0.01
        return {'hidden_states': hidden_states, 'encoder_hidden_states': encoder_hidden_states, 'Wq': Wq, 'Wk': Wk, 'Wv': Wv, 'Wo': Wo, 'bo': bo}
    _L1_xattn_all = _L1_xattn_setup()
    _L1_xattn_in = {k: v for k, v in _L1_xattn_all.items() if k in ('Wq', 'Wk', 'Wv', 'Wo', 'bo')}
    del _L1_xattn_all

    def _L1_ffn_setup():
        import jax, jax.numpy as jnp
        import numpy as np
        EPS = 1e-06
        LN_EPS = 1e-05

        def _absmean_core(W):
            gamma = jnp.mean(jnp.abs(W)) + EPS
            Ws = W / gamma
            Wq = jnp.sign(Ws) * jnp.minimum(jnp.round(jnp.abs(Ws)), 1.0)
            return (Wq, gamma)

        @jax.custom_vjp
        def absmean(W):
            return _absmean_core(W)[0]

        def _absmean_fwd(W):
            Wq, gamma = _absmean_core(W)
            return (Wq, gamma)

        def _absmean_bwd(gamma, g):
            return (g / gamma,)
        absmean.defvjp(_absmean_fwd, _absmean_bwd)

        def layernorm(x, w, b, eps=LN_EPS):
            mu = jnp.mean(x, axis=-1, keepdims=True)
            var = jnp.mean((x - mu) ** 2, axis=-1, keepdims=True)
            return (x - mu) * jax.lax.rsqrt(var + eps) * w + b
        key = jax.random.key(seed)
        k1, k2, k3 = jax.random.split(key, 3)
        d, h = (128, 512)
        B, T = (8, 256)
        return {'x': jax.random.normal(k1, (B, T, d), jnp.float32), 'W_fc': jax.random.normal(k2, (h, d), jnp.float32), 'ln_w': jnp.ones((h,), jnp.float32), 'ln_b': jnp.zeros((h,), jnp.float32), 'W_proj': jax.random.normal(k3, (d, h), jnp.float32)}
    _L1_ffn_all = _L1_ffn_setup()
    _L1_ffn_in = {k: v for k, v in _L1_ffn_all.items() if k in ('W_fc', 'ln_w', 'ln_b', 'W_proj')}
    del _L1_ffn_all
    return {'x': x, 'ctx_768': ctx_768, 'L0_attn_mask': _L0_attn_in['mask'], 'L0_attn_Wq': _L0_attn_in['Wq'], 'L0_attn_Wk': _L0_attn_in['Wk'], 'L0_attn_Wv': _L0_attn_in['Wv'], 'L0_attn_Wout': _L0_attn_in['Wout'], 'L0_xattn_Wq': _L0_xattn_in['Wq'], 'L0_xattn_Wk': _L0_xattn_in['Wk'], 'L0_xattn_Wv': _L0_xattn_in['Wv'], 'L0_xattn_Wout': _L0_xattn_in['Wout'], 'L0_xattn_bout': _L0_xattn_in['bout'], 'L0_ffn_g_info': _L0_ffn_in['g_info'], 'L0_ffn_W_qkv': _L0_ffn_in['W_qkv'], 'L0_ffn_W_proj': _L0_ffn_in['W_proj'], 'L0_ffn_b_proj': _L0_ffn_in['b_proj'], 'L1_attn_Wq': _L1_attn_in['Wq'], 'L1_attn_Wk': _L1_attn_in['Wk'], 'L1_attn_Wv': _L1_attn_in['Wv'], 'L1_attn_Wbeta': _L1_attn_in['Wbeta'], 'L1_attn_Wg': _L1_attn_in['Wg'], 'L1_attn_Wout': _L1_attn_in['Wout'], 'L1_attn_ln_g': _L1_attn_in['ln_g'], 'L1_attn_ln_b': _L1_attn_in['ln_b'], 'L1_xattn_Wq': _L1_xattn_in['Wq'], 'L1_xattn_Wk': _L1_xattn_in['Wk'], 'L1_xattn_Wv': _L1_xattn_in['Wv'], 'L1_xattn_Wo': _L1_xattn_in['Wo'], 'L1_xattn_bo': _L1_xattn_in['bo'], 'L1_ffn_W_fc': _L1_ffn_in['W_fc'], 'L1_ffn_ln_w': _L1_ffn_in['ln_w'], 'L1_ffn_ln_b': _L1_ffn_in['ln_b'], 'L1_ffn_W_proj': _L1_ffn_in['W_proj']}

def reference(x, ctx_768, L0_attn_mask, L0_attn_Wq, L0_attn_Wk, L0_attn_Wv, L0_attn_Wout, L0_xattn_Wq, L0_xattn_Wk, L0_xattn_Wv, L0_xattn_Wout, L0_xattn_bout, L0_ffn_g_info, L0_ffn_W_qkv, L0_ffn_W_proj, L0_ffn_b_proj, L1_attn_Wq, L1_attn_Wk, L1_attn_Wv, L1_attn_Wbeta, L1_attn_Wg, L1_attn_Wout, L1_attn_ln_g, L1_attn_ln_b, L1_xattn_Wq, L1_xattn_Wk, L1_xattn_Wv, L1_xattn_Wo, L1_xattn_bo, L1_ffn_W_fc, L1_ffn_ln_w, L1_ffn_ln_b, L1_ffn_W_proj):
    import jax
    import jax.numpy as jnp

    def _L0_attn_ref(x, mask, Wq, Wk, Wv, Wout):
        import jax, jax.numpy as jnp
        import numpy as np
        B, S, D, H = (4, 256, 128, 16)
        DH = D // H
        n, s, d = x.shape
        scale = 1.0 / np.sqrt(DH).astype(np.float32)
        q = (x @ Wq).reshape(n, s, H, DH)
        k = (x @ Wk).reshape(n, s, H, DH)
        v = (x @ Wv).reshape(n, s, H, DH)
        attn = jnp.einsum('nqhd,nkhd->nqkh', q, k) * scale
        attn = jax.nn.softmax(attn, axis=-2)
        z = jnp.einsum('nqkh,nkhd->nqhd', attn, v).reshape(n, s, d)
        z = jnp.einsum('nqd,de->nqe', z, Wout)
        return x + z

    def _L0_xattn_ref(x, context, Wq, Wk, Wv, Wout, bout):
        import jax, jax.numpy as jnp
        import numpy as np
        HEADS = 8
        DIM_HEAD = 64
        SCALE = DIM_HEAD ** (-0.5)
        b, n, _ = x.shape
        m = context.shape[1]
        q = (x @ Wq).reshape(b, n, HEADS, DIM_HEAD)
        k = (context @ Wk).reshape(b, m, HEADS, DIM_HEAD)
        v = (context @ Wv).reshape(b, m, HEADS, DIM_HEAD)
        sim = jnp.einsum('bihd,bjhd->bhij', q, k) * SCALE
        attn = jax.nn.softmax(sim, axis=-1)
        out = jnp.einsum('bhij,bjhd->bihd', attn, v).reshape(b, n, HEADS * DIM_HEAD)
        return out @ Wout + bout

    def _L0_ffn_ref(x, g_info, W_qkv, W_proj, b_proj):
        import jax, jax.numpy as jnp
        import numpy as np
        B, N, C, H, REG = (1, 2309, 128, 16, 5)
        D = C // H
        Bx, Nx, Cx = x.shape
        scale = D ** (-0.5)
        qkv = (x @ W_qkv).reshape(Bx, Nx, 3, H, D)
        q, k, v = (qkv[:, :, 0], qkv[:, :, 1], qkv[:, :, 2])
        g_layer = g_info[0].reshape(-1, H, D)
        q_g = g_layer[0]
        q_pure = q[:, REG:]
        q_n = q_pure / jnp.linalg.norm(q_pure, axis=-1, keepdims=True)
        qg_n = q_g / jnp.linalg.norm(q_g, axis=-1, keepdims=True)
        sim = (qg_n[None, None] * q_n).sum(-1).mean(-1)
        sim = (sim - sim.min()) / (sim.max() - sim.min())
        pos = sim > 0.9
        logits = jnp.einsum('bqhd,bkhd->bhqk', q * scale, k)

        def masked_attn(tok_mask):
            key_mask = jnp.concatenate([jnp.ones((Bx, REG), bool), tok_mask], axis=1)
            l = jnp.where(key_mask[:, None, None, :], logits, -jnp.inf)
            a = jax.nn.softmax(l, axis=-1)
            return jnp.einsum('bhqk,bkhd->bqhd', a, v)
        x_pos = masked_attn(pos)
        x_neg = masked_attn(~pos)
        reg_out = (x_pos[:, :REG] + x_neg[:, :REG]) * 0.5
        tok_out = jnp.where(pos[:, :, None, None], x_pos[:, REG:], x_neg[:, REG:])
        out = jnp.concatenate([reg_out, tok_out], axis=1).reshape(Bx, Nx, Cx)
        return out @ W_proj + b_proj

    def _L1_attn_ref(x, Wq, Wk, Wv, Wbeta, Wg, Wout, ln_g, ln_b):
        import jax, jax.numpy as jnp
        import numpy as np
        B, S, HID, NH = (8, 512, 128, 16)
        D = HID // NH
        LN_EPS = 1e-05

        def _l2norm(a):
            n = jnp.sqrt(jnp.sum(a * a, axis=-1, keepdims=True))
            return a / jnp.maximum(n, 1e-12)
        b, s, _ = x.shape
        nh = Wbeta.shape[1]
        d = Wq.shape[1] // nh
        q = _l2norm((x @ Wq).reshape(b, s, nh, d))
        k = _l2norm((x @ Wk).reshape(b, s, nh, d))
        v = (x @ Wv).reshape(b, s, nh, d)
        beta = jax.nn.sigmoid(x @ Wbeta)
        qT = jnp.moveaxis(q, 1, 0)
        kT = jnp.moveaxis(k, 1, 0)
        vT = jnp.moveaxis(v, 1, 0)
        bT = jnp.moveaxis(beta, 1, 0)
        state0 = jnp.zeros((b, nh, d, d), x.dtype)

        def step(state, inp):
            qt, kt, vt, bt = inp
            kk = kt[..., :, None] * kt[..., None, :]
            bb = bt[..., None, None]
            state = state * (1.0 - bb * kk) + bb * (vt[..., :, None] * kt[..., None, :])
            out_t = jnp.einsum('bhij,bhj->bhi', state, qt)
            return (state, out_t)
        _, outs = jax.lax.scan(step, state0, (qT, kT, vT, bT))
        out = jnp.moveaxis(outs, 0, 1).reshape(b, s, nh * d)
        mu = jnp.mean(out, axis=-1, keepdims=True)
        var = jnp.mean((out - mu) ** 2, axis=-1, keepdims=True)
        out = (out - mu) / jnp.sqrt(var + LN_EPS) * ln_g + ln_b
        out = out * jax.nn.silu(x @ Wg)
        return out @ Wout

    def _L1_xattn_ref(hidden_states, encoder_hidden_states, Wq, Wk, Wv, Wo, bo):
        import jax, jax.numpy as jnp
        import numpy as np
        HEADS = 16
        DIM_HEAD = 64
        B, S, D = hidden_states.shape
        K = encoder_hidden_states.shape[1]
        H, Dh = (HEADS, DIM_HEAD)
        scale = 1.0 / np.sqrt(Dh)
        q = hidden_states @ Wq
        k = encoder_hidden_states @ Wk
        v = encoder_hidden_states @ Wv
        q = q.reshape(B, S, H, Dh).transpose(0, 2, 1, 3)
        k = k.reshape(B, K, H, Dh).transpose(0, 2, 1, 3)
        v = v.reshape(B, K, H, Dh).transpose(0, 2, 1, 3)
        scores = jnp.einsum('bhsd,bhkd->bhsk', q, k) * scale
        probs = jax.nn.softmax(scores, axis=-1)
        out = jnp.einsum('bhsk,bhkd->bhsd', probs, v)
        out = out.transpose(0, 2, 1, 3).reshape(B, S, H * Dh)
        out = out @ Wo + bo
        return out

    def _L1_ffn_ref(x, W_fc, ln_w, ln_b, W_proj):
        import jax, jax.numpy as jnp
        import numpy as np
        EPS = 1e-06
        LN_EPS = 1e-05

        def _absmean_core(W):
            gamma = jnp.mean(jnp.abs(W)) + EPS
            Ws = W / gamma
            Wq = jnp.sign(Ws) * jnp.minimum(jnp.round(jnp.abs(Ws)), 1.0)
            return (Wq, gamma)

        @jax.custom_vjp
        def absmean(W):
            return _absmean_core(W)[0]

        def _absmean_fwd(W):
            Wq, gamma = _absmean_core(W)
            return (Wq, gamma)

        def _absmean_bwd(gamma, g):
            return (g / gamma,)
        absmean.defvjp(_absmean_fwd, _absmean_bwd)

        def layernorm(x, w, b, eps=LN_EPS):
            mu = jnp.mean(x, axis=-1, keepdims=True)
            var = jnp.mean((x - mu) ** 2, axis=-1, keepdims=True)
            return (x - mu) * jax.lax.rsqrt(var + eps) * w + b
        h = jnp.einsum('btd,hd->bth', x, absmean(W_fc))
        h = jax.nn.gelu(h, approximate=False)
        h = layernorm(h, ln_w, ln_b)
        return jnp.einsum('bth,dh->btd', h, absmean(W_proj))
    x = x + _L0_attn_ref(_layernorm(x, axis=-1), L0_attn_mask, L0_attn_Wq, L0_attn_Wk, L0_attn_Wv, L0_attn_Wout)
    x = x + _L0_xattn_ref(_layernorm(x, axis=-1), ctx_768, L0_xattn_Wq, L0_xattn_Wk, L0_xattn_Wv, L0_xattn_Wout, L0_xattn_bout)
    x = x + _L0_ffn_ref(_layernorm(x, axis=-1), L0_ffn_g_info, L0_ffn_W_qkv, L0_ffn_W_proj, L0_ffn_b_proj)
    x = x + _L1_attn_ref(_layernorm(x, axis=-1), L1_attn_Wq, L1_attn_Wk, L1_attn_Wv, L1_attn_Wbeta, L1_attn_Wg, L1_attn_Wout, L1_attn_ln_g, L1_attn_ln_b)
    x = x + _L1_xattn_ref(_layernorm(x, axis=-1), ctx_768, L1_xattn_Wq, L1_xattn_Wk, L1_xattn_Wv, L1_xattn_Wo, L1_xattn_bo)
    x = x + _L1_ffn_ref(_layernorm(x, axis=-1), L1_ffn_W_fc, L1_ffn_ln_w, L1_ffn_ln_b, L1_ffn_W_proj)
    return x

_drawn_inputs = setup_inputs


def setup_inputs(seed=0):
    import zlib

    import numpy as np

    out = dict(_drawn_inputs(seed))
    spreads = {'L0_ffn_b_proj': (0.0, 0.1),
     'L1_attn_ln_g': (1.0, 0.6),
     'L1_attn_ln_b': (0.0, 0.8),
     'L1_ffn_ln_w': (1.0, 0.2),
     'L1_ffn_ln_b': (0.0, 0.1)}
    factors = {'L0_xattn_bout': 8.0,
     'L0_ffn_g_info': 8.0,
     'L0_ffn_W_qkv': 8.0,
     'L0_ffn_W_proj': 8.0,
     'L1_attn_Wq': 4.628,
     'L1_attn_Wk': 4.571,
     'L1_attn_Wv': 4.793,
     'L1_attn_Wbeta': 8.0,
     'L1_attn_Wg': 4.619,
     'L1_attn_Wout': 4.538,
     'L1_xattn_bo': 8.0}
    for name, (base, spread) in spreads.items():
        noise = np.random.default_rng([zlib.crc32(name.encode()), seed]).standard_normal(out[name].shape)
        drawn = base * np.exp(spread * noise) if base else spread * noise
        out[name] = jnp.asarray(drawn.astype(out[name].dtype))
    for name, factor in factors.items():
        out[name] = (out[name] * factor).astype(out[name].dtype)
    return out
```

```python
from contextlib import ExitStack

import numpy as np

import concourse.bass as bass
from concourse import mybir

ALU = mybir.AluOpType
ACT = mybir.ActivationFunctionType
AX = mybir.AxisListType.X
F32 = mybir.dt.float32
F16 = mybir.dt.float16

P = 128
B = 2
S = 256
T = B * S
NT = T // P
D = 128
SC = 512
DC = 96
NC_T = B * SC // P
REG = 5
H16 = 16
LN_EPS = 1e-5
BIG = 32768.0

C_ID, C_G, C_DEN, C_MASK = 0, 128, 256, 384
M_NQ, M_NK, M_BIASK, M_BLK = 0, 1, 2, 3
NCF = C_MASK + 8
R_SEL, R_POS, R_NEG = 0, 8 * 128, 9 * 128
NCH = 10 * 128


def constants():
    c = np.zeros((P, NCF), np.float32)
    p = np.arange(P)
    c[:, C_ID:C_ID + P] = np.eye(P)
    c[:, C_G:C_G + P] = (p[:, None] // 8 == p[None, :] // 8)
    c[:, C_DEN:C_DEN + P] = (p[:, None] == (p[None, :] // 32) * 32 + 8)
    r, row = (p % 32) // 8, p % 32
    m = c[:, C_MASK:]
    m[:, M_NQ] = -1.0 * (r == 1)
    m[:, M_NK] = -1.0 * (r == 2) + 1.0 * (row == 24)
    m[:, M_BIASK] = row == 24
    for j in range(4):
        m[:, M_BLK + j] = p // 32 == j
    half = np.zeros((P, NCH), np.float16)
    for j in range(8):
        half[:, R_SEL + j * P:R_SEL + (j + 1) * P] = p[:, None] == (p[None, :] // 8) * 8 + j
    half[0, R_POS:R_POS + P] = row == 25
    half[0, R_NEG:R_NEG + P] = row == 26
    return c, half


class Phase:

    def __init__(self, name, heads, dh, first_unit, first_slot, first_aux):
        self.name, self.heads, self.dh = name, heads, dh
        self.small = dh == 8
        self.hu = 4 if self.small else 2
        self.U = heads // self.hu
        self.scale = dh ** -0.5
        self.nprep = 2 if self.small else 6
        self.unit0, self.chunk0, self.aux0 = first_unit, first_slot, first_aux
        self.order = []
        self.slots = []
        self.plan()
        self.index = {job: first_aux + i for i, job in enumerate(self.order)}

    def plan(self):
        U = self.U
        prep = lambda u: [("prep", u, i) for i in range(self.nprep)] if u < U else []
        mx = lambda u, a, b: [("max", u, i) for i in range(a, b)] if u < U else []
        turn = lambda u: [("turn", u, 0)] if u < U else []
        self.head = prep(0) + mx(0, 0, 8) + turn(0) + prep(1)
        self.order += self.head
        for s in range(4 * U + 4):
            u, c = divmod(s, 4)
            jobs = []
            if u < U:
                late = prep(u + 2)
                h = len(late) // 2
                jobs = [mx(u + 1, 0, 4), mx(u + 1, 4, 8), turn(u + 1) + late[:h], late[h:]][c]
            self.order += jobs
            ended = lambda k: (s - k) // 2 - 1 if s >= 2 + k and (s - k) % 2 == 0 and (s - k) // 2 - 1 < 2 * U else None
            self.slots.append(dict(
                main=s if s < 4 * U else None,
                pv=s - 1 if 1 <= s <= 4 * U else None,
                aux=jobs,
                norm=ended(0), select=ended(1) if self.small else None,
                norm2=ended(1) if self.small else None))

    def aux_done(self, job):
        return self.index[job] + 1


INPUTS = {
    "x": (B, S, D), "ctx": (B, SC, DC),
    "a_Wq": (D, D), "a_Wk": (D, D), "a_Wv": (D, D), "a_Wo": (D, D),
    "c0_Wq": (D, 512), "c0_Wk": (DC, 512), "c0_Wv": (DC, 512), "c0_Wo": (512, D), "c0_bo": (D,),
    "m_g": (12, 2, D), "m_Wqkv": (D, 3 * D), "m_Wo": (D, D), "m_bo": (D,),
    "d_Wq": (D, D), "d_Wk": (D, D), "d_Wv": (D, D), "d_Wbeta": (D, H16), "d_Wg": (D, D), "d_Wo": (D, D),
    "d_lng": (D,), "d_lnb": (D,),
    "c1_Wq": (D, 1024), "c1_Wk": (DC, 1024), "c1_Wv": (DC, 1024), "c1_Wo": (1024, D), "c1_bo": (D,),
    "f_Wfc": (512, D), "f_lnw": (512,), "f_lnb": (512,), "f_Wpj": (D, 512),
}


def decoder(nc, g, cf, ch, out):
    A0 = Phase("attn0", 16, 8, 0, 0, 0)
    X0 = Phase("cross0", 8, 64, 4, 16, A0.aux0 + len(A0.order))
    F0 = Phase("mixer", 16, 8, 8, 32, X0.aux0 + len(X0.order))
    Y1 = Phase("cross1", 16, 64, 12, 48, F0.aux0 + len(F0.order))
    phases = [A0, X0, F0, Y1]

    with ExitStack() as ctx:
        def sb(name, shape, dt=F32):
            return ctx.enter_context(nc.sbuf_tensor(name, shape, dt))

        sems = {}

        def sem(name):
            if name not in sems:
                sems[name] = ctx.enter_context(nc.semaphore(name))
            return sems[name]

        cst = sb("cst", [P, NCF])
        csth = sb("csth", [P, NCH], F16)
        ident = cst[:, C_ID:C_ID + P]
        head_sum = cst[:, C_G:C_G + P]
        den_row = cst[:, C_DEN:C_DEN + P]

        def col(i):
            return cst[:, C_MASK + i:C_MASK + i + 1]

        ones = sb("ones", [P, P])
        x = sb("x", [P, NT, D])
        xn = sb("xn", [P, NT, D])
        xnT = sb("xnT", [P, T])
        stats = sb("stats", [P, NT, 6])
        mv = sb("mv", [P, NT, 2])
        rstd = sb("rstd", [P, NT])
        rt1 = sb("rt1", [P, NT])
        rt2 = sb("rt2", [P, NT])
        ctxT = sb("ctxT", [DC, NC_T * P])
        wa = {n: sb("wa_" + n, [P, D]) for n in ("q", "k", "v")}
        wqkv = sb("wqkv", [P, 3 * D])
        WR = {(f, n): sb(f"wr_{f}_{n}", [P, 4 * P]) for f in ("attn0", "mixer") for n in "qk"}
        woP = {f: sb(f"wo_{f}", [P, 4, D]) for f in ("attn0", "mixer")}
        wk2 = {"cross0": sb("wk_c0", [DC, 8, 2, 64]), "cross1": sb("wk_c1", [DC, 16, 2, 64])}
        wq2 = {"cross0": sb("wq_c0", [P, 8, 2, 64]), "cross1": sb("wq_c1", [P, 16, 2, 64])}
        wv2 = {"cross0": sb("wv_c0", [DC, 512]), "cross1": sb("wv_c1", [DC, 1024])}
        wo2 = {"cross0": sb("wo_c0", [P, 4, D]), "cross1": sb("wo_c1", [P, 8, D])}
        bias_out = {n: sb("bias_" + n, [P, D]) for n in ("cross0", "mixer", "cross1")}
        K1 = sb("K1", [P, 3, 2, B * SC], F16)
        K2 = sb("K2", [P, 3, 2, B * SC], F16)
        Q1 = sb("Q1", [P, 3, 2, T], F16)
        Q2 = sb("Q2", [P, 3, 2, T], F16)
        Kr = sb("Kr", [P, 4, T], F16)
        Qr = K1[:, :, :, :].rearrange("p r h (j t) -> p r (h j) t", j=2)
        hi = sb("hi", [P, 2, T], F16)
        qn = sb("qn", [P, T], F16)
        V = sb("V", [P, NC_T, 1024])
        V8 = sb("V8", [P, NT, 16, 32])
        Pr = sb("Pr", [P, 2, 1024])
        mx = sb("mx", [P, 2, NT, 4])
        mrow = sb("mrow", [4, 2, T], F16)
        rden = sb("rden", [P, 2, S])
        Zs = sb("Zs", [P, 2, S])
        zn = sb("zn", [P, 8, T])
        qg = sb("qg", [P, D])
        gn = sb("gn", [P, 2, H16])
        n2 = sb("n2", [P, NT * H16])
        dot = sb("dot", [P, NT * H16])
        sim = sb("sim", [P, NT])
        simrow = sb("simrow", [1, B, S])
        posrow = sb("posrow", [1, B, S])
        ext = sb("ext", [1, 4])
        cls_q = sb("cls_q", [1, 2, B, S], F16)
        cls_k = sb("cls_k", [1, 2, B, S], F16)
        negx = sb("negx", [1, B * REG], F16)
        xreg = sb("xreg", [P, B * REG])
        NR = 4 * B * REG
        Qx = sb("Qx", [P, B, 4, 4, REG], F16)
        qxh = sb("qxh", [P, NR], F16)
        qxn = sb("qxn", [P, NR], F16)
        mreg = sb("mreg", [4 * REG, 8])
        PregT = sb("PregT", [P, 16, 4 * REG])
        Zreg = sb("Zreg", [P, NR])
        rreg = sb("rreg", [P, NR])
        wd = {n: sb("wd_" + n, [P, D]) for n in ("q", "k", "v", "g", "o")}
        wbeta = sb("wbeta", [P, H16])
        wbeta8 = sb("wbeta8", [P, H16, 8])
        lng = sb("lng", [P, D])
        lnb = sb("lnb", [P, D])
        wfc = sb("wfc", [P, 4, P])
        wpj = sb("wpj", [P, 512])
        gam = sb("gam", [P, 8])
        fcT = sb("fcT", [P, 4, P], F16)
        pjT = sb("pjT", [P, 4, P], F16)
        lnw1 = sb("lnw1", [P, 512])
        lnb1 = sb("lnb1", [P, 512])
        Vf = V[:, :, :].rearrange("p a b -> p (a b)")

        def room(i, n=1):
            return Vf[:, 512 * i:512 * (i + n)]

        Preg = room(0, 4)[0:4 * REG, :].rearrange("p (a s) -> p a s", a=8)
        ctx_tok = Pr[:, 0, 0:NC_T * DC].rearrange("p (a c) -> p a c", c=DC)

        SCR = ctx.enter_context(nc.psum_tensor("SCR", [P, 4, 512], F32))
        AUX = ctx.enter_context(nc.psum_tensor("AUX", [P, 2, 512], F32))
        ACC = ctx.enter_context(nc.psum_tensor("ACC", [P, 2, 512], F32))

        prep_jobs = [(ph.name, *job[1:]) for ph in phases for job in ph.order if job[0] == "prep"]
        hi_count = {job: i + 1 for i, job in enumerate(prep_jobs)}
        q2_jobs = [j for j in prep_jobs if j[0].startswith("cross") and j[2] >= 4]
        q2_count = {job: i + 1 for i, job in enumerate(q2_jobs)}
        row_count, n_rows = {}, [0, 0]
        for ph in phases:
            for u in range(ph.U):
                gu = ph.unit0 + u
                n_rows[gu % 2] += 16 * ph.hu
                row_count[ph.name, u] = (f"rows_set{gu % 2}", n_rows[gu % 2])


        def d_half(i, part):
            return room(10).bitcast(F16)[:, part * T:(part + 1) * T] if i == 0 else hi[:, part, :]

        def h_half(t, part):
            return room(8 + t % 2).bitcast(F16)[:, part * 512:(part + 1) * 512]

        def split_h(dve, v, t):
            dve.wait_ge(sem("hT_high"), t + 1)
            v.tensor_tensor(h_half(t, 1), AUX[:, t % 2, :], h_half(t, 0), ALU.subtract).then_inc(sem("hT_split"), 1)

        z_count = {(ph.name, a): k * 8 + a + 1 for k, ph in enumerate((A0, F0)) for a in range(8)}

        block = ctx.enter_context(nc.Block())

        @block.sync
        def _(sp):
            def load(dst, src, name, n=1):
                sp.dma_start(dst, src).then_inc(sem(name), 16)

            def bcast(v):
                return v.unsqueeze(0).to_broadcast([P, v.shape[0]])

            load(x[:], g["x"].rearrange("b (t p) d -> p (b t) d", p=P), "x_in")
            load(cst[:], cf, "cst_in")
            for n in "qkv":
                load(wa[n][:], g["a_W" + n], "wa_in")
            load(ctx_tok, g["ctx"].rearrange("b (t p) d -> p (b t) d", p=P), "ctx_in")
            load(csth[:], ch, "csth_in")
            sp.wait_ge(sem("wo_zero"), 2)
            for f, w in (("attn0", "a_Wo"), ("mixer", "m_Wo")):
                for j in range(4):
                    load(woP[f][32 * j:32 * j + 8, :, :],
                         g[w].rearrange("(u j d) n -> j d u n", j=4, d=8)[j], "wo8_in")
            for f, c in (("cross0", "c0"), ("cross1", "c1")):
                h = 8 if f == "cross0" else 16
                for r in range(2):
                    load(wk2[f][:, :, r, :], g[c + "_Wk"].rearrange("k (h d) -> k h d", h=h), f + "_w_in")
                    load(wq2[f][:, :, r, :], g[c + "_Wq"].rearrange("k (h d) -> k h d", h=h), f + "_w_in")
                load(wv2[f][:], g[c + "_Wv"], f + "_w_in")
                load(wo2[f][:], g[c + "_Wo"].rearrange("(u p) n -> p u n", p=P), f + "_w_in")
                load(bias_out[f][:], bcast(g[c + "_bo"]), f + "_w_in")
            load(wqkv[:], g["m_Wqkv"], "wm_in")
            load(qg[:], bcast(g["m_g"][0, 0, :]), "wm_in")
            load(bias_out["mixer"][:], bcast(g["m_bo"]), "wm_in")
            for n in "qkvgo":
                load(wd[n][:], g["d_W" + n], "wd_in")
            load(wbeta[:], g["d_Wbeta"], "wd_in")
            load(lng[:], bcast(g["d_lng"]), "wd_in")
            load(lnb[:], bcast(g["d_lnb"]), "wd_in")
            load(wfc[:], g["f_Wfc"].rearrange("(a p) d -> p a d", p=P), "wf_in")
            load(wpj[:], g["f_Wpj"], "wf_in")
            load(lnw1[:], bcast(g["f_lnw"]), "wf_in")
            load(lnb1[:], bcast(g["f_lnb"]), "wf_in")

            for ph in phases:
                for u in range(ph.U):
                    sp.wait_ge(sem("aux_free"), ph.aux_done(("turn", u, 0)))
                    name, _ = row_count[ph.name, u]
                    for j in range(ph.hu):
                        if ph.small:
                            dst = Qr[32 * j + 24:32 * j + 25, u % 3, j, :]
                        else:
                            if j == 0:
                                sp.wait_ge(sem("q2_done"), q2_count[ph.name, u, 5])
                            dst = Q2[64:65, u % 3, j, :]
                        sp.dma_start(dst, mrow[j:j + 1, (ph.unit0 + u) % 2, :]).then_inc(sem(name), 16)
            sp.wait_ge(sem("y_done"), 1)
            sp.dma_start(out.rearrange("b (t p) d -> p (b t) d", p=P), x[:]).then_inc(sem("out_done"), 16)
            sp.wait_ge(sem("out_done"), 16)

        @block.gpsimd
        def _(pool):
            done = {}

            def alone(ins, name):
                done[name] = done.get(name, 0) + 1
                ins.then_inc(sem(name), 1)
                pool.wait_ge(sem(name), done[name])

            for f in ("attn0", "mixer"):
                alone(nc.gpsimd.memset(woP[f][:], 0.0), "wo_zero")
            alone(nc.gpsimd.memset(V8[:], 0.0), "v8_zero")
            alone(nc.gpsimd.memset(V8[:].rearrange("p t h c -> p (t h) c")[:, :, 8:9], 1.0), "v8_set")
            alone(nc.gpsimd.memset(ones[:], 1.0), "ones_set")
            alone(nc.gpsimd.memset(negx[:], 1.0), "ones_set")
            alone(nc.gpsimd.memset(K2[64:P, :, :, :].rearrange("p a b c -> p (a b c)").bitcast(F32), 0.0), "k2_zero")
            alone(nc.gpsimd.memset(Q2[64:P, :, :, :].rearrange("p a b c -> p (a b c)").bitcast(F32), 0.0), "k2_zero")
            alone(nc.gpsimd.memset(K2[64:65, :, :, :].rearrange("p a b c -> p (a b c)"), 1.0), "k2_set")
            for ph in phases:
                if ph.small:
                    continue
                for kind, u, i in ph.order:
                    if kind == "prep" and i >= 4:
                        pool.wait_ge(sem("hi_done"), hi_count[ph.name, u, i])
                        alone(nc.gpsimd.tensor_copy(Q2[0:64, u % 3, i - 4, :], Q1[0:64, u % 3, i - 4, :]), "q2_done")

        @block.tensor
        def _(pe):
            mm = nc.tensor.matmul

            def norm_transpose(n):
                pe.wait_ge(sem("xn_done"), n + 1)
                for t in range(NT):
                    last = nc.tensor.transpose(SCR[:, 1, t * P:(t + 1) * P], xn[:, t, :], ident)
                last.then_inc(sem("xnT_ready"), 1)
                pe.wait_ge(sem("xnT_done"), n + 1)

            def aux(ph, job):
                kind, u, i = job
                n = ph.index[job]
                dst = AUX[:, n % 2, :]
                if n >= 2:
                    pe.wait_ge(sem("aux_free"), n - 1)
                if kind == "prep" and ph.small:
                    which = "k" if i == 0 else "q"
                    classes = ph.name == "mixer"
                    last = mm(dst, WR[ph.name, which][:, u * P:(u + 1) * P], xnT[:], start=True, stop=not classes)
                    if classes:
                        rows = cls_k if which == "k" else cls_q
                        for c, r in enumerate((R_POS, R_NEG)):
                            last = mm(dst, csth[0:1, r:r + P], rows[0:1, c, :, :].rearrange("p b s -> p (b s)"),
                                      start=False, stop=(c == 1))
                elif kind == "prep" and i < 4:
                    h, b = i // 2, i % 2
                    last = mm(dst, wk2[ph.name][:, 2 * u + h, :, :].rearrange("p r d -> p (r d)"),
                              ctxT[:, b * SC:(b + 1) * SC], start=True, stop=True)
                elif kind == "prep":
                    last = mm(dst, wq2[ph.name][:, 2 * u + i - 4, :, :].rearrange("p r d -> p (r d)"),
                              xnT[:], start=True, stop=True)
                elif kind == "max":
                    t, b = i // 2, i // 4
                    if ph.small:
                        for e in range(2):
                            j = 2 * (i % 2) + e
                            last = mm(dst[:, e * S:(e + 1) * S], Qr[:, u % 3, j, t * P:(t + 1) * P],
                                      Kr[:, u, b * S:(b + 1) * S], start=True, stop=True)
                    else:
                        if i == 0:
                            pe.wait_ge(sem("k2_set"), 1)
                        last = mm(dst, Q1[:, u % 3, i % 2, t * P:(t + 1) * P],
                                  K1[:, u % 3, i % 2, b * SC:(b + 1) * SC], start=True, stop=True)
                else:
                    pe.wait_ge(sem("aux_free"), ph.aux_done(("max", u, 7)))
                    for t in range(NT):
                        last = nc.tensor.transpose(dst[0:ph.hu, t * P:(t + 1) * P],
                                                   mx[:, u % 2, t, 0:ph.hu], ident)
                last.then_inc(sem("aux_ready"), 1)

            def prepared(ph, u):
                pe.wait_ge(sem("aux_free"), ph.aux_done(("prep", u, ph.nprep - 1)))

            def scores(ph, s, half):
                u, c = divmod(s, 4)
                b, k = c // 2, c % 2
                n = ph.chunk0 + s
                if half == 0:
                    if n >= 2:
                        pe.wait_ge(sem("exp_done"), n - 1)
                    if c == 0:
                        name, count = row_count[ph.name, u]
                        pe.wait_ge(sem(name), count)
                        prepared(ph, u)
                dst = SCR[:, 2 * (n % 2) + half, :]
                if ph.small:
                    last = mm(dst, Kr[:, u, b * S + k * P:b * S + (k + 1) * P],
                              Qr[:, u % 3, 2 * half:2 * half + 2, b * S:(b + 1) * S], start=True, stop=True)
                else:
                    for kk in range(2):
                        keys = slice(b * SC + (2 * k + kk) * P, b * SC + (2 * k + kk + 1) * P)
                        for first, (K_, Q_) in enumerate(((K1, Q1), (K2, Q2))):
                            last = mm(dst[:, kk * S:(kk + 1) * S], K_[:, u % 3, half, keys],
                                      Q_[:, u % 3, half, b * S:(b + 1) * S], start=(first == 0), stop=(first == 1))
                if half == 1:
                    last.then_inc(sem("scores_ready"), 1)

            def values(ph, s, half):
                u, c = divmod(s, 4)
                b, k = c // 2, c % 2
                n = ph.chunk0 + s
                a = n // 2
                if half == 0:
                    pe.wait_ge(sem("exp_done"), n + 1)
                    if k == 0 and a >= 2:
                        pe.wait_ge(sem("norm_done"), a - 1)
                if ph.small:
                    if half == 0:
                        return
                    for j in range(4):
                        last = mm(ACC[32 * j:32 * j + 32, a % 2, 0:S], V8[:, 2 * b + k, 4 * u + j, :],
                                  Pr[:, n % 2, j * S:(j + 1) * S], start=(k == 0), stop=(k == 1),
                                  tile_position=(0, 32 * j))
                else:
                    kk = half
                    kt = 2 * k + kk
                    for part in range(2):
                        for h in range(2):
                            w = ones[:, 0:64] if part else V[:, b * 4 + kt, (2 * u + h) * 64:(2 * u + h + 1) * 64]
                            last = mm(ACC[64 * h:64 * h + 64, a % 2, part * S:(part + 1) * S], w,
                                      Pr[:, n % 2, (2 * h + kk) * S:(2 * h + kk + 1) * S],
                                      start=(kt == 0 and part == 0), stop=(kt == 3), skip_group_check=True,
                                      tile_position=(0, 64 * h))
                if half == 1:
                    last.then_inc(sem("values_done"), 1)

            def select(ph, a):
                n = ph.chunk0 // 2 + a
                pe.wait_ge(sem("z_copied"), z_count[ph.name, a])
                mm(ACC[:, n % 2, S:2 * S], den_row, Zs[:, n % 2, :], start=True, stop=True).then_inc(sem("den_ready"), 1)

            def run_units(ph):
                for job in ph.head:
                    if job[0] == "max" and job[2] == 0:
                        prepared(ph, job[1])
                    aux(ph, job)
                for slot in ph.slots:
                    jobs = list(slot["aux"])
                    if jobs and jobs[0][0] == "max" and jobs[0][2] == 0:
                        prepared(ph, jobs[0][1])
                    parts = []
                    if slot["main"] is not None:
                        parts += [(scores, slot["main"], 0), (scores, slot["main"], 1)]
                    if slot["pv"] is not None:
                        parts += [(values, slot["pv"], 0), (values, slot["pv"], 1)]
                    while parts or jobs:
                        if parts:
                            f, s, half = parts.pop(0)
                            f(ph, s, half)
                        if jobs:
                            aux(ph, jobs.pop(0))
                    if slot["select"] is not None:
                        select(ph, slot["select"])

            def project_out(ph, w):
                a = (ph.chunk0 + 4 * ph.U) // 2
                pe.wait_ge(sem("norm_done"), a)
                if ph.name == "mixer":
                    pe.wait_ge(sem("regs_merged"), 1)
                for t in range(NT):
                    for u in range(ph.U):
                        last = mm(SCR[:, 0, t * P:(t + 1) * P], zn[:, u, t * P:(t + 1) * P], w[:, u, :],
                                  start=(u == 0), stop=(u == ph.U - 1))
                last.then_inc(sem("out_ready"), 1)

            def values_small(w, n):
                for t in range(NT):
                    last = mm(SCR[:, 2, t * P:(t + 1) * P], xnT[:, t * P:(t + 1) * P], w, start=True, stop=True)
                last.then_inc(sem("v8_ready"), 1)

            def values_big(ph, first):
                halves = 1 if ph.heads == 8 else 2
                for i in range(NC_T * halves):
                    t, hf = divmod(i, halves)
                    if i >= 4:
                        pe.wait_ge(sem("v_done"), first + i - 3)
                    mm(SCR[:, i % 4, :], ctxT[:, t * P:(t + 1) * P], wv2[ph.name][:, hf * 512:(hf + 1) * 512],
                       start=True, stop=True).then_inc(sem("v_ready"), 1)
                pe.wait_ge(sem("v_done"), first + NC_T * halves)

            pe.wait_ge(sem("cst_in"), 16)
            pe.wait_ge(sem("ctx_in"), 16)
            for t in range(NC_T):
                last = nc.tensor.transpose(ACC[0:DC, t // 4, (t % 4) * P:(t % 4 + 1) * P], ctx_tok[:, t, :], ident)
            last.then_inc(sem("ctxT_ready"), 1)

            norm_transpose(0)
            pe.wait_ge(sem("wa_in"), 48)
            pe.wait_ge(sem("ctxT_done"), 1)
            values_small(wa["v"][:], 0)
            pe.wait_ge(sem("wr_done"), 1)
            pe.wait_ge(sem("v8_done"), 1)
            run_units(A0)
            pe.wait_ge(sem("wo8_in"), 128)
            project_out(A0, woP["attn0"])

            norm_transpose(1)
            pe.wait_ge(sem("cross0_w_in"), 16 * 7)
            pe.wait_ge(sem("ones_set"), 2)
            pe.wait_ge(sem("x_done"), 1)
            values_big(X0, 0)
            run_units(X0)
            project_out(X0, wo2["cross0"])

            norm_transpose(2)
            pe.wait_ge(sem("wm_in"), 48)
            pe.wait_ge(sem("x_done"), 2)
            for t in range(NT):
                last = mm(SCR[:, 0, t * P:(t + 1) * P], xnT[:, t * P:(t + 1) * P], wqkv[:, 0:D], start=True, stop=True)
            last.then_inc(sem("qtok_ready"), 1)
            values_small(wqkv[:, 2 * D:3 * D], 1)
            pe.wait_ge(sem("sim_done"), 1)
            for t in range(NT):
                last = nc.tensor.transpose(SCR[0:1, 3, t * P:(t + 1) * P], sim[:, t:t + 1], ident)
            last.then_inc(sem("simrow_ready"), 1)
            pe.wait_ge(sem("wr_done"), 2)
            pe.wait_ge(sem("xreg_done"), 1)
            pe.wait_ge(sem("csth_in"), 16)
            qx_out = SCR[:, 1, 0:NR].rearrange("p (b u r) -> p b u r", b=B, u=4)
            for u in range(4):
                mm(qx_out[:, :, u, :], WR["mixer", "q"][:, u * P:(u + 1) * P], xreg[:], start=True, stop=False)
                last = mm(qx_out[:, :, u, :], csth[0:1, R_NEG:R_NEG + P], negx[:], start=False, stop=True)
            last.then_inc(sem("qx_ready"), 1)
            pe.wait_ge(sem("cls_done"), 1)
            pe.wait_ge(sem("v8_done"), 2)
            pe.wait_ge(sem("qx_done"), 1)
            run_units(F0)
            for u in range(4):
                for b in range(B):
                    last = mm(SCR[0:4 * REG, u, b * S:(b + 1) * S],
                              Qx[:, b, u, :, :].rearrange("p j r -> p (j r)"),
                              Kr[:, u, b * S:(b + 1) * S], start=True, stop=True)
            last.then_inc(sem("reg_scores"), 1)
            pe.wait_ge(sem("reg_exp"), 1)
            for ub in range(8):
                for k in range(2):
                    c = (ub * 2 + k) * 4 * REG
                    last = nc.tensor.transpose(AUX[:, 0, c:c + 4 * REG], Preg[:, ub, k * P:(k + 1) * P],
                                               ident[0:4 * REG, 0:4 * REG])
            last.then_inc(sem("regT_ready"), 1)
            pe.wait_ge(sem("regT_done"), 1)
            for u in range(4):
                for b in range(B):
                    for k in range(2):
                        for j in range(4):
                            c = (u * B + b) * REG
                            last = mm(AUX[32 * j:32 * j + 32, 1, c:c + REG], V8[:, 2 * b + k, 4 * u + j, :],
                                      PregT[:, (u * B + b) * 2 + k, j * REG:(j + 1) * REG],
                                      start=(k == 0), stop=(k == 1), tile_position=(0, 32 * j))
            last.then_inc(sem("reg_z"), 1)
            pe.wait_ge(sem("reg_z_done"), 1)
            mm(AUX[:, 0, 0:NR], den_row, Zreg[:], start=True, stop=True).then_inc(sem("reg_den"), 1)
            project_out(F0, woP["mixer"])

            norm_transpose(3)
            pe.wait_ge(sem("wd_in"), 16 * 8)
            pe.wait_ge(sem("wbeta_done"), 1)
            pe.wait_ge(sem("x_done"), 3)
            mm(SCR[:, 0, :], wd["k"][:], xnT[:], start=True, stop=True).then_inc(sem("d_proj"), 1)
            mm(SCR[:, 1, :], wd["q"][:], xnT[:], start=True, stop=True).then_inc(sem("d_proj"), 1)
            mm(SCR[:, 3, :], wbeta8[:].rearrange("p h i -> p (h i)"), xnT[:], start=True, stop=True).then_inc(sem("d_proj"), 1)
            mm(SCR[:, 2, :], wd["v"][:], xnT[:], start=True, stop=True).then_inc(sem("d_proj"), 1)
            for t in range(NT):
                last = mm(ACC[:, 0, t * P:(t + 1) * P], xnT[:, t * P:(t + 1) * P], wd["g"][:], start=True, stop=True)
            last.then_inc(sem("d_proj"), 1)
            for i in range(2):
                pe.wait_ge(sem("d_sq"), i + 1)
                mm(AUX[:, i, :], head_sum, room(i), start=True, stop=True).then_inc(sem("d_n2"), 1)
            pe.wait_ge(sem("d_split"), 2)
            pe.wait_ge(sem("csth_in"), 16)

            def spread(j):
                for i in range(2):
                    if j >= 2:
                        pe.wait_ge(sem("d_kfree" if i == 0 else "d_prod"), j - 1)
                    for part in range(2):
                        last = mm(SCR[:, 2 * i + j % 2, :], csth[:, R_SEL + j * P:R_SEL + (j + 1) * P],
                                  d_half(i, part), start=(part == 0), stop=(part == 1))
                    last.then_inc(sem("d_spread"), 1)

            pe.wait_ge(sem("d_terms"), 1)
            spread(0)
            for j in range(8):
                if j + 1 < 8:
                    spread(j + 1)
                pe.wait_ge(sem("d_prod"), j + 1)
                mm(AUX[:, 0, :], ident, room(12 + j % 2), start=(j == 0), stop=(j == 7)).then_inc(sem("d_sum"), 1)
            pe.wait_ge(sem("d_oT"), 1)
            for t in range(NT):
                last = nc.tensor.transpose(AUX[:, 1, t * P:(t + 1) * P], room(0)[:, t * P:(t + 1) * P], ident)
            last.then_inc(sem("d_o_ready"), 1)
            pe.wait_ge(sem("d_y"), 1)
            for t in range(NT):
                last = nc.tensor.transpose(ACC[:, 1, t * P:(t + 1) * P], room(1)[:, t * P:(t + 1) * P], ident)
            last.then_inc(sem("d_yT_ready"), 1)
            pe.wait_ge(sem("d_yT"), 1)
            for t in range(NT):
                last = mm(SCR[:, 0, t * P:(t + 1) * P], room(2)[:, t * P:(t + 1) * P], wd["o"][:], start=True, stop=True)
            last.then_inc(sem("out_ready"), 1)

            norm_transpose(4)
            pe.wait_ge(sem("cross1_w_in"), 16 * 7)
            pe.wait_ge(sem("x_done"), 4)
            values_big(Y1, 8)
            run_units(Y1)
            project_out(Y1, wo2["cross1"])

            pe.wait_ge(sem("abs_sums"), 1)
            pe.wait_ge(sem("x_done"), 5)
            mm(ACC[:, 0, 0:2], ones[:], gam[:, 0:2], start=True, stop=True).then_inc(sem("gamma_ready"), 1)
            pe.wait_ge(sem("ternary"), 1)
            for a in range(4):
                nc.tensor.transpose(AUX[:, 0, a * P:(a + 1) * P], wfc[:, a, :], ident)
                last = nc.tensor.transpose(AUX[:, 1, a * P:(a + 1) * P], wpj[:, a * P:(a + 1) * P], ident)
            last.then_inc(sem("ternT_ready"), 1)
            norm_transpose(5)
            pe.wait_ge(sem("x_split"), 1)
            pe.wait_ge(sem("ternT_done"), 2)
            for t in range(NT):
                for part in range(2):
                    last = mm(SCR[:, t, :], hi[:, part, t * P:(t + 1) * P],
                              fcT[:].rearrange("p a b -> p (a b)"), start=(part == 0), stop=(part == 1))
                last.then_inc(sem("h_ready"), 1)
            for t in range(NT):
                pe.wait_ge(sem("h_norm"), t + 1)
                if t >= 2:
                    pe.wait_ge(sem("hT_split"), t - 1)
                for a in range(4):
                    last = nc.tensor.transpose(AUX[:, t % 2, a * P:(a + 1) * P],
                                               room(2 * t + 1)[:, a * P:(a + 1) * P], ident)
                last.then_inc(sem("hT_ready"), 1)
                pe.wait_ge(sem("hT_split"), t + 1)
                for a in range(4):
                    for part in range(2):
                        last = mm(ACC[:, 1, t * P:(t + 1) * P], h_half(t, part)[:, a * P:(a + 1) * P],
                                  pjT[:, a, :], start=(a == 0 and part == 0), stop=(a == 3 and part == 1))
            last.then_inc(sem("out_ready"), 1)

        @block.scalar
        def _(act):
            A = nc.scalar.activation

            def inv_root(n):
                act.wait_ge(sem("var_done"), n + 1)
                A(rt1[:], rt1[:], ACT.Ln).then_inc(sem("act_ln"), 1)
                act.wait_ge(sem("act_ln"), n + 1)
                A(rstd[:], rt1[:], ACT.Exp, scale=-0.5).then_inc(sem("root_done"), 1)

            def norm_copy(n):
                act.wait_ge(sem("xnT_ready"), n + 1)
                A(xnT[:], SCR[:, 1, :], ACT.Identity).then_inc(sem("xnT_done"), 1)

            def aux(ph, job):
                kind, u, i = job
                if kind != "prep":
                    return
                n = ph.index[job]
                src = AUX[:, n % 2, :]
                act.wait_ge(sem("aux_ready"), n + 1)
                if ph.small:
                    k = hi_count[ph.name, u, i]
                    if k > 2:
                        before = prep_jobs[k - 3]
                        bp = next(p for p in phases if p.name == before[0])
                        act.wait_ge(sem("aux_free"), bp.aux_done(("prep", *before[1:])))
                    bias = col(M_BIASK) if i == 0 else 0.0
                    A(hi[:, i, :], src, ACT.Identity, bias=bias).then_inc(sem("hi_done"), 1)
                elif i < 4:
                    h, b = i // 2, i % 2
                    A(K1[:, u % 3, h, b * SC:(b + 1) * SC], src, ACT.Identity).then_inc(sem("hi_done"), 1)
                else:
                    A(Q1[:, u % 3, i - 4, :], src, ACT.Identity).then_inc(sem("hi_done"), 1)

            def run_units(ph):
                for job in ph.head:
                    aux(ph, job)
                for slot in ph.slots:
                    for job in slot["aux"][:2]:
                        aux(ph, job)
                    if slot["main"] is not None:
                        n = ph.chunk0 + slot["main"]
                        act.wait_ge(sem("scores_ready"), n + 1)
                        if n >= 2:
                            act.wait_ge(sem("values_done"), n - 1)
                        A(Pr[:, n % 2, :], SCR[:, 2 * (n % 2):2 * (n % 2) + 2, :].rearrange("p a b -> p (a b)"),
                          ACT.Exp, scale=ph.scale).then_inc(sem("exp_done"), 1)
                    for job in slot["aux"][2:]:
                        aux(ph, job)

            def values_small(n):
                act.wait_ge(sem("v8_ready"), n + 1)
                act.wait_ge(sem("v8_set"), 1)
                A(V8[:].rearrange("p t h c -> p (t h) c")[:, :, 0:8],
                  SCR[:, 2, :].rearrange("p (a d) -> p a d", d=8), ACT.Identity).then_inc(sem("v8_done"), 1)

            def values_big(ph, first):
                halves = 1 if ph.heads == 8 else 2
                for i in range(NC_T * halves):
                    t, hf = divmod(i, halves)
                    act.wait_ge(sem("v_ready"), first + i + 1)
                    A(V[:, t, hf * 512:(hf + 1) * 512], SCR[:, i % 4, :], ACT.Identity).then_inc(sem("v_done"), 1)

            act.wait_ge(sem("ctxT_ready"), 1)
            A(ctxT[:], ACC[0:DC, :, :].rearrange("p a b -> p (a b)"), ACT.Identity).then_inc(sem("ctxT_done"), 1)
            inv_root(0)
            norm_copy(0)
            values_small(0)
            act.wait_ge(sem("ctxT_done"), 1)
            run_units(A0)

            inv_root(1)
            norm_copy(1)
            values_big(X0, 0)
            run_units(X0)

            inv_root(2)
            norm_copy(2)
            act.wait_ge(sem("qtok_ready"), 1)
            A(room(1), SCR[:, 0, :], ACT.Square).then_inc(sem("qsq_done"), 1)
            act.wait_ge(sem("norms2"), 1)
            A(n2[:], n2[:], ACT.Sqrt).then_inc(sem("norms"), 1)
            A(gn[:, 0, :], gn[:, 0, :], ACT.Sqrt).then_inc(sem("norms"), 1)
            values_small(1)
            act.wait_ge(sem("xnT_done"), 3)
            A(xreg[:].rearrange("p (b r) -> p b r", b=B), xnT[:].rearrange("p (b s) -> p b s", b=B)[:, :, 0:REG],
              ACT.Identity).then_inc(sem("xreg_done"), 1)
            act.wait_ge(sem("qx_ready"), 1)
            A(qxh[:], SCR[:, 1, 0:NR], ACT.Identity).then_inc(sem("qxh_done"), 1)
            run_units(F0)
            act.wait_ge(sem("reg_shifted"), 1)
            A(Preg, Preg, ACT.Exp, scale=F0.scale).then_inc(sem("reg_exp"), 1)

            inv_root(3)
            norm_copy(3)
            for i in range(2):
                act.wait_ge(sem("d_proj"), i + 1)
                A(room(i), SCR[:, i, :], ACT.Square).then_inc(sem("d_sq"), 1)
            act.wait_ge(sem("d_proj"), 3)
            A(room(2), SCR[:, 3, :], ACT.Exp, scale=-1.0).then_inc(sem("d_ebeta"), 1)
            act.wait_ge(sem("d_proj"), 5)
            A(room(3), ACC[:, 0, :], ACT.Exp, scale=-1.0).then_inc(sem("d_egate"), 1)
            for i in range(2):
                act.wait_ge(sem("d_n2"), i + 1)
                A(room(4 + i), AUX[:, i, :], ACT.Sqrt).then_inc(sem("d_root"), 1)
            for j in range(8):
                act.wait_ge(sem("d_kk"), j + 1)
                A(room(8 + j % 2), room(8 + j % 2), ACT.Identity, bias=1.0).then_inc(sem("d_decay"), 1)
            act.wait_ge(sem("d_sum"), 8)
            A(room(0), AUX[:, 0, :], ACT.Identity).then_inc(sem("d_oT"), 1)
            act.wait_ge(sem("d_var"), 1)
            A(rt1[:], rt1[:], ACT.Ln).then_inc(sem("d_ln"), 1)
            act.wait_ge(sem("d_ln"), 1)
            A(rstd[:], rt1[:], ACT.Exp, scale=-0.5).then_inc(sem("d_rstd"), 1)
            act.wait_ge(sem("d_yT_ready"), 1)
            A(room(2), ACC[:, 1, :], ACT.Identity).then_inc(sem("d_yT"), 1)

            inv_root(4)
            norm_copy(4)
            values_big(Y1, 8)
            run_units(Y1)

            act.wait_ge(sem("ternT_ready"), 1)
            A(fcT[:].rearrange("p a b -> p (a b)"), AUX[:, 0, :], ACT.Identity).then_inc(sem("ternT_done"), 1)
            A(pjT[:].rearrange("p a b -> p (a b)"), AUX[:, 1, :], ACT.Identity).then_inc(sem("ternT_done"), 1)
            inv_root(5)
            norm_copy(5)
            act.wait_ge(sem("xnT_done"), 6)
            A(hi[:, 0, :], xnT[:], ACT.Identity).then_inc(sem("x_high"), 1)
            for t in range(NT):
                act.wait_ge(sem("h_ready"), t + 1)
                A(room(2 * t), SCR[:, t, :], ACT.Gelu).then_inc(sem("gelu_done"), 1)
            act.wait_ge(sem("h_var"), 1)
            A(rt1[:], rt1[:], ACT.Ln).then_inc(sem("h_ln"), 1)
            act.wait_ge(sem("h_ln"), 1)
            A(rstd[:], rt1[:], ACT.Exp, scale=-0.5).then_inc(sem("h_rstd"), 1)
            for t in range(NT):
                act.wait_ge(sem("hT_ready"), t + 1)
                A(h_half(t, 0), AUX[:, t % 2, :], ACT.Identity).then_inc(sem("hT_high"), 1)

        @block.vector
        def _(dve):
            v = nc.vector
            chain = [0]

            def then(ins):
                chain[0] += 1
                ins.then_inc(sem("dve_step"), 1)
                dve.wait_ge(sem("dve_step"), chain[0])

            def refine():
                then(v.tensor_tensor(rt1[:], rstd[:], rstd[:], ALU.mult))
                then(v.tensor_tensor(rt1[:], rt1[:], rt2[:], ALU.mult))
                then(v.tensor_scalar(rt1[:], rt1[:], -0.5, 1.5, ALU.mult, ALU.add))
                then(v.tensor_tensor(rstd[:], rstd[:], rt1[:], ALU.mult))

            def variance(src, ready, name):
                for t in range(NT):
                    if ready:
                        dve.wait_ge(sem(ready), t + 1)
                    then(v.bn_stats(stats[:, t, :], src(t)))
                    then(v.bn_aggr(mv[:, t, :], stats[:, t, :]))
                then(v.tensor_scalar(rt2[:], mv[:, :, 1], LN_EPS, None, ALU.add))
                v.tensor_copy(rt1[:], rt2[:]).then_inc(sem(name), 1)

            def layer_norm(n):
                variance(lambda t: x[:, t, :], None, "var_done")
                dve.wait_ge(sem("root_done"), n + 1)
                refine()
                for t in range(NT):
                    last = v.tensor_scalar(xn[:, t, :], x[:, t, :], mv[:, t, 0:1], rstd[:, t:t + 1],
                                           ALU.subtract, ALU.mult)
                last.then_inc(sem("xn_done"), 1)

            def aux(ph, job):
                kind, u, i = job
                n = ph.index[job]
                src = AUX[:, n % 2, :]
                if kind == "max":
                    dve.wait_ge(sem("aux_ready"), n + 1)
                    t = i // 2
                    if ph.small:
                        e = 2 * (i % 2)
                        last = v.tensor_reduce(mx[:, u % 2, t, e:e + 2], src.rearrange("p (a s) -> p a s", a=2), AX, ALU.max)
                    else:
                        last = v.tensor_reduce(mx[:, u % 2, t, i % 2:i % 2 + 1], src, AX, ALU.max)
                elif kind == "turn":
                    dve.wait_ge(sem("aux_ready"), n + 1)
                    gu = ph.unit0 + u
                    if gu >= 2:
                        prev = ph if u >= 2 else phases[phases.index(ph) - 1]
                        pu = u - 2 if u >= 2 else prev.U - 2 + u
                        name, count = row_count[prev.name, pu]
                        dve.wait_ge(sem(name), count)
                    last = v.tensor_scalar(mrow[0:ph.hu, gu % 2, :], src[0:ph.hu, :], -1.0, None, ALU.mult)
                else:
                    dve.wait_ge(sem("hi_done"), hi_count[ph.name, u, i])
                    if ph.small and i == 0:
                        last = v.scalar_tensor_tensor(Kr[:, u, :], hi[:, 0, :], col(M_NK), src, ALU.mult, ALU.add)
                    elif ph.small:
                        then(v.scalar_tensor_tensor(qn[:], hi[:, 1, :], col(M_NQ), src, ALU.mult, ALU.add))
                        for j in range(4):
                            last = v.tensor_scalar(Qr[:, u % 3, j, :], qn[:], col(M_BLK + j), None, ALU.mult)
                    elif i < 4:
                        h, b = i // 2, i % 2
                        keys = slice(b * SC, (b + 1) * SC)
                        last = v.tensor_tensor(K2[0:64, u % 3, h, keys], src[0:64, :], K1[0:64, u % 3, h, keys], ALU.subtract)
                    else:
                        q = Q1[64:P, u % 3, i - 4, :]
                        last = v.tensor_tensor(q, src[64:P, :], q, ALU.subtract)
                last.then_inc(sem("aux_free"), 1)

            def norm(ph, a, part):
                n = ph.chunk0 // 2 + a
                u, b = divmod(a, 2)
                zs, rd = Zs[:, n % 2, :], rden[:, n % 2, :]
                if n >= 2:
                    dve.wait_ge(sem("norm_done"), n - 1)
                num, den = ACC[:, n % 2, 0:S], ACC[:, n % 2, S:2 * S]
                dst = zn[:, u, b * S:(b + 1) * S]
                if ph.small and part == 0:
                    dve.wait_ge(sem("values_done"), ph.chunk0 + 2 * a + 2)
                    v.tensor_copy(zs, num).then_inc(sem("z_copied"), 1)
                elif ph.small:
                    dve.wait_ge(sem("den_ready"), z_count[ph.name, a])
                    then(v.reciprocal(rd, den))
                    v.tensor_tensor(dst, zs, rd, ALU.mult).then_inc(sem("norm_done"), 1)
                else:
                    dve.wait_ge(sem("values_done"), ph.chunk0 + 2 * a + 2)
                    then(v.reciprocal(rd, den))
                    v.tensor_tensor(dst, num, rd, ALU.mult).then_inc(sem("norm_done"), 1)

            def run_units(ph):
                for job in ph.head:
                    aux(ph, job)
                for slot in ph.slots:
                    for job in slot["aux"]:
                        aux(ph, job)
                    if slot["norm2"] is not None:
                        norm(ph, slot["norm2"], 1)
                    if slot["norm"] is not None:
                        norm(ph, slot["norm"], 0)

            def residual(n, bias=None, also=None):
                if bias is not None:
                    then(v.tensor_tensor(x[:], x[:], bias[:].unsqueeze(1).to_broadcast([P, NT, D]), ALU.add))
                if also is not None:
                    then(v.tensor_tensor(x[:], x[:], also[:], ALU.add))
                dve.wait_ge(sem("out_ready"), n + 1)
                src = ACC[:, 1, :] if n == 5 else SCR[:, 0, :]
                last = v.tensor_tensor(x[:], x[:], src.rearrange("p (t d) -> p t d", d=D), ALU.add)
                chain[0] += 0
                last.then_inc(sem("x_done" if n < 5 else "y_done"), 1)
                if n < 5:
                    dve.wait_ge(sem("x_done"), n + 1)

            def repeat(f, srcs, n):
                for which, src in srcs:
                    w = WR[f, which][:].rearrange("p (h r d) -> p h r d", h=16, r=4)
                    v.memset(w[:, :, 3, :], 0.0)
                    for r in range(3):
                        last = v.tensor_copy(w[:, :, r, :], src.rearrange("p (h d) -> p h d", h=16))
                last.then_inc(sem("wr_done"), 1)

            dve.wait_ge(sem("x_in"), 16)
            layer_norm(0)
            dve.wait_ge(sem("cst_in"), 16)
            dve.wait_ge(sem("wa_in"), 48)
            repeat("attn0", (("q", wa["q"][:]), ("k", wa["k"][:])), 0)
            run_units(A0)
            residual(0, also=xn)

            layer_norm(1)
            run_units(X0)
            dve.wait_ge(sem("cross0_w_in"), 16 * 7)
            residual(1, bias=bias_out["cross0"])

            layer_norm(2)
            dve.wait_ge(sem("wm_in"), 48)
            repeat("mixer", (("q", wqkv[:, 0:D]), ("k", wqkv[:, D:2 * D])), 1)
            then(v.tensor_tensor(room(2)[:, 0:D], qg[:], qg[:], ALU.mult))
            then(v.tensor_reduce(gn[:, 0, :], room(2)[:, 0:D].rearrange("p (h d) -> p h d", d=8), AX, ALU.add))
            dve.wait_ge(sem("qsq_done"), 1)
            v.tensor_reduce(n2[:], room(1).rearrange("p (a d) -> p a d", d=8), AX, ALU.add).then_inc(sem("norms2"), 1)
            then(v.tensor_tensor(room(0).rearrange("p (t c) -> p t c", t=NT), SCR[:, 0, :].rearrange("p (t c) -> p t c", t=NT),
                                 qg[:].unsqueeze(1).to_broadcast([P, NT, D]), ALU.mult))
            then(v.tensor_reduce(dot[:], room(0).rearrange("p (a d) -> p a d", d=8), AX, ALU.add))
            dve.wait_ge(sem("norms"), 2)
            then(v.reciprocal(n2[:], n2[:]))
            then(v.reciprocal(gn[:, 1, :], gn[:, 0, :]))
            then(v.tensor_tensor(dot[:], dot[:], n2[:], ALU.mult))
            dot3 = dot[:].rearrange("p (t h) -> p t h", t=NT)
            then(v.tensor_tensor(dot3, dot3, gn[:, 1, :].unsqueeze(1).to_broadcast([P, NT, H16]), ALU.mult))
            then(v.tensor_reduce(sim[:], dot3, AX, ALU.add))
            v.tensor_scalar(sim[:], sim[:], 1.0 / H16, None, ALU.mult).then_inc(sem("sim_done"), 1)
            dve.wait_ge(sem("simrow_ready"), 1)
            then(v.tensor_copy(simrow[:].rearrange("p b s -> p (b s)"), SCR[0:1, 3, :]))
            for i, op in enumerate((ALU.min, ALU.max)):
                then(v.tensor_reduce(ext[:, i:i + 1], simrow[:, :, REG:S], mybir.AxisListType.XY, op))
            then(v.tensor_tensor(ext[:, 2:3], ext[:, 1:2], ext[:, 0:1], ALU.subtract))
            then(v.reciprocal(ext[:, 3:4], ext[:, 2:3]))
            then(v.tensor_scalar(simrow[:], simrow[:], ext[:, 0:1], ext[:, 3:4], ALU.subtract, ALU.mult))
            then(v.tensor_scalar(posrow[:], simrow[:], 0.9, None, ALU.is_gt))
            then(v.tensor_copy(cls_q[:, 0, :, :], posrow[:]))
            then(v.tensor_scalar(cls_q[:, 1, :, :], posrow[:], -1.0, 1.0, ALU.mult, ALU.add))
            then(v.tensor_scalar(cls_k[:, 0, :, :], posrow[:], BIG, -BIG, ALU.mult, ALU.add))
            then(v.tensor_scalar(cls_k[:, 1, :, :], posrow[:], -BIG, None, ALU.mult))
            v.memset(cls_q[:, 0, :, 0:REG], 1.0)
            v.memset(cls_q[:, 1, :, 0:REG], 0.0)
            then(v.memset(cls_k[:, 0, :, 0:REG], 0.0))
            v.memset(cls_k[:, 1, :, 0:REG], 0.0).then_inc(sem("cls_done"), 1)
            dve.wait_ge(sem("qxh_done"), 1)
            then(v.scalar_tensor_tensor(qxn[:], qxh[:], col(M_NQ), SCR[:, 1, 0:NR], ALU.mult, ALU.add))
            for j in range(4):
                last = v.tensor_scalar(Qx[:, :, :, j, :].rearrange("p b u r -> p (b u) r"),
                                       qxn[:].rearrange("p (a r) -> p a r", r=REG), col(M_BLK + j), None, ALU.mult)
            last.then_inc(sem("qx_done"), 1)
            run_units(F0)
            dve.wait_ge(sem("reg_scores"), 1)
            rs = SCR[0:4 * REG, :, :].rearrange("p u (b s) -> p (u b) s", b=B)
            then(v.tensor_reduce(mreg[:], rs, AX, ALU.max))
            v.tensor_tensor(Preg, rs, mreg[:].unsqueeze(2).to_broadcast([4 * REG, 8, S]), ALU.subtract)\
                .then_inc(sem("reg_shifted"), 1)
            dve.wait_ge(sem("regT_ready"), 1)
            v.tensor_copy(PregT[:].rearrange("p a b -> p (a b)"), AUX[:, 0, 0:16 * 4 * REG]).then_inc(sem("regT_done"), 1)
            dve.wait_ge(sem("reg_z"), 1)
            v.tensor_copy(Zreg[:], AUX[:, 1, 0:NR]).then_inc(sem("reg_z_done"), 1)
            dve.wait_ge(sem("reg_den"), 1)
            then(v.reciprocal(rreg[:], AUX[:, 0, 0:NR]))
            then(v.scalar_tensor_tensor(Zreg[:], Zreg[:], 0.5, rreg[:], ALU.mult, ALU.mult))
            for u in range(4):
                z = zn[:, u, :].rearrange("p (b s) -> p b s", b=B)[:, :, 0:REG]
                last = v.scalar_tensor_tensor(z, z, 0.5, Zreg[:, u * B * REG:(u + 1) * B * REG].rearrange(
                    "p (b r) -> p b r", b=B), ALU.mult, ALU.add)
                if u < 3:
                    then(last)
            last.then_inc(sem("regs_merged"), 1)
            residual(2, bias=bias_out["mixer"])

            layer_norm(3)
            dve.wait_ge(sem("wd_in"), 16 * 8)
            v.tensor_copy(wbeta8[:], wbeta[:].unsqueeze(2).to_broadcast([P, H16, 8])).then_inc(sem("wbeta_done"), 1)
            beta, gate = room(2), room(3)
            for src, name in ((beta, "d_ebeta"), (gate, "d_egate")):
                dve.wait_ge(sem(name), 1)
                then(v.tensor_scalar(src, src, 1.0, None, ALU.add))
                then(v.reciprocal(src, src))
            then(v.tensor_tensor(gate, gate, ACC[:, 0, :], ALU.mult))
            for i in range(2):
                r = room(4 + i)
                dve.wait_ge(sem("d_root"), i + 1)
                then(v.tensor_scalar(r, r, 1e-12, None, ALU.max))
                then(v.reciprocal(r, r))
                then(v.tensor_tensor(r, r, SCR[:, i, :], ALU.mult))
                then(v.tensor_copy(d_half(i, 0), r))
                v.tensor_tensor(d_half(i, 1), r, d_half(i, 0), ALU.subtract).then_inc(sem("d_split"), 1)
            kb, vb = room(14), room(15)
            then(v.scalar_tensor_tensor(kb, room(4), -1.0, beta, ALU.mult, ALU.mult))
            dve.wait_ge(sem("d_proj"), 4)
            then(v.tensor_tensor(vb, beta, SCR[:, 2, :], ALU.mult))
            v.tensor_copy(stats[:, 0, 0:1], mv[:, 0, 0:1]).then_inc(sem("d_terms"), 1)

            def recur(j):
                dve.wait_ge(sem("d_decay"), j + 1)
                if j >= 1:
                    dve.wait_ge(sem("d_prod"), j)
                for b in range(B):
                    ts = slice(b * S, (b + 1) * S)
                    last = v.tensor_tensor_scan(room(11)[:, ts], room(8 + j % 2)[:, ts], room(6 + j % 2)[:, ts],
                                                0.0, ALU.mult, ALU.add)
                    if b == 0:
                        last.then_inc(sem("d_scan"), 1)
                last.then_inc(sem("d_scan"), 1)
                dve.wait_ge(sem("d_scan"), 2 * j + 2)
                if j >= 2:
                    dve.wait_ge(sem("d_sum"), j - 1)
                dve.wait_ge(sem("d_spread"), 2 * j + 2)
                v.tensor_tensor(room(12 + j % 2), room(11), SCR[:, 2 + j % 2, :], ALU.mult).then_inc(sem("d_prod"), 1)

            for j in range(8):
                dve.wait_ge(sem("d_spread"), 2 * j + 1)
                v.tensor_tensor(room(8 + j % 2), SCR[:, j % 2, :], kb, ALU.mult).then_inc(sem("d_kk"), 1)
                v.tensor_tensor(room(6 + j % 2), SCR[:, j % 2, :], vb, ALU.mult).then_inc(sem("d_kfree"), 1)
                if j >= 1:
                    dve.wait_ge(sem("d_kfree"), j)
                    recur(j - 1)
            dve.wait_ge(sem("d_kfree"), 8)
            recur(7)
            dve.wait_ge(sem("d_o_ready"), 1)
            variance(lambda t: AUX[:, 1, t * P:(t + 1) * P], None, "d_var")
            dve.wait_ge(sem("d_rstd"), 1)
            refine()
            y = room(1)
            y3 = y.rearrange("p (t d) -> p t d", t=NT)
            for t in range(NT):
                last = v.tensor_scalar(y[:, t * P:(t + 1) * P], AUX[:, 1, t * P:(t + 1) * P], mv[:, t, 0:1],
                                       rstd[:, t:t + 1], ALU.subtract, ALU.mult)
                then(last)
            then(v.tensor_tensor(y3, y3, lng[:].unsqueeze(1).to_broadcast([P, NT, D]), ALU.mult))
            then(v.tensor_tensor(y3, y3, lnb[:].unsqueeze(1).to_broadcast([P, NT, D]), ALU.add))
            v.tensor_tensor(y, y, gate, ALU.mult).then_inc(sem("d_y"), 1)
            residual(3)

            layer_norm(4)
            run_units(Y1)
            dve.wait_ge(sem("cross1_w_in"), 16 * 7)
            residual(4, bias=bias_out["cross1"])

            dve.wait_ge(sem("wf_in"), 64)
            wfc2 = wfc[:].rearrange("p a b -> p (a b)")
            for i, w in enumerate((wfc2, wpj[:])):
                last = v.tensor_reduce(gam[:, i:i + 1], w, AX, ALU.add, apply_absolute_value=True)
                if i == 0:
                    then(last)
            last.then_inc(sem("abs_sums"), 1)
            dve.wait_ge(sem("gamma_ready"), 1)
            then(v.tensor_scalar(gam[:, 2:4], ACC[:, 0, 0:2], 0.5 / (D * 512), 0.5e-6, ALU.mult, ALU.add))
            then(v.tensor_scalar(gam[:, 4:6], gam[:, 2:4], -1.0, None, ALU.mult))
            for i, w in enumerate((wfc2, wpj[:])):
                then(v.tensor_scalar(room(14), w, gam[:, 4 + i:5 + i], None, ALU.is_lt))
                last = v.scalar_tensor_tensor(w, w, gam[:, 2 + i:3 + i], room(14), ALU.is_gt, ALU.subtract)
                if i == 0:
                    then(last)
            last.then_inc(sem("ternary"), 1)
            layer_norm(5)
            dve.wait_ge(sem("x_high"), 1)
            v.tensor_tensor(hi[:, 1, :], xnT[:], hi[:, 0, :], ALU.subtract).then_inc(sem("x_split"), 1)
            variance(lambda t: room(2 * t), "gelu_done", "h_var")
            dve.wait_ge(sem("h_rstd"), 1)
            refine()
            for t in range(NT):
                h = room(2 * t + 1)
                then(v.tensor_scalar(h, room(2 * t), mv[:, t, 0:1], rstd[:, t:t + 1], ALU.subtract, ALU.mult))
                then(v.tensor_tensor(h, h, lnw1[:], ALU.mult))
                v.tensor_tensor(h, h, lnb1[:], ALU.add).then_inc(sem("h_norm"), 1)
                if t >= 1:
                    split_h(dve, v, t - 1)
            split_h(dve, v, NT - 1)
            residual(5)


NAMES = {
    "x": "x", "ctx": "ctx_768",
    "a_Wq": "L0_attn_Wq", "a_Wk": "L0_attn_Wk", "a_Wv": "L0_attn_Wv", "a_Wo": "L0_attn_Wout",
    "c0_Wq": "L0_xattn_Wq", "c0_Wk": "L0_xattn_Wk", "c0_Wv": "L0_xattn_Wv", "c0_Wo": "L0_xattn_Wout",
    "c0_bo": "L0_xattn_bout",
    "m_g": "L0_ffn_g_info", "m_Wqkv": "L0_ffn_W_qkv", "m_Wo": "L0_ffn_W_proj", "m_bo": "L0_ffn_b_proj",
    "d_Wq": "L1_attn_Wq", "d_Wk": "L1_attn_Wk", "d_Wv": "L1_attn_Wv", "d_Wbeta": "L1_attn_Wbeta",
    "d_Wg": "L1_attn_Wg", "d_Wo": "L1_attn_Wout", "d_lng": "L1_attn_ln_g", "d_lnb": "L1_attn_ln_b",
    "c1_Wq": "L1_xattn_Wq", "c1_Wk": "L1_xattn_Wk", "c1_Wv": "L1_xattn_Wv", "c1_Wo": "L1_xattn_Wo",
    "c1_bo": "L1_xattn_bo",
    "f_Wfc": "L1_ffn_W_fc", "f_lnw": "L1_ffn_ln_w", "f_lnb": "L1_ffn_ln_b", "f_Wpj": "L1_ffn_W_proj",
}


def kernel(**inputs):
    import numpy as _np
    import concourse.bacc as _bacc
    from concourse import mybir as _mybir
    from concourse.bass_utils import run_bass_kernel_spmd as _run

    nc = _bacc.Bacc("TRN2", target_bir_lowering=False, num_devices=1)
    arrays, aps = {}, {}
    for name in INPUTS:
        a = _np.ascontiguousarray(inputs[NAMES[name]])
        arrays[f"in_{name}_dram"] = a
        aps[name] = nc.dram_tensor(f"in_{name}_dram", a.shape, _mybir.dt.from_np(a.dtype), kind="ExternalInput").ap()
    consts = []
    for name, a in zip(("const32", "const16"), constants()):
        arrays[f"in_{name}_dram"] = a
        consts.append(nc.dram_tensor(f"in_{name}_dram", a.shape, _mybir.dt.from_np(a.dtype), kind="ExternalInput").ap())
    out = nc.dram_tensor("out_0_dram", (B, S, D), _mybir.dt.float32, kind="ExternalOutput").ap()
    decoder(nc, aps, *consts, out)
    r = _run(nc, [arrays], core_ids=[0])
    return r.results[0]["out_0_dram"]
```

```python
from contextlib import ExitStack

import numpy as np

import concourse.bass as bass
from concourse import mybir

ALU = mybir.AluOpType
ACT = mybir.ActivationFunctionType
AX = mybir.AxisListType.X
F32 = mybir.dt.float32
F16 = mybir.dt.float16

P = 128
B = 2
S = 256
T = B * S
NT = T // P
D = 128
SC = 512
DC = 96
NC_T = B * SC // P
REG = 5
H16 = 16
LN_EPS = 1e-5
LN_EXP = "natural_log_exp_and_others"
BIG = 32768.0

C_ID, C_MASK = 0, 128
M_NQ, M_NK, M_BIASK, M_BLK = 0, 1, 2, 3
NCF = C_MASK + 8
R_SEL, R_POS, R_NEG = 0, 8 * 128, 9 * 128
NCH = 10 * 128


def constants():
    c = np.zeros((P, NCF), np.float32)
    p = np.arange(P)
    c[:, C_ID:C_ID + P] = np.eye(P)
    r, row = (p % 32) // 8, p % 32
    m = c[:, C_MASK:]
    m[:, M_NQ] = -1.0 * (r == 1)
    m[:, M_NK] = -1.0 * (r == 2) + 1.0 * (row == 24)
    m[:, M_BIASK] = row == 24
    for j in range(4):
        m[:, M_BLK + j] = p // 32 == j
    half = np.zeros((P, NCH), np.float16)
    for j in range(8):
        half[:, R_SEL + j * P:R_SEL + (j + 1) * P] = p[:, None] == (p[None, :] // 8) * 8 + j
    half[0, R_POS:R_POS + P] = row == 25
    half[0, R_NEG:R_NEG + P] = row == 26
    return c, half


class Phase:

    def __init__(self, name, heads, dh, first_unit, first_slot, ahead):
        self.name, self.heads, self.dh = name, heads, dh
        self.small = dh == 8
        self.hu = 4 if self.small else 2
        self.U = heads // self.hu
        self.scale = dh ** -0.5
        self.unit0, self.chunk0 = first_unit, first_slot
        self.ahead = [(ahead.name, "k", u, i) for u in range(3) for i in range(2)] if ahead else []
        self.before, self.after = [], []
        self.order = []
        self.slots = []
        self.plan()

    def values(self, a, b):
        return [(self.name, "v", 0, i) for i in range(a, b)]

    def plan(self):
        U = self.U
        one = lambda kind, u, i=0: [(self.name, kind, u, i)] if u < U else []
        mx = lambda u, a, b: [(self.name, "max", u, i) for i in range(a, b)] if u < U else []
        ahead = list(self.ahead)
        if self.small:
            self.head = one("k", 0) + one("q", 0) + ahead[:2] + mx(0, 0, 8) + one("turn", 0) + one("k", 1) + \
                one("q", 1) + ahead[2:4]
            ahead = ahead[4:]
        else:
            self.head = one("q", 0) + one("q", 1) + mx(0, 0, 8) + one("turn", 0)
        self.order += self.head
        for s in range(4 * U + 4):
            u, c = divmod(s, 4)
            jobs = []
            if u < U and self.small:
                jobs = [one("k", u + 2) + mx(u + 1, 0, 4), mx(u + 1, 4, 8),
                        one("turn", u + 1) + one("q", u + 2), []][c]
                if c == 3:
                    jobs += ahead[:1]
                    ahead = ahead[1:]
            elif u < U:
                jobs = [mx(u + 1, 0, 1) + (one("k", u + 2, 1) if u >= 1 else []) + mx(u + 1, 1, 4),
                        mx(u + 1, 4, 8), one("turn", u + 1) + one("q", u + 2), one("k", u + 3)][c]
            self.order += jobs
            ended = lambda k: (s - k) // 2 - 1 if s >= 2 + k and (s - k) % 2 == 0 and (s - k) // 2 - 1 < 2 * U else None
            self.slots.append(dict(
                main=s if s < 4 * U else None,
                pv=s - 1 if 1 <= s <= 4 * U else None,
                aux=jobs,
                norm=ended(0) if self.small else None, select=ended(1), norm2=ended(1)))


INPUTS = {
    "x": (B, S, D), "ctx": (B, SC, DC),
    "a_Wq": (D, D), "a_Wk": (D, D), "a_Wv": (D, D), "a_Wo": (D, D),
    "c0_Wq": (D, 512), "c0_Wk": (DC, 512), "c0_Wv": (DC, 512), "c0_Wo": (512, D), "c0_bo": (D,),
    "m_g": (12, 2, D), "m_Wqkv": (D, 3 * D), "m_Wo": (D, D), "m_bo": (D,),
    "d_Wq": (D, D), "d_Wk": (D, D), "d_Wv": (D, D), "d_Wbeta": (D, H16), "d_Wg": (D, D), "d_Wo": (D, D),
    "d_lng": (D,), "d_lnb": (D,),
    "c1_Wq": (D, 1024), "c1_Wk": (DC, 1024), "c1_Wv": (DC, 1024), "c1_Wo": (1024, D), "c1_bo": (D,),
    "f_Wfc": (512, D), "f_lnw": (512,), "f_lnb": (512,), "f_Wpj": (D, 512),
}


def decoder(nc, g, cf, ch, out):
    Y1 = Phase("cross1", 16, 64, 12, 48, None)
    F0 = Phase("mixer", 16, 8, 8, 32, Y1)
    X0 = Phase("cross0", 8, 64, 4, 16, None)
    A0 = Phase("attn0", 16, 8, 0, 0, X0)
    phases = [A0, X0, F0, Y1]
    by_name = {ph.name: ph for ph in phases}
    X0.before = X0.values(0, 8)
    F0.before, F0.after, Y1.before = Y1.values(0, 5), Y1.values(5, 12), Y1.values(12, 16)
    aux_index = {job: i for i, job in enumerate(
        job for ph in phases for job in ph.before + ph.order + ph.after)}

    def freed(*job):
        return f"aux_free{aux_index[job] % 3}", aux_index[job] // 3 + 1

    with ExitStack() as ctx:
        def sb(name, shape, dt=F32):
            return ctx.enter_context(nc.sbuf_tensor(name, shape, dt))

        sems = {}

        def sem(name):
            if name not in sems:
                sems[name] = ctx.enter_context(nc.semaphore(name))
            return sems[name]

        cst = sb("cst", [P, NCF])
        csth = sb("csth", [P, NCH], F16)
        ident = cst[:, C_ID:C_ID + P]

        def col(i):
            return cst[:, C_MASK + i:C_MASK + i + 1]

        ones = sb("ones", [P, P])
        x = sb("x", [P, NT, D])
        xn = sb("xn", [P, NT, D])
        xnT = sb("xnT", [P, T])
        stats = sb("stats", [P, NT, 6])
        mv = sb("mv", [P, NT, 2])
        rstd = sb("rstd", [P, NT])
        rt1 = sb("rt1", [P, NT])
        rt2 = sb("rt2", [P, NT])
        ctxT = sb("ctxT", [DC, NC_T * P])
        wa = {n: sb("wa_" + n, [P, D]) for n in ("q", "k", "v")}
        wqkv = sb("wqkv", [P, 3 * D])
        WR = {(f, n): sb(f"wr_{f}_{n}", [P, 4 * P]) for f in ("attn0", "mixer") for n in "qk"}
        wo8 = {f: sb(f"wo_{f}", [P, D]) for f in ("attn0", "mixer")}
        wk_c0, wv_c0 = sb("wk_c0", [P, 512]), sb("wv_c0", [P, 512])
        wk2 = {"cross0": wk_c0[0:DC, :], "cross1": sb("wk_c1", [DC, 1024])[:, :]}
        wq2 = {"cross0": sb("wq_c0", [P, 512]), "cross1": sb("wq_c1", [P, 1024])}
        wv2 = {"cross0": wv_c0[0:DC, :], "cross1": sb("wv_c1", [DC, 1024])[:, :]}
        wo2 = {"cross0": sb("wo_c0", [P, 4, D]), "cross1": sb("wo_c1", [P, 8, D])}
        bias_out = {n: sb("bias_" + n, [P, D]) for n in ("cross0", "mixer", "cross1")}
        K1 = sb("K1", [P, 3, 2, B * SC], F16)
        K2 = sb("K2", [P, 3, 2, B * SC], F16)
        Q12 = sb("Q12", [P, 3, 4, T], F16)
        Q1, Q2 = Q12[:, :, 0:2, :], Q12[:, :, 2:4, :]
        Kr = sb("Kr", [P, 4, T], F16)
        Qr = Q12
        Kh = sb("Kh", [P, 2, B * SC], F16)
        Kl = sb("Kl", [P, 2, B * SC], F16)
        Qh = sb("Qh", [P, 2, T], F16)
        Ql = sb("Ql", [P, 2, T], F16)
        hi = sb("hi", [P, 2, T], F16)
        qn = sb("qn", [P, T], F16)
        V = sb("V", [P, NC_T, 1024])
        V8 = sb("V8", [P, NT, 16, 32])
        Pr = sb("Pr", [P, 3, 1024])
        Psum = sb("Psum", [P, 2, 512])
        mx = sb("mx", [P, 2, NT, 4])
        mrow = sb("mrow", [4, 2, T], F16)
        Zs = sb("Zs", [P, 2, 2 * S])
        zn = sb("zn", [P, 8, T])
        zt = sb("zt", [P, NT, 16, 8])
        rd8 = sb("rd8", [P, 2, 2, 4])
        qg = sb("qg", [P, D])
        gn = sb("gn", [P, 2, H16])
        n2 = sb("n2", [P, NT * H16])
        dot = sb("dot", [P, NT * H16])
        sim = sb("sim", [P, NT])
        simrow = sb("simrow", [1, B, S])
        posrow = sb("posrow", [1, B, S])
        ext = sb("ext", [1, 4])
        cls_q = sb("cls_q", [1, 2, B, S], F16)
        cls_k = sb("cls_k", [1, 2, B, S], F16)
        negx = sb("negx", [1, B * REG], F16)
        xreg = sb("xreg", [P, B * REG])
        NR = 4 * B * REG
        Qx = sb("Qx", [P, B, 4, 4, REG], F16)
        qxh = sb("qxh", [P, NR], F16)
        qxn = sb("qxn", [P, NR], F16)
        mreg = sb("mreg", [4 * REG, 8])
        PregT = sb("PregT", [P, 16, 4 * REG])
        Zreg = sb("Zreg", [P, NR])
        rreg = sb("rreg", [REG, 8, 4])
        zreg = sb("zreg", [REG, 32, 8])
        wd = {n: sb("wd_" + n, [P, D]) for n in ("q", "k", "v", "g", "o")}
        wbeta = sb("wbeta", [P, H16])
        kqn = sb("kqn", [P, 2, NT * H16])
        beta = sb("beta", [P, NT * H16])
        lng = sb("lng", [P, D])
        lnb = sb("lnb", [P, D])
        wfc, wpj, lnw1, lnb1 = wo2["cross0"], wq2["cross0"], wk_c0, wv_c0
        gam = sb("gam", [P, 8])
        fcT = sb("fcT", [P, 4, P], F16)
        pjT = sb("pjT", [P, 4, P], F16)

        def room(i):
            if i < 8:
                return zn[:, i, :]
            if i < 12:
                return V8[:, i - 8, :, :].rearrange("p h c -> p (h c)")
            return Pr[:, (i - 12) // 2, (i - 12) % 2 * 512:(i - 12) % 2 * 512 + 512]

        Preg = Pr[:, 0:2, :].rearrange("p a b -> p (a b)")[0:4 * REG, :].rearrange("p (a s) -> p a s", a=8)
        ctx_tok = Pr[:, 0, 0:NC_T * DC].rearrange("p (a c) -> p a c", c=DC)

        PS = ctx.enter_context(nc.psum_tensor("PS", [P, 6, 512], F32))
        SC3 = PS[:, 0:3, :]
        AUX = PS[:, 3:6, :]
        SCR, WORK = PS[:, 0:4, :], PS[:, 4:6, :]
        ACC = ctx.enter_context(nc.psum_tensor("ACC", [P, 2, 512], F32))

        prep_jobs = [job for ph in phases for job in ph.order if job[1] in "kq"]
        hi_count = {job: i + 1 for i, job in enumerate(prep_jobs)}
        place_count, n_placed = {}, {}
        for ph in phases:
            for u in range(0 if ph.small else ph.U):
                for kind in "kq":
                    name = f"placed_{kind}{u % 3}"
                    n_placed[name] = n_placed.get(name, 0) + 16 * (6 if kind == "k" else 2)
                    place_count[ph.name, kind, u] = (name, n_placed[name])
        big_units = [(ph, u) for ph in phases if not ph.small for u in range(ph.U)]
        big_index = {(ph.name, u): i for i, (ph, u) in enumerate(big_units)}
        big_chunks = [ph.chunk0 + s for ph in phases if not ph.small for s in range(4 * ph.U)]
        sum_count = {n: (i // 2) * 3 + (1 if i % 2 == 0 else 3) for i, n in enumerate(big_chunks)}
        row_count, n_rows = {}, [0, 0]
        for ph in phases:
            for u in range(ph.U):
                gu = ph.unit0 + u
                n_rows[gu % 2] += 16 * ph.hu
                row_count[ph.name, u] = (f"rows_set{gu % 2}", n_rows[gu % 2])


        def d_half(i, part):
            return room(10).bitcast(F16)[:, part * T:(part + 1) * T] if i == 0 else hi[:, part, :]

        def h_half(t, part):
            return room(8 + t % 2).bitcast(F16)[:, part * 512:(part + 1) * 512]

        def split_h(dve, v, t):
            dve.wait_ge(sem("hT_high"), t + 1)
            v.tensor_tensor(h_half(t, 1), WORK[:, t % 2, :], h_half(t, 0), ALU.subtract).then_inc(sem("hT_split"), 1)

        den_count = {(ph.name, a): ph.chunk0 // 2 + a + 1 for ph in phases for a in range(2 * ph.U)}
        z_count = {(ph.name, a): k * 8 + a + 1 for k, ph in enumerate((A0, F0)) for a in range(8)}

        def wait_free(engine, *job):
            name, count = freed(*job)
            engine.wait_ge(sem(name), count)

        block = ctx.enter_context(nc.Block())

        @block.sync
        def _(sp):
            def load(dst, src, name, n=1):
                sp.dma_start(dst, src).then_inc(sem(name), 16)

            def bcast(v):
                return v.unsqueeze(0).to_broadcast([P, v.shape[0]])

            load(x[:], g["x"].rearrange("b (t p) d -> p (b t) d", p=P), "x_in")
            load(cst[:], cf, "cst_in")
            for n in "qkv":
                load(wa[n][:], g["a_W" + n], "wa_in")
            load(ctx_tok, g["ctx"].rearrange("b (t p) d -> p (b t) d", p=P), "ctx_in")
            load(csth[:], ch, "csth_in")
            load(wo8["attn0"][:], g["a_Wo"], "wo8_in")
            load(wo8["mixer"][:], g["m_Wo"], "wo8_in")
            for f, c in (("cross0", "c0"), ("cross1", "c1")):
                load(wk2[f], g[c + "_Wk"], f + "_w_in")
                load(wq2[f][:], g[c + "_Wq"], f + "_w_in")
                load(wv2[f], g[c + "_Wv"], f + "_w_in")
                load(wo2[f][:], g[c + "_Wo"].rearrange("(u p) n -> p u n", p=P), f + "_w_in")
                load(bias_out[f][:], bcast(g[c + "_bo"]), f + "_w_in")
            load(wqkv[:], g["m_Wqkv"], "wm_in")
            load(qg[:], bcast(g["m_g"][0, 0, :]), "wm_in")
            load(bias_out["mixer"][:], bcast(g["m_bo"]), "wm_in")
            for n in "qkvgo":
                load(wd[n][:], g["d_W" + n], "wd_in")
            load(wbeta[:], g["d_Wbeta"], "wd_in")
            load(lng[:], bcast(g["d_lng"]), "wd_in")
            load(lnb[:], bcast(g["d_lnb"]), "wd_in")
            def rows(ph, u):
                wait_free(sp, ph.name, "turn", u, 0)
                name, _ = row_count[ph.name, u]
                for j in range(ph.hu):
                    dst = Qr[32 * j + 24:32 * j + 25, u % 3, j, :] if ph.small else \
                        Q2[64 - 64 * j:65 - 64 * j, u % 3, j, :]
                    sp.dma_start(dst, mrow[j:j + 1, (ph.unit0 + u) % 2, :]).then_inc(sem(name), 16)

            def place(ph, kind, u):
                if kind == "q":
                    sp.wait_ge(sem("q_low"), big_index[ph.name, u] + 1)
                for i in range(2 if kind == "k" else 0):
                    wait_free(sp, ph.name, kind, u, i)
                r, e = u % 3, big_index[ph.name, u] % 2
                name, _ = place_count[ph.name, kind, u]
                for h in range(2):
                    own, other = slice(64 * h, 64 * h + 64), slice(64 - 64 * h, P - 64 * h)
                    if kind == "k":
                        pairs = ((K1[own, r, h, :], Kh[own, e, :]), (K1[other, r, h, :], Kh[own, e, :]),
                                 (K2[own, r, h, :], Kl[own, e, :]))
                    else:
                        pairs = ((Q1[other, r, h, :], Ql[own, e, :]),)
                    for dst, src in pairs:
                        sp.dma_start(dst, src).then_inc(sem(name), 16)

            sp.wait_ge(sem("k2_set"), 6)
            for ph in phases:
                if ph is F0:
                    sp.wait_ge(sem("x_done"), 2)
                    load(wfc[:], g["f_Wfc"].rearrange("(a p) d -> p a d", p=P), "wf_in")
                    load(wpj[:], g["f_Wpj"], "wf_in")
                    load(lnw1[:], bcast(g["f_lnw"]), "wf_in")
                    load(lnb1[:], bcast(g["f_lnb"]), "wf_in")
                for name, kind, u, i in ph.order:
                    if kind == "turn":
                        rows(ph, u)
                    elif not by_name[name].small and (kind, i) in (("k", 1), ("q", 0)):
                        place(by_name[name], kind, u)
            sp.wait_ge(sem("y_done"), 1)
            sp.dma_start(out.rearrange("b (t p) d -> p (b t) d", p=P), x[:]).then_inc(sem("out_done"), 16)
            sp.wait_ge(sem("out_done"), 16)

        @block.gpsimd
        def _(pool):
            done = {}

            def alone(ins, name):
                done[name] = done.get(name, 0) + 1
                ins.then_inc(sem(name), 1)
                pool.wait_ge(sem(name), done[name])

            alone(nc.gpsimd.memset(V8[:], 0.0), "v8_zero")
            alone(nc.gpsimd.memset(V8[:].rearrange("p t h c -> p (t h) c")[:, :, 8:9], 1.0), "v8_set")
            alone(nc.gpsimd.memset(ones[:], 1.0), "ones_set")
            alone(nc.gpsimd.memset(negx[:], 1.0), "ones_set")
            for h in range(2):
                for r in range(3):
                    alone(nc.gpsimd.memset(K2[64 - 64 * h:P - 64 * h, r, h, :].bitcast(F32), 0.0), "k2_zero")
                for r in range(3):
                    alone(nc.gpsimd.memset(K2[64 - 64 * h:65 - 64 * h, r, h, :], 1.0), "k2_set")
            def delta_sums():
                by_tok = lambda r: r.rearrange("p (t d) -> p t d", t=NT)
                pool.wait_ge(sem("wd_in"), 16 * 8)
                pool.wait_ge(sem("d_gate"), 1)
                pool.wait_ge(sem("d_turned"), 4)
                for i, w in enumerate((lng, lnb)):
                    nc.gpsimd.tensor_tensor(by_tok(room(4 + i)), by_tok(room(3)), w[:].unsqueeze(1).to_broadcast([P, NT, D]),
                                            ALU.mult).then_inc(sem("gates_set"), 1)
                for j in range(1, 8):
                    pool.wait_ge(sem("d_prod"), j + 1)
                    before = room(12) if j == 1 else room(0)
                    alone(nc.gpsimd.tensor_tensor(room(0), before, room(12 + j % 2), ALU.add), "d_sum")

            for ph in phases:
                if ph is Y1:
                    delta_sums()
                for c in range(0 if ph.small else 4 * ph.U):
                    n = ph.chunk0 + c
                    a = n // 2
                    if a >= 2 and n % 2 == 0:
                        pool.wait_ge(sem("den_ready"), a - 1)
                    pool.wait_ge(sem("exp_done"), 2 * n + 2)
                    p = Pr[:, n % 3, :].rearrange("p (k hq) -> p k hq", k=2)
                    t = Psum[:, a % 2, :]
                    if n % 2 == 0:
                        alone(nc.gpsimd.tensor_tensor(t, p[:, 0, :], p[:, 1, :], ALU.add), "sums_done")
                    else:
                        alone(nc.gpsimd.tensor_tensor(t, t, p[:, 0, :], ALU.add), "sums_done")
                        alone(nc.gpsimd.tensor_tensor(t, t, p[:, 1, :], ALU.add), "sums_done")

        @block.tensor
        def _(pe):
            mm = nc.tensor.matmul

            def norm_transpose(n, jobs=()):
                for job in jobs:
                    aux(job)
                pe.wait_ge(sem("xn_done"), n + 1)
                for t in range(NT):
                    last = nc.tensor.transpose(SCR[:, 1, t * P:(t + 1) * P], xn[:, t, :], ident)
                last.then_inc(sem("xnT_ready"), 1)
                pe.wait_ge(sem("xnT_done"), n + 1)
                for job in jobs[-3:]:
                    wait_free(pe, *job)

            def aux(job):
                name, kind, u, i = job
                ph = by_name[name]
                n = aux_index[job]
                dst = AUX[:, n % 3, :]
                if n >= 3:
                    pe.wait_ge(sem(f"aux_free{n % 3}"), n // 3)
                if kind in "kq" and ph.small:
                    classes = ph.name == "mixer"
                    last = mm(dst, WR[ph.name, kind][:, u * P:(u + 1) * P], xnT[:], start=True, stop=not classes)
                    if classes:
                        rows = cls_k if kind == "k" else cls_q
                        for c, r in enumerate((R_POS, R_NEG)):
                            last = mm(dst, csth[0:1, r:r + P], rows[0:1, c, :, :].rearrange("p b s -> p (b s)"),
                                      start=False, stop=(c == 1))
                elif kind == "k":
                    last = mm(dst, wk2[ph.name][:, u * P:(u + 1) * P], ctxT[:, i * SC:(i + 1) * SC], start=True, stop=True)
                elif kind == "q":
                    last = mm(dst, wq2[ph.name][:, u * P:(u + 1) * P], xnT[:], start=True, stop=True)
                elif kind == "v":
                    t, half = divmod(i, ph.heads // 8)
                    last = mm(dst, ctxT[:, t * P:(t + 1) * P], wv2[ph.name][:, half * 512:(half + 1) * 512],
                              start=True, stop=True)
                elif kind == "max":
                    if i == 0:
                        prepared(ph, u)
                    t, b = i // 2, i // 4
                    if ph.small:
                        for e in range(2):
                            j = 2 * (i % 2) + e
                            last = mm(dst[:, e * S:(e + 1) * S], Qr[:, u % 3, j, t * P:(t + 1) * P],
                                      Kr[:, u, b * S:(b + 1) * S], start=True, stop=True)
                    else:
                        last = mm(dst, Q1[:, u % 3, i % 2, t * P:(t + 1) * P],
                                  K1[:, u % 3, i % 2, b * SC:(b + 1) * SC], start=True, stop=True)
                else:
                    for last_max in (5, 6, 7):
                        wait_free(pe, name, "max", u, last_max)
                    for t in range(NT):
                        last = nc.tensor.transpose(dst[0:ph.hu, t * P:(t + 1) * P],
                                                   mx[:, u % 2, t, 0:ph.hu], ident)
                last.then_inc(sem("aux_ready"), 1)

            def prepared(ph, u):
                if ph.small:
                    wait_free(pe, ph.name, "k", u, 0)
                    wait_free(pe, ph.name, "q", u, 0)
                else:
                    for kind in "kq":
                        name, count = place_count[ph.name, kind, u]
                        pe.wait_ge(sem(name), count)
                    wait_free(pe, ph.name, "q", u, 0)

            def scores(ph, s, half):
                u, c = divmod(s, 4)
                b, k = c // 2, c % 2
                n = ph.chunk0 + s
                m = 2 * n + half
                if m >= 3:
                    pe.wait_ge(sem("exp_done"), m - 2)
                if half == 0 and c == 0:
                    name, count = row_count[ph.name, u]
                    pe.wait_ge(sem(name), count)
                    prepared(ph, u)
                dst = SC3[:, m % 3, :]
                if ph.small:
                    last = mm(dst, Kr[:, u, b * S + k * P:b * S + (k + 1) * P],
                              Qr[:, u % 3, 2 * half:2 * half + 2, b * S:(b + 1) * S], start=True, stop=True)
                else:
                    keys = slice(b * SC + (2 * k + half) * P, b * SC + (2 * k + half + 1) * P)
                    for h in range(2):
                        for first, (K_, Q_) in enumerate(((K1, Q1), (K2, Q2))):
                            last = mm(dst[:, h * S:(h + 1) * S], K_[:, u % 3, h, keys],
                                      Q_[:, u % 3, h, b * S:(b + 1) * S], start=(first == 0), stop=(first == 1))
                last.then_inc(sem("scores_ready"), 1)

            def values(ph, s, half):
                u, c = divmod(s, 4)
                b, k = c // 2, c % 2
                n = ph.chunk0 + s
                a = n // 2
                pe.wait_ge(sem("exp_done"), 2 * n + 1 + half)
                if half == 0:
                    if k == 0 and a >= 2:
                        pe.wait_ge(sem("norm_done"), a - 1)
                    if s == 0 and not ph.small:
                        for i in range(3):
                            wait_free(pe, ph.name, "v", 0, NC_T * ph.heads // 8 - 3 + i)
                if ph.small:
                    if half == 0:
                        return
                    for j in range(4):
                        last = mm(ACC[32 * j:32 * j + 32, a % 2, 0:S], V8[:, 2 * b + k, 4 * u + j, :],
                                  Pr[:, n % 3, j * S:(j + 1) * S], start=(k == 0), stop=(k == 1),
                                  tile_position=(0, 32 * j))
                else:
                    kk = half
                    kt = 2 * k + kk
                    for h in range(2):
                        last = mm(ACC[64 * h:64 * h + 64, a % 2, 0:S],
                                  V[:, b * 4 + kt, (2 * u + h) * 64:(2 * u + h + 1) * 64],
                                  Pr[:, n % 3, (2 * kk + h) * S:(2 * kk + h + 1) * S],
                                  start=(kt == 0), stop=(kt == 3), tile_position=(0, 64 * h))
                if half == 1:
                    last.then_inc(sem("values_done"), 1)

            def select(ph, a):
                n = ph.chunk0 // 2 + a
                if ph.small:
                    pe.wait_ge(sem("z_copied"), z_count[ph.name, a])
                    for t in range(2):
                        last = nc.tensor.transpose(ACC[:, n % 2, S + t * P:S + (t + 1) * P],
                                                   Zs[:, n % 2, t * P:(t + 1) * P], ident)
                else:
                    pe.wait_ge(sem("sums_done"), sum_count[2 * n + 1])
                    for h in range(2):
                        last = mm(ACC[64 * h:64 * h + 64, n % 2, S:2 * S], ones[:, 0:64],
                                  Psum[:, n % 2, h * S:(h + 1) * S], start=True, stop=True,
                                  tile_position=(0, 64 * h))
                last.then_inc(sem("den_ready"), 1)

            def run_units(ph):
                for job in ph.head:
                    aux(job)
                for slot in ph.slots:
                    jobs = list(slot["aux"])
                    parts = []
                    if slot["main"] is not None:
                        parts += [(scores, slot["main"], 0), (scores, slot["main"], 1)]
                    if slot["pv"] is not None:
                        parts += [(values, slot["pv"], 0), (values, slot["pv"], 1)]
                    while parts or jobs:
                        if parts:
                            f, s, half = parts.pop(0)
                            f(ph, s, half)
                        if jobs:
                            aux(jobs.pop(0))
                    if slot["select"] is not None:
                        select(ph, slot["select"])
                for job in ph.order[-3:]:
                    wait_free(pe, *job)

            def project_out(ph, w):
                a = (ph.chunk0 + 4 * ph.U) // 2
                pe.wait_ge(sem("norm_done"), a)
                if ph.name == "mixer":
                    pe.wait_ge(sem("regs_merged"), 1)
                if ph.small:
                    for t in range(NT):
                        last = nc.tensor.transpose(SCR[:, 1, t * P:(t + 1) * P],
                                                   zt[:, t, :, :].rearrange("p h d -> p (h d)"), ident)
                    last.then_inc(sem("zT_ready"), 1)
                    pe.wait_ge(sem("zT_done"), 1 if ph.name == "attn0" else 2)
                    for t in range(NT):
                        last = mm(SCR[:, 0, t * P:(t + 1) * P], xnT[:, t * P:(t + 1) * P], w, start=True, stop=True)
                    last.then_inc(sem("out_ready"), 1)
                    return
                for t in range(NT):
                    for u in range(ph.U):
                        last = mm(SCR[:, 0, t * P:(t + 1) * P], zn[:, u, t * P:(t + 1) * P], w[:, u, :],
                                  start=(u == 0), stop=(u == ph.U - 1))
                last.then_inc(sem("out_ready"), 1)

            def values_small(w, n):
                for t in range(NT):
                    last = mm(SCR[:, 2, t * P:(t + 1) * P], xnT[:, t * P:(t + 1) * P], w, start=True, stop=True)
                last.then_inc(sem("v8_ready"), 1)

            pe.wait_ge(sem("cst_in"), 16)
            pe.wait_ge(sem("ctx_in"), 16)
            for t in range(NC_T):
                last = nc.tensor.transpose(ACC[0:DC, t // 4, (t % 4) * P:(t % 4 + 1) * P], ctx_tok[:, t, :], ident)
            last.then_inc(sem("ctxT_ready"), 1)

            norm_transpose(0)
            pe.wait_ge(sem("wa_in"), 48)
            pe.wait_ge(sem("ctxT_done"), 1)
            values_small(wa["v"][:], 0)
            pe.wait_ge(sem("wr_done"), 1)
            pe.wait_ge(sem("v8_done"), 1)
            pe.wait_ge(sem("cross0_w_in"), 16 * 5)
            run_units(A0)
            pe.wait_ge(sem("wo8_in"), 32)
            project_out(A0, wo8["attn0"][:])

            norm_transpose(1, X0.before)
            pe.wait_ge(sem("ones_set"), 2)
            pe.wait_ge(sem("x_done"), 1)
            run_units(X0)
            project_out(X0, wo2["cross0"])

            pe.wait_ge(sem("cross1_w_in"), 16 * 5)
            norm_transpose(2, F0.before)
            pe.wait_ge(sem("wm_in"), 48)
            pe.wait_ge(sem("x_done"), 2)
            for t in range(NT):
                last = mm(SCR[:, 0, t * P:(t + 1) * P], xnT[:, t * P:(t + 1) * P], wqkv[:, 0:D], start=True, stop=True)
            last.then_inc(sem("qtok_ready"), 1)
            values_small(wqkv[:, 2 * D:3 * D], 1)
            pe.wait_ge(sem("sim_done"), 1)
            for t in range(NT):
                last = nc.tensor.transpose(SCR[0:1, 3, t * P:(t + 1) * P], sim[:, t:t + 1], ident)
            last.then_inc(sem("simrow_ready"), 1)
            pe.wait_ge(sem("wr_done"), 2)
            pe.wait_ge(sem("xreg_done"), 1)
            pe.wait_ge(sem("csth_in"), 16)
            qx_out = SCR[:, 1, 0:NR].rearrange("p (b u r) -> p b u r", b=B, u=4)
            for u in range(4):
                mm(qx_out[:, :, u, :], WR["mixer", "q"][:, u * P:(u + 1) * P], xreg[:], start=True, stop=False)
                last = mm(qx_out[:, :, u, :], csth[0:1, R_NEG:R_NEG + P], negx[:], start=False, stop=True)
            last.then_inc(sem("qx_ready"), 1)
            pe.wait_ge(sem("cls_done"), 1)
            pe.wait_ge(sem("v8_done"), 2)
            pe.wait_ge(sem("qx_done"), 1)
            run_units(F0)
            for u in range(4):
                for b in range(B):
                    last = mm(SCR[0:4 * REG, u, b * S:(b + 1) * S],
                              Qx[:, b, u, :, :].rearrange("p j r -> p (j r)"),
                              Kr[:, u, b * S:(b + 1) * S], start=True, stop=True)
            last.then_inc(sem("reg_scores"), 1)
            pe.wait_ge(sem("reg_exp"), 1)
            for ub in range(8):
                for k in range(2):
                    c = (ub * 2 + k) * 4 * REG
                    last = nc.tensor.transpose(WORK[:, 0, c:c + 4 * REG], Preg[:, ub, k * P:(k + 1) * P],
                                               ident[0:4 * REG, 0:4 * REG])
            last.then_inc(sem("regT_ready"), 1)
            pe.wait_ge(sem("regT_done"), 1)
            for u in range(4):
                for b in range(B):
                    for k in range(2):
                        for j in range(4):
                            c = (u * B + b) * REG
                            last = mm(WORK[32 * j:32 * j + 32, 1, c:c + REG], V8[:, 2 * b + k, 4 * u + j, :],
                                      PregT[:, (u * B + b) * 2 + k, j * REG:(j + 1) * REG],
                                      start=(k == 0), stop=(k == 1), tile_position=(0, 32 * j))
            last.then_inc(sem("reg_z"), 1)
            pe.wait_ge(sem("reg_z_done"), 1)
            for ub in range(8):
                last = nc.tensor.transpose(SCR[0:REG, ub // 4, (ub % 4) * P:(ub % 4 + 1) * P],
                                           Zreg[:, ub * REG:(ub + 1) * REG], ident)
            last.then_inc(sem("reg_den"), 1)
            project_out(F0, wo8["mixer"][:])

            norm_transpose(3, F0.after)
            pe.wait_ge(sem("wd_in"), 16 * 8)
            pe.wait_ge(sem("x_done"), 3)

            def by_token(dst, w, width):
                for t in range(NT):
                    last = mm(dst[:, t * width:(t + 1) * width], xnT[:, t * P:(t + 1) * P], w, start=True, stop=True)
                last.then_inc(sem("d_proj"), 1)

            by_token(SCR[:, 0, :], wd["k"][:], P)
            by_token(SCR[:, 1, :], wd["q"][:], P)
            by_token(SCR[:, 3, :], wbeta[:], H16)
            by_token(SCR[:, 2, :], wd["v"][:], P)
            by_token(ACC[:, 0, :], wd["g"][:], P)
            for i, (src, dst) in enumerate(((4, WORK[:, 0, :]), (5, WORK[:, 1, :]), (14, ACC[:, 1, :]), (15, SCR[:, 3, :]))):
                pe.wait_ge(sem("d_token"), i + 1)
                for t in range(NT):
                    last = nc.tensor.transpose(dst[:, t * P:(t + 1) * P], room(src)[:, t * P:(t + 1) * P], ident)
                last.then_inc(sem("d_turned"), 1)
            pe.wait_ge(sem("d_split"), 2)
            pe.wait_ge(sem("csth_in"), 16)

            def spread(i, j):
                if j >= 2:
                    pe.wait_ge(sem("d_kfree" if i == 0 else "d_prod"), j - 1)
                if i == 1 and j == 1:
                    pe.wait_ge(sem("d_terms"), 2)
                for part in range(2):
                    last = mm(SCR[:, 2 * i + j % 2, :], csth[:, R_SEL + j * P:R_SEL + (j + 1) * P],
                              d_half(i, part), start=(part == 0), stop=(part == 1))
                last.then_inc(sem("d_spread_k" if i == 0 else "d_spread_q"), 1)

            for j in range(8):
                spread(0, j)
                spread(1, j)
            pe.wait_ge(sem("d_sum"), 7)
            for t in range(NT):
                last = nc.tensor.transpose(WORK[:, 1, t * P:(t + 1) * P], room(0)[:, t * P:(t + 1) * P], ident)
            last.then_inc(sem("d_o_ready"), 1)
            pe.wait_ge(sem("d_y"), 1)
            for t in range(NT):
                last = nc.tensor.transpose(ACC[:, 1, t * P:(t + 1) * P], room(1)[:, t * P:(t + 1) * P], ident)
            last.then_inc(sem("d_yT_ready"), 1)
            pe.wait_ge(sem("d_yT"), 1)
            for t in range(NT):
                last = mm(SCR[:, 0, t * P:(t + 1) * P], room(2)[:, t * P:(t + 1) * P], wd["o"][:], start=True, stop=True)
            last.then_inc(sem("out_ready"), 1)

            norm_transpose(4, Y1.before)
            pe.wait_ge(sem("x_done"), 4)
            run_units(Y1)
            project_out(Y1, wo2["cross1"])

            pe.wait_ge(sem("abs_sums"), 1)
            pe.wait_ge(sem("x_done"), 5)
            mm(ACC[:, 0, 0:2], ones[:], gam[:, 0:2], start=True, stop=True).then_inc(sem("gamma_ready"), 1)
            pe.wait_ge(sem("ternary"), 1)
            for a in range(4):
                nc.tensor.transpose(WORK[:, 0, a * P:(a + 1) * P], wfc[:, a, :], ident)
                last = nc.tensor.transpose(WORK[:, 1, a * P:(a + 1) * P], wpj[:, a * P:(a + 1) * P], ident)
            last.then_inc(sem("ternT_ready"), 1)
            norm_transpose(5)
            pe.wait_ge(sem("x_split"), 1)
            pe.wait_ge(sem("ternT_done"), 2)
            for t in range(NT):
                for part in range(2):
                    last = mm(SCR[:, t, :], hi[:, part, t * P:(t + 1) * P],
                              fcT[:].rearrange("p a b -> p (a b)"), start=(part == 0), stop=(part == 1))
                last.then_inc(sem("h_ready"), 1)
            for t in range(NT):
                pe.wait_ge(sem("h_norm"), t + 1)
                if t >= 2:
                    pe.wait_ge(sem("hT_split"), t - 1)
                for a in range(4):
                    last = nc.tensor.transpose(WORK[:, t % 2, a * P:(a + 1) * P],
                                               room(2 * t + 1)[:, a * P:(a + 1) * P], ident)
                last.then_inc(sem("hT_ready"), 1)
                pe.wait_ge(sem("hT_split"), t + 1)
                for a in range(4):
                    for part in range(2):
                        last = mm(ACC[:, 1, t * P:(t + 1) * P], h_half(t, part)[:, a * P:(a + 1) * P],
                                  pjT[:, a, :], start=(a == 0 and part == 0), stop=(a == 3 and part == 1))
            last.then_inc(sem("out_ready"), 1)

        @block.scalar
        def _(act):
            A = nc.scalar.activation
            wide_sums = [0]

            def inv_root(n, jobs=()):
                for job in jobs[:3]:
                    aux(job)
                act.wait_ge(sem("var_done"), n + 1)
                A(rt1[:], rt2[:], ACT.Ln).then_inc(sem("act_ln"), 1)
                act.wait_ge(sem("act_ln"), n + 1)
                A(rstd[:], rt1[:], ACT.Exp, scale=-0.5).then_inc(sem("root_done"), 1)
                for job in jobs[3:]:
                    aux(job)

            def norm_copy(n):
                act.wait_ge(sem("xnT_ready"), n + 1)
                A(xnT[:], SCR[:, 1, :], ACT.Identity).then_inc(sem("xnT_done"), 1)

            def aux(job):
                name, kind, u, i = job
                ph = by_name[name]
                if kind == "max":
                    return
                n = aux_index[job]
                src = AUX[:, n % 3, :]
                act.wait_ge(sem("aux_ready"), n + 1)
                if kind == "turn":
                    gu = ph.unit0 + u
                    if gu >= 2:
                        prev = ph if u >= 2 else phases[phases.index(ph) - 1]
                        pu = u - 2 if u >= 2 else prev.U - 2 + u
                        sent, count = row_count[prev.name, pu]
                        act.wait_ge(sem(sent), count)
                    A(mrow[0:ph.hu, gu % 2, :], src[0:ph.hu, :], ACT.Identity,
                      scale=-1.0).then_inc(sem(f"aux_free{n % 3}"), 1)
                elif kind == "v":
                    t, half = divmod(i, ph.heads // 8)
                    A(V[:, t, half * 512:(half + 1) * 512], src, ACT.Identity).then_inc(sem(f"aux_free{n % 3}"), 1)
                elif ph.small:
                    before = [j for j in prep_jobs[:hi_count[job] - 1] if j[1] == kind and by_name[j[0]].small]
                    if before:
                        wait_free(act, *before[-1])
                    bias = col(M_BIASK) if kind == "k" else 0.0
                    A(hi[:, "kq".index(kind), :], src, ACT.Identity, bias=bias).then_inc(sem("hi_done"), 1)
                else:
                    bi = big_index[name, u]
                    if bi >= 2:
                        pp, pu = big_units[bi - 2]
                        if kind == "k":
                            placed, count = place_count[pp.name, kind, pu]
                            act.wait_ge(sem(placed), count)
                        else:
                            wait_free(act, pp.name, "q", pu, 0)
                    dst = Kh[:, bi % 2, i * SC:(i + 1) * SC] if kind == "k" else Qh[:, bi % 2, :]
                    A(dst, src, ACT.Identity).then_inc(sem("hi_done"), 1)

            def run_units(ph):
                for job in ph.head:
                    aux(job)
                for slot in ph.slots:
                    jobs = list(slot["aux"])
                    for half in range(0 if slot["main"] is None else 2):
                        n = ph.chunk0 + slot["main"]
                        m = 2 * n + half
                        act.wait_ge(sem("scores_ready"), m + 1)
                        if n >= 3 and half == 0:
                            act.wait_ge(sem("values_done"), n - 2)
                            if n - 3 in sum_count:
                                act.wait_ge(sem("sums_done"), sum_count[n - 3])
                        A(Pr[:, n % 3, half * 512:(half + 1) * 512], SC3[:, m % 3, :],
                          ACT.Exp, scale=ph.scale).then_inc(sem("exp_done"), 1)
                        for job in jobs[half:half + 1]:
                            aux(job)
                    for job in jobs[2 if slot["main"] is not None else 0:]:
                        aux(job)
                    if slot["select"] is not None and not ph.small:
                        a = slot["select"]
                        n = ph.chunk0 // 2 + a
                        act.wait_ge(sem("den_ready"), den_count[ph.name, a])
                        if n >= 2:
                            act.wait_ge(sem("norm_done"), n - 1)
                        A(Zs[:, n % 2, 0:S], ACC[:, n % 2, S:2 * S], ACT.Ln).then_inc(sem("den_ln"), 1)
                        wide_sums[0] += 1
                        act.wait_ge(sem("den_ln"), wide_sums[0])
                        A(Zs[:, n % 2, S:2 * S], Zs[:, n % 2, 0:S], ACT.Exp, scale=-1.0).then_inc(sem("den_inverted"), 1)

            def project_copy(n):
                act.wait_ge(sem("zT_ready"), n)
                A(xnT[:], SCR[:, 1, :], ACT.Identity).then_inc(sem("zT_done"), 1)

            def values_small(n):
                act.wait_ge(sem("v8_ready"), n + 1)
                act.wait_ge(sem("v8_set"), 1)
                A(V8[:].rearrange("p t h c -> p (t h) c")[:, :, 0:8],
                  SCR[:, 2, :].rearrange("p (a d) -> p a d", d=8), ACT.Identity).then_inc(sem("v8_done"), 1)

            nc.scalar.preload_act_table_set(LN_EXP)
            act.wait_ge(sem("ctxT_ready"), 1)
            A(ctxT[:], ACC[0:DC, :, :].rearrange("p a b -> p (a b)"), ACT.Identity).then_inc(sem("ctxT_done"), 1)
            inv_root(0)
            norm_copy(0)
            values_small(0)
            act.wait_ge(sem("ctxT_done"), 1)
            run_units(A0)

            project_copy(1)
            inv_root(1, X0.before)
            norm_copy(1)
            run_units(X0)

            inv_root(2, F0.before)
            norm_copy(2)
            act.wait_ge(sem("qtok_ready"), 1)
            A(room(1), SCR[:, 0, :], ACT.Square).then_inc(sem("qsq_done"), 1)
            act.wait_ge(sem("norms2"), 1)
            A(n2[:], n2[:], ACT.Sqrt).then_inc(sem("norms"), 1)
            A(gn[:, 0, :], gn[:, 0, :], ACT.Sqrt).then_inc(sem("norms"), 1)
            nc.scalar.preload_act_table_set(LN_EXP)
            values_small(1)
            act.wait_ge(sem("xnT_done"), 3)
            A(xreg[:].rearrange("p (b r) -> p b r", b=B), xnT[:].rearrange("p (b s) -> p b s", b=B)[:, :, 0:REG],
              ACT.Identity).then_inc(sem("xreg_done"), 1)
            act.wait_ge(sem("qx_ready"), 1)
            A(qxh[:], SCR[:, 1, 0:NR], ACT.Identity).then_inc(sem("qxh_done"), 1)
            run_units(F0)
            act.wait_ge(sem("reg_shifted"), 1)
            A(Preg, Preg, ACT.Exp, scale=F0.scale).then_inc(sem("reg_exp"), 1)

            project_copy(2)

            inv_root(3, F0.after)
            norm_copy(3)
            for i in range(2):
                act.wait_ge(sem("d_proj"), i + 1)
                A(room(i), SCR[:, i, :], ACT.Square).then_inc(sem("d_sq"), 1)
            act.wait_ge(sem("d_proj"), 3)
            A(beta[:], SCR[:, 3, 0:NT * H16], ACT.Exp, scale=-1.0).then_inc(sem("d_ebeta"), 1)
            act.wait_ge(sem("d_n2"), 2)
            A(kqn[:], kqn[:], ACT.Sqrt).then_inc(sem("d_root"), 1)
            nc.scalar.preload_act_table_set(LN_EXP)
            act.wait_ge(sem("d_proj"), 5)
            gate = room(3)
            A(gate, ACC[:, 0, :], ACT.Exp, scale=-1.0).then_inc(sem("d_egate"), 1)
            act.wait_ge(sem("d_egate"), 1)
            A(gate, gate, ACT.Ln, bias=1.0).then_inc(sem("d_egate"), 1)
            act.wait_ge(sem("d_egate"), 2)
            A(gate, gate, ACT.Exp, scale=-1.0).then_inc(sem("d_egate"), 1)
            for i in range(2):
                act.wait_ge(sem("d_turned"), i + 1)
                A(d_half(i, 0), WORK[:, i, :], ACT.Identity).then_inc(sem("d_high"), 1)
            for i, (dst, src) in enumerate(((room(2), ACC[:, 1, :]), (room(1), SCR[:, 3, :]))):
                act.wait_ge(sem("d_turned"), i + 3)
                A(dst, src, ACT.Identity).then_inc(sem("d_terms"), 1)
            for j in range(8):
                act.wait_ge(sem("d_kk"), j + 1)
                A(room(8 + j % 2), room(8 + j % 2), ACT.Identity, bias=1.0).then_inc(sem("d_decay"), 1)
            act.wait_ge(sem("d_var"), 1)
            A(rt1[:], rt2[:], ACT.Ln).then_inc(sem("d_ln"), 1)
            act.wait_ge(sem("d_ln"), 1)
            A(rstd[:], rt1[:], ACT.Exp, scale=-0.5).then_inc(sem("d_rstd"), 1)
            act.wait_ge(sem("d_yT_ready"), 1)
            A(room(2), ACC[:, 1, :], ACT.Identity).then_inc(sem("d_yT"), 1)

            inv_root(4, Y1.before)
            norm_copy(4)
            run_units(Y1)

            act.wait_ge(sem("ternT_ready"), 1)
            A(fcT[:].rearrange("p a b -> p (a b)"), WORK[:, 0, :], ACT.Identity).then_inc(sem("ternT_done"), 1)
            A(pjT[:].rearrange("p a b -> p (a b)"), WORK[:, 1, :], ACT.Identity).then_inc(sem("ternT_done"), 1)
            inv_root(5)
            norm_copy(5)
            act.wait_ge(sem("xnT_done"), 6)
            A(hi[:, 0, :], xnT[:], ACT.Identity).then_inc(sem("x_high"), 1)
            for t in range(NT):
                act.wait_ge(sem("h_ready"), t + 1)
                A(room(2 * t), SCR[:, t, :], ACT.Gelu).then_inc(sem("gelu_done"), 1)
            nc.scalar.preload_act_table_set(LN_EXP)
            act.wait_ge(sem("h_var"), 1)
            A(rt1[:], rt2[:], ACT.Ln).then_inc(sem("h_ln"), 1)
            act.wait_ge(sem("h_ln"), 1)
            A(rstd[:], rt1[:], ACT.Exp, scale=-0.5).then_inc(sem("h_rstd"), 1)
            for t in range(NT):
                act.wait_ge(sem("hT_ready"), t + 1)
                A(h_half(t, 0), WORK[:, t % 2, :], ACT.Identity).then_inc(sem("hT_high"), 1)

        @block.vector
        def _(dve):
            v = nc.vector
            chain, wide_sums = [0], [0]

            def then(ins):
                chain[0] += 1
                ins.then_inc(sem("dve_step"), 1)
                dve.wait_ge(sem("dve_step"), chain[0])

            def refine():
                then(v.tensor_tensor(rt1[:], rstd[:], rstd[:], ALU.mult))
                then(v.tensor_tensor(rt1[:], rt1[:], rt2[:], ALU.mult))
                then(v.tensor_scalar(rt1[:], rt1[:], -0.5, 1.5, ALU.mult, ALU.add))
                then(v.tensor_tensor(rstd[:], rstd[:], rt1[:], ALU.mult))

            def variance(src, ready, name):
                for t in range(NT):
                    if ready:
                        dve.wait_ge(sem(ready), t + 1)
                    last = v.bn_stats(stats[:, t, :], src(t))
                then(last)
                for t in range(NT):
                    last = v.bn_aggr(mv[:, t, :], stats[:, t, :])
                then(last)
                v.tensor_scalar(rt2[:], mv[:, :, 1], LN_EPS, None, ALU.add).then_inc(sem(name), 1)

            def layer_norm(n):
                variance(lambda t: x[:, t, :], None, "var_done")
                dve.wait_ge(sem("root_done"), n + 1)
                refine()
                for t in range(NT):
                    last = v.tensor_scalar(xn[:, t, :], x[:, t, :], mv[:, t, 0:1], rstd[:, t:t + 1],
                                           ALU.subtract, ALU.mult)
                last.then_inc(sem("xn_done"), 1)

            def aux(job):
                name, kind, u, i = job
                ph = by_name[name]
                n = aux_index[job]
                src = AUX[:, n % 3, :]
                if kind in ("v", "turn"):
                    return
                if kind == "max":
                    dve.wait_ge(sem("aux_ready"), n + 1)
                    t = i // 2
                    if ph.small:
                        e = 2 * (i % 2)
                        last = v.tensor_reduce(mx[:, u % 2, t, e:e + 2], src.rearrange("p (a s) -> p a s", a=2), AX, ALU.max)
                    else:
                        last = v.tensor_reduce(mx[:, u % 2, t, i % 2:i % 2 + 1], src, AX, ALU.max)
                else:
                    dve.wait_ge(sem("hi_done"), hi_count[job])
                    if ph.small and kind == "k":
                        last = v.scalar_tensor_tensor(Kr[:, u, :], hi[:, 0, :], col(M_NK), src, ALU.mult, ALU.add)
                    elif ph.small:
                        then(v.scalar_tensor_tensor(qn[:], hi[:, 1, :], col(M_NQ), src, ALU.mult, ALU.add))
                        for j in range(4):
                            last = v.tensor_scalar(Qr[:, u % 3, j, :], qn[:], col(M_BLK + j), None, ALU.mult)
                    else:
                        bi = big_index[name, u]
                        e = bi % 2
                        if kind == "q" and bi >= 2:
                            pp, pu = big_units[bi - 2]
                            placed, count = place_count[pp.name, "q", pu]
                            dve.wait_ge(sem(placed), count)
                        keys = slice(i * SC, (i + 1) * SC)
                        high, low = (Kh[:, e, keys], Kl[:, e, keys]) if kind == "k" else (Qh[:, e, :], Ql[:, e, :])
                        last = v.tensor_tensor(low, src, high, ALU.subtract)
                        if kind == "q":
                            last.then_inc(sem("q_low"), 1)
                            for h in range(2):
                                own = slice(64 * h, 64 * h + 64)
                                for Q_ in (Q1, Q2):
                                    last = v.tensor_copy(Q_[own, u % 3, h, :], high[own, :])
                last.then_inc(sem(f"aux_free{n % 3}"), 1)

            def norm(ph, a, part):
                n = ph.chunk0 // 2 + a
                u, b = divmod(a, 2)
                if part == 0:
                    if n >= 2:
                        dve.wait_ge(sem("norm_done"), n - 1)
                    dve.wait_ge(sem("values_done"), ph.chunk0 + 2 * a + 2)
                    v.tensor_copy(Zs[:, n % 2, 0:S], ACC[:, n % 2, 0:S]).then_inc(sem("z_copied"), 1)
                    return
                if not ph.small:
                    dst, t, r = zn[:, u, b * S:(b + 1) * S], Zs[:, n % 2, 0:S], Zs[:, n % 2, S:2 * S]
                    wide_sums[0] += 1
                    dve.wait_ge(sem("den_inverted"), wide_sums[0])
                    then(v.tensor_tensor(t, ACC[:, n % 2, S:2 * S], r, ALU.mult))
                    then(v.tensor_tensor(dst, ACC[:, n % 2, 0:S], r, ALU.mult))
                    v.scalar_tensor_tensor(dst, t, 2.0, dst, ALU.subtract, ALU.mult).then_inc(sem("norm_done"), 1)
                    return
                dve.wait_ge(sem("den_ready"), den_count[ph.name, a])
                z = ACC[:, n % 2, S:2 * S].rearrange("p (t j c) -> p t j c", t=2, j=4)
                r = rd8[:, n % 2, :, :]
                then(v.reciprocal(r, z[:, :, :, 8]))
                last = v.tensor_tensor(zt[:, 2 * b:2 * b + 2, 4 * u:4 * u + 4, :], z[:, :, :, 0:8],
                                       r.unsqueeze(3).to_broadcast([P, 2, 4, 8]), ALU.mult)
                last.then_inc(sem("norm_done"), 1)

            def run_units(ph):
                for job in ph.head:
                    aux(job)
                for slot in ph.slots:
                    for job in slot["aux"]:
                        aux(job)
                    if slot["norm2"] is not None:
                        norm(ph, slot["norm2"], 1)
                    if slot["norm"] is not None:
                        norm(ph, slot["norm"], 0)

            def residual(n, bias=None, also=None, negative=False):
                if bias is not None:
                    then(v.tensor_tensor(x[:], x[:], bias[:].unsqueeze(1).to_broadcast([P, NT, D]), ALU.add))
                if also is not None:
                    then(v.tensor_tensor(x[:], x[:], also[:], ALU.add))
                dve.wait_ge(sem("out_ready"), n + 1)
                src = ACC[:, 1, :] if n == 5 else SCR[:, 0, :]
                last = v.tensor_tensor(x[:], x[:], src.rearrange("p (t d) -> p t d", d=D),
                                       ALU.subtract if negative else ALU.add)
                last.then_inc(sem("x_done" if n < 5 else "y_done"), 1)
                if n < 5:
                    dve.wait_ge(sem("x_done"), n + 1)

            def repeat(f, srcs, n):
                for which, src in srcs:
                    w = WR[f, which][:].rearrange("p (h r d) -> p h r d", h=16, r=4)
                    v.memset(w[:, :, 3, :], 0.0)
                    for r in range(3):
                        last = v.tensor_copy(w[:, :, r, :], src.rearrange("p (h d) -> p h d", h=16))
                last.then_inc(sem("wr_done"), 1)

            dve.wait_ge(sem("x_in"), 16)
            layer_norm(0)
            dve.wait_ge(sem("cst_in"), 16)
            dve.wait_ge(sem("wa_in"), 48)
            repeat("attn0", (("q", wa["q"][:]), ("k", wa["k"][:])), 0)
            run_units(A0)
            residual(0, also=xn)

            layer_norm(1)
            run_units(X0)
            dve.wait_ge(sem("cross0_w_in"), 16 * 5)
            residual(1, bias=bias_out["cross0"], negative=True)

            layer_norm(2)
            dve.wait_ge(sem("wm_in"), 48)
            repeat("mixer", (("q", wqkv[:, 0:D]), ("k", wqkv[:, D:2 * D])), 1)
            then(v.tensor_tensor(room(2)[:, 0:D], qg[:], qg[:], ALU.mult))
            then(v.tensor_reduce(gn[:, 0, :], room(2)[:, 0:D].rearrange("p (h d) -> p h d", d=8), AX, ALU.add))
            dve.wait_ge(sem("qsq_done"), 1)
            v.tensor_reduce(n2[:], room(1).rearrange("p (a d) -> p a d", d=8), AX, ALU.add).then_inc(sem("norms2"), 1)
            then(v.tensor_tensor(room(0).rearrange("p (t c) -> p t c", t=NT), SCR[:, 0, :].rearrange("p (t c) -> p t c", t=NT),
                                 qg[:].unsqueeze(1).to_broadcast([P, NT, D]), ALU.mult))
            then(v.tensor_reduce(dot[:], room(0).rearrange("p (a d) -> p a d", d=8), AX, ALU.add))
            dve.wait_ge(sem("norms"), 2)
            then(v.reciprocal(n2[:], n2[:]))
            then(v.reciprocal(gn[:, 1, :], gn[:, 0, :]))
            then(v.tensor_tensor(dot[:], dot[:], n2[:], ALU.mult))
            dot3 = dot[:].rearrange("p (t h) -> p t h", t=NT)
            then(v.tensor_tensor(dot3, dot3, gn[:, 1, :].unsqueeze(1).to_broadcast([P, NT, H16]), ALU.mult))
            then(v.tensor_reduce(sim[:], dot3, AX, ALU.add))
            v.tensor_scalar(sim[:], sim[:], 1.0 / H16, None, ALU.mult).then_inc(sem("sim_done"), 1)
            dve.wait_ge(sem("simrow_ready"), 1)
            then(v.tensor_copy(simrow[:].rearrange("p b s -> p (b s)"), SCR[0:1, 3, :]))
            for i, op in enumerate((ALU.min, ALU.max)):
                then(v.tensor_reduce(ext[:, i:i + 1], simrow[:, :, REG:S], mybir.AxisListType.XY, op))
            then(v.tensor_tensor(ext[:, 2:3], ext[:, 1:2], ext[:, 0:1], ALU.subtract))
            then(v.reciprocal(ext[:, 3:4], ext[:, 2:3]))
            then(v.tensor_scalar(simrow[:], simrow[:], ext[:, 0:1], ext[:, 3:4], ALU.subtract, ALU.mult))
            then(v.tensor_scalar(posrow[:], simrow[:], 0.9, None, ALU.is_gt))
            then(v.tensor_copy(cls_q[:, 0, :, :], posrow[:]))
            then(v.tensor_scalar(cls_q[:, 1, :, :], posrow[:], -1.0, 1.0, ALU.mult, ALU.add))
            then(v.tensor_scalar(cls_k[:, 0, :, :], posrow[:], BIG, -BIG, ALU.mult, ALU.add))
            then(v.tensor_scalar(cls_k[:, 1, :, :], posrow[:], -BIG, None, ALU.mult))
            v.memset(cls_q[:, 0, :, 0:REG], 1.0)
            v.memset(cls_q[:, 1, :, 0:REG], 0.0)
            then(v.memset(cls_k[:, 0, :, 0:REG], 0.0))
            v.memset(cls_k[:, 1, :, 0:REG], 0.0).then_inc(sem("cls_done"), 1)
            dve.wait_ge(sem("qxh_done"), 1)
            then(v.scalar_tensor_tensor(qxn[:], qxh[:], col(M_NQ), SCR[:, 1, 0:NR], ALU.mult, ALU.add))
            for j in range(4):
                last = v.tensor_scalar(Qx[:, :, :, j, :].rearrange("p b u r -> p (b u) r"),
                                       qxn[:].rearrange("p (a r) -> p a r", r=REG), col(M_BLK + j), None, ALU.mult)
            last.then_inc(sem("qx_done"), 1)
            run_units(F0)
            dve.wait_ge(sem("reg_scores"), 1)
            rs = SCR[0:4 * REG, :, :].rearrange("p u (b s) -> p (u b) s", b=B)
            then(v.tensor_reduce(mreg[:], rs, AX, ALU.max))
            v.tensor_tensor(Preg, rs, mreg[:].unsqueeze(2).to_broadcast([4 * REG, 8, S]), ALU.subtract)\
                .then_inc(sem("reg_shifted"), 1)
            dve.wait_ge(sem("regT_ready"), 1)
            v.tensor_copy(PregT[:].rearrange("p a b -> p (a b)"), WORK[:, 0, 0:16 * 4 * REG]).then_inc(sem("regT_done"), 1)
            dve.wait_ge(sem("reg_z"), 1)
            v.tensor_copy(Zreg[:], WORK[:, 1, 0:NR]).then_inc(sem("reg_z_done"), 1)
            dve.wait_ge(sem("reg_den"), 1)
            zrt = SCR[0:REG, 0:2, :].rearrange("p a b -> p (a b)").rearrange("p (u b j c) -> p (u b) j c", u=4, b=B, j=4)
            then(v.reciprocal(rreg[:], zrt[:, :, :, 8]))
            then(v.tensor_scalar(rreg[:], rreg[:], 0.5, None, ALU.mult))
            then(v.tensor_tensor(zreg[:].rearrange("p (a j) d -> p a j d", j=4), zrt[:, :, :, 0:8],
                                 rreg[:].unsqueeze(3).to_broadcast([REG, 8, 4, 8]), ALU.mult))
            for b in range(B):
                z = zt[0:REG, 2 * b, :, :].rearrange("p (u j) d -> p u (j d)", u=4)
                last = v.scalar_tensor_tensor(z, z, 0.5, zreg[:].rearrange(
                    "p (u b j) d -> p u b (j d)", u=4, b=B)[:, :, b, :], ALU.mult, ALU.add)
            last.then_inc(sem("regs_merged"), 1)
            residual(2, bias=bias_out["mixer"])

            layer_norm(3)
            dve.wait_ge(sem("wd_in"), 16 * 8)
            heads = lambda r: r.rearrange("p (a d) -> p a d", d=8)
            over = lambda r: r.unsqueeze(2).to_broadcast([P, NT * H16, 8])
            for i in range(2):
                dve.wait_ge(sem("d_sq"), i + 1)
                v.tensor_reduce(kqn[:, i, :], heads(room(i)), AX, ALU.add).then_inc(sem("d_n2"), 1)
            dve.wait_ge(sem("d_ebeta"), 1)
            then(v.tensor_scalar(beta[:], beta[:], 1.0, None, ALU.add))
            then(v.reciprocal(beta[:], beta[:]))
            dve.wait_ge(sem("d_root"), 1)
            then(v.tensor_scalar(kqn[:], kqn[:], 1e-12, None, ALU.max))
            then(v.reciprocal(kqn[:], kqn[:]))
            for i in range(2):
                last = v.tensor_tensor(heads(room(4 + i)), heads(SCR[:, i, :]), over(kqn[:, i, :]), ALU.mult)
                last.then_inc(sem("d_token"), 1)
            dve.wait_ge(sem("d_token"), 1)
            v.scalar_tensor_tensor(heads(room(14)), heads(room(4)), -1.0, over(beta[:]), ALU.mult, ALU.mult)\
                .then_inc(sem("d_token"), 1)
            dve.wait_ge(sem("d_proj"), 4)
            v.tensor_tensor(heads(room(15)), heads(SCR[:, 2, :]), over(beta[:]), ALU.mult).then_inc(sem("d_token"), 1)
            for i in range(2):
                dve.wait_ge(sem("d_high"), i + 1)
                v.tensor_tensor(d_half(i, 1), WORK[:, i, :], d_half(i, 0), ALU.subtract).then_inc(sem("d_split"), 1)
            gate, kb, vb = room(3), room(2), room(1)
            dve.wait_ge(sem("d_egate"), 3)
            v.tensor_tensor(gate, gate, ACC[:, 0, :], ALU.mult).then_inc(sem("d_gate"), 1)

            def recur(j):
                dve.wait_ge(sem("d_decay"), j + 1)
                if j >= 1:
                    dve.wait_ge(sem("d_prod"), j)
                for b in range(B):
                    ts = slice(b * S, (b + 1) * S)
                    last = v.tensor_tensor_scan(room(11)[:, ts], room(8 + j % 2)[:, ts], room(6 + j % 2)[:, ts],
                                                0.0, ALU.mult, ALU.add)
                    if b == 0:
                        last.then_inc(sem("d_scan"), 1)
                last.then_inc(sem("d_scan"), 1)
                dve.wait_ge(sem("d_scan"), 2 * j + 2)
                if j >= 2:
                    dve.wait_ge(sem("d_sum"), max(1, j - 2))
                dve.wait_ge(sem("d_spread_q"), j + 1)
                v.tensor_tensor(room(12 + j % 2), room(11), SCR[:, 2 + j % 2, :], ALU.mult).then_inc(sem("d_prod"), 1)

            dve.wait_ge(sem("d_terms"), 2)
            for j in range(8):
                dve.wait_ge(sem("d_spread_k"), j + 1)
                v.tensor_tensor(room(8 + j % 2), SCR[:, j % 2, :], kb, ALU.mult).then_inc(sem("d_kk"), 1)
                v.tensor_tensor(room(6 + j % 2), SCR[:, j % 2, :], vb, ALU.mult).then_inc(sem("d_kfree"), 1)
                if j >= 1:
                    dve.wait_ge(sem("d_kfree"), j)
                    recur(j - 1)
            dve.wait_ge(sem("d_kfree"), 8)
            recur(7)
            dve.wait_ge(sem("d_o_ready"), 1)
            variance(lambda t: WORK[:, 1, t * P:(t + 1) * P], None, "d_var")
            dve.wait_ge(sem("d_rstd"), 1)
            refine()
            y = room(1)
            y3 = y.rearrange("p (t d) -> p t d", t=NT)
            for t in range(NT):
                last = v.tensor_scalar(y[:, t * P:(t + 1) * P], WORK[:, 1, t * P:(t + 1) * P], mv[:, t, 0:1],
                                       rstd[:, t:t + 1], ALU.subtract, ALU.mult)
            then(last)
            dve.wait_ge(sem("gates_set"), 2)
            then(v.tensor_tensor(y, y, room(4), ALU.mult))
            v.tensor_tensor(y, y, room(5), ALU.add).then_inc(sem("d_y"), 1)
            residual(3)

            layer_norm(4)
            run_units(Y1)
            dve.wait_ge(sem("cross1_w_in"), 16 * 5)
            residual(4, bias=bias_out["cross1"], negative=True)

            dve.wait_ge(sem("wf_in"), 64)
            wfc2 = wfc[:].rearrange("p a b -> p (a b)")
            for i, w in enumerate((wfc2, wpj[:])):
                last = v.tensor_reduce(gam[:, i:i + 1], w, AX, ALU.add, apply_absolute_value=True)
                if i == 0:
                    then(last)
            last.then_inc(sem("abs_sums"), 1)
            dve.wait_ge(sem("gamma_ready"), 1)
            then(v.tensor_scalar(gam[:, 2:4], ACC[:, 0, 0:2], 0.5 / (D * 512), 0.5e-6, ALU.mult, ALU.add))
            then(v.tensor_scalar(gam[:, 4:6], gam[:, 2:4], -1.0, None, ALU.mult))
            for i, w in enumerate((wfc2, wpj[:])):
                then(v.tensor_scalar(room(14), w, gam[:, 4 + i:5 + i], None, ALU.is_lt))
                last = v.scalar_tensor_tensor(w, w, gam[:, 2 + i:3 + i], room(14), ALU.is_gt, ALU.subtract)
                if i == 0:
                    then(last)
            last.then_inc(sem("ternary"), 1)
            layer_norm(5)
            dve.wait_ge(sem("x_high"), 1)
            v.tensor_tensor(hi[:, 1, :], xnT[:], hi[:, 0, :], ALU.subtract).then_inc(sem("x_split"), 1)
            variance(lambda t: room(2 * t), "gelu_done", "h_var")
            dve.wait_ge(sem("h_rstd"), 1)
            refine()
            for t in range(NT):
                h = room(2 * t + 1)
                then(v.tensor_scalar(h, room(2 * t), mv[:, t, 0:1], rstd[:, t:t + 1], ALU.subtract, ALU.mult))
                then(v.tensor_tensor(h, h, lnw1[:], ALU.mult))
                v.tensor_tensor(h, h, lnb1[:], ALU.add).then_inc(sem("h_norm"), 1)
                if t >= 1:
                    split_h(dve, v, t - 1)
            split_h(dve, v, NT - 1)
            residual(5)


NAMES = {
    "x": "x", "ctx": "ctx_768",
    "a_Wq": "L0_attn_Wq", "a_Wk": "L0_attn_Wk", "a_Wv": "L0_attn_Wv", "a_Wo": "L0_attn_Wout",
    "c0_Wq": "L0_xattn_Wq", "c0_Wk": "L0_xattn_Wk", "c0_Wv": "L0_xattn_Wv", "c0_Wo": "L0_xattn_Wout",
    "c0_bo": "L0_xattn_bout",
    "m_g": "L0_ffn_g_info", "m_Wqkv": "L0_ffn_W_qkv", "m_Wo": "L0_ffn_W_proj", "m_bo": "L0_ffn_b_proj",
    "d_Wq": "L1_attn_Wq", "d_Wk": "L1_attn_Wk", "d_Wv": "L1_attn_Wv", "d_Wbeta": "L1_attn_Wbeta",
    "d_Wg": "L1_attn_Wg", "d_Wo": "L1_attn_Wout", "d_lng": "L1_attn_ln_g", "d_lnb": "L1_attn_ln_b",
    "c1_Wq": "L1_xattn_Wq", "c1_Wk": "L1_xattn_Wk", "c1_Wv": "L1_xattn_Wv", "c1_Wo": "L1_xattn_Wo",
    "c1_bo": "L1_xattn_bo",
    "f_Wfc": "L1_ffn_W_fc", "f_lnw": "L1_ffn_ln_w", "f_lnb": "L1_ffn_ln_b", "f_Wpj": "L1_ffn_W_proj",
}


def kernel(**inputs):
    import numpy as _np
    import concourse.bacc as _bacc
    from concourse import mybir as _mybir
    from concourse.bass_utils import run_bass_kernel_spmd as _run

    nc = _bacc.Bacc("TRN2", target_bir_lowering=False, num_devices=1)
    arrays, aps = {}, {}
    for name in INPUTS:
        a = _np.ascontiguousarray(inputs[NAMES[name]])
        arrays[f"in_{name}_dram"] = a
        aps[name] = nc.dram_tensor(f"in_{name}_dram", a.shape, _mybir.dt.from_np(a.dtype), kind="ExternalInput").ap()
    consts = []
    for name, a in zip(("const32", "const16"), constants()):
        arrays[f"in_{name}_dram"] = a
        consts.append(nc.dram_tensor(f"in_{name}_dram", a.shape, _mybir.dt.from_np(a.dtype), kind="ExternalInput").ap())
    out = nc.dram_tensor("out_0_dram", (B, S, D), _mybir.dt.float32, kind="ExternalOutput").ap()
    decoder(nc, aps, *consts, out)
    r = _run(nc, [arrays], core_ids=[0])
    return r.results[0]["out_0_dram"]
```

```python
from contextlib import ExitStack

import numpy as np

import concourse.bass as bass
from concourse import mybir

ALU = mybir.AluOpType
ACT = mybir.ActivationFunctionType
AX = mybir.AxisListType.X
F32 = mybir.dt.float32
F16 = mybir.dt.float16

P = 128
B = 2
S = 256
T = B * S
NT = T // P
D = 128
SC = 512
DC = 96
NC_T = B * SC // P
REG = 5
H16 = 16
LN_EPS = 1e-5
LN_EXP = "natural_log_exp_and_others"
BIG = 32768.0

C_ID, C_MASK = 0, 128
M_NQ, M_NK, M_BIASK, M_BLK = 0, 1, 2, 3
NCF = C_MASK + 8
R_SEL, R_POS, R_NEG = 0, 8 * 128, 9 * 128
NCH = 10 * 128


def constants():
    c = np.zeros((P, NCF), np.float32)
    p = np.arange(P)
    c[:, C_ID:C_ID + P] = np.eye(P)
    r, row = (p % 32) // 8, p % 32
    m = c[:, C_MASK:]
    m[:, M_NQ] = -1.0 * (r == 1)
    m[:, M_NK] = -1.0 * (r == 2) + 1.0 * (row == 24)
    m[:, M_BIASK] = row == 24
    for j in range(4):
        m[:, M_BLK + j] = p // 32 == j
    half = np.zeros((P, NCH), np.float16)
    for j in range(8):
        half[:, R_SEL + j * P:R_SEL + (j + 1) * P] = p[:, None] == (p[None, :] // 8) * 8 + j
    half[0, R_POS:R_POS + P] = row == 25
    half[0, R_NEG:R_NEG + P] = row == 26
    return c, half


class Phase:

    def __init__(self, name, heads, dh, first_unit, first_slot, wide):
        self.name, self.heads, self.dh = name, heads, dh
        self.small = dh == 8
        self.hu = 4 if self.small else 2
        self.U = heads // self.hu
        self.scale = dh ** -0.5
        self.unit0, self.chunk0 = first_unit, first_slot
        self.ahead = [(wide.name, "k", u, i) for u in range(3) for i in range(2)] if wide else []
        self.before, self.after = [], []
        self.order = []
        self.slots = []
        self.plan(wide)

    def values(self, a, b):
        return [(self.name, "v", 0, i) for i in range(a, b)]

    def plan(self, wide):
        U = self.U
        one = lambda kind, u, i=0: [(self.name, kind, u, i)] if u < U else []
        mx = lambda u, a, b: [(self.name, "max", u, i) for i in range(a, b)] if u < U else []
        ahead = list(self.ahead)
        first = mx(0, 0, 6) + one("turn", 0, 0) + mx(0, 6, 8)
        if self.small:
            self.head = one("k", 0) + one("q", 0) + first + one("k", 1) + one("turn", 0, 1) + one("q", 1) + ahead[:4]
            ahead = ahead[4:]
            if self.name == "mixer":
                self.head = wide.values(0, 3) + self.head
        else:
            n = NC_T * self.heads // 8
            self.head = one("q", 0) + one("q", 1) + self.values(n - 3, n - 1) + first + \
                self.values(n - 1, n) + one("turn", 0, 1)
        self.order += self.head
        for s in range(4 * U + 4):
            u, c = divmod(s, 4)
            jobs = []
            if u < U and self.small:
                jobs = [mx(u + 1, 0, 4), mx(u + 1, 4, 8),
                        one("turn", u + 1, 2) + one("q", u + 2) + one("k", u + 2), []][c]
                if c == 3:
                    jobs += ahead[:1]
                    ahead = ahead[1:]
                if self.name == "mixer":
                    jobs += [(self.name, *job) for job in {
                        3: [("rs", 0, 0)], 6: [("rs", 1, 0)], 7: [("rs", 2, 0), ("rs", 3, 0)],
                        8: [("rt", 0, 0)], 10: [("rv", 0, 0), ("rv", 1, 0)],
                        11: [("rv", 2, 0), ("rv", 3, 0), ("rz", 0, 0), ("rz", 0, 1)]}.get(s, [])]
            elif u < U:
                jobs = [mx(u + 1, 0, 1) + (one("k", u + 2, 1) if u >= 1 else []) + mx(u + 1, 1, 4),
                        mx(u + 1, 4, 8), one("turn", u + 1, 2) + one("q", u + 2), one("k", u + 3)][c]
                if self.name == "cross1":
                    jobs += [(self.name, *job) for job in {
                        3: [("tg", 0, 0)], 15: [("tt", 0, 0)], 19: [("tt", 0, 1)]}.get(s, [])]
            self.order += jobs
            ended = lambda k: (s - k) // 2 - 1 if s >= 2 + k and (s - k) % 2 == 0 and (s - k) // 2 - 1 < 2 * U else None
            self.slots.append(dict(
                main=s if s < 4 * U else None,
                pv=s - 1 if 1 <= s <= 4 * U else None,
                aux=jobs,
                copy=ended(0) if self.small else None, norm=ended(1)))


INPUTS = {
    "x": (B, S, D), "ctx": (B, SC, DC),
    "a_Wq": (D, D), "a_Wk": (D, D), "a_Wv": (D, D), "a_Wo": (D, D),
    "c0_Wq": (D, 512), "c0_Wk": (DC, 512), "c0_Wv": (DC, 512), "c0_Wo": (512, D), "c0_bo": (D,),
    "m_g": (12, 2, D), "m_Wqkv": (D, 3 * D), "m_Wo": (D, D), "m_bo": (D,),
    "d_Wq": (D, D), "d_Wk": (D, D), "d_Wv": (D, D), "d_Wbeta": (D, H16), "d_Wg": (D, D), "d_Wo": (D, D),
    "d_lng": (D,), "d_lnb": (D,),
    "c1_Wq": (D, 1024), "c1_Wk": (DC, 1024), "c1_Wv": (DC, 1024), "c1_Wo": (1024, D), "c1_bo": (D,),
    "f_Wfc": (512, D), "f_lnw": (512,), "f_lnb": (512,), "f_Wpj": (D, 512),
}


def decoder(nc, g, cf, ch, out):
    Y1 = Phase("cross1", 16, 64, 12, 48, None)
    F0 = Phase("mixer", 16, 8, 8, 32, Y1)
    X0 = Phase("cross0", 8, 64, 4, 16, None)
    A0 = Phase("attn0", 16, 8, 0, 0, X0)
    phases = [A0, X0, F0, Y1]
    by_name = {ph.name: ph for ph in phases}
    X0.before = X0.values(0, 5)
    F0.before, F0.after, Y1.before = Y1.values(3, 7), Y1.values(7, 11), Y1.values(11, 13)
    aux_index = {job: i for i, job in enumerate(
        job for ph in phases for job in ph.before + ph.order + ph.after)}

    def freed(*job):
        return f"aux_free{aux_index[job] % 3}", aux_index[job] // 3 + 1

    with ExitStack() as ctx:
        def sb(name, shape, dt=F32):
            return ctx.enter_context(nc.sbuf_tensor(name, shape, dt))

        sems = {}

        def sem(name):
            if name not in sems:
                sems[name] = ctx.enter_context(nc.semaphore(name))
            return sems[name]

        cst = sb("cst", [P, NCF])
        csth = sb("csth", [P, NCH], F16)
        ident = cst[:, C_ID:C_ID + P]

        def col(i):
            return cst[:, C_MASK + i:C_MASK + i + 1]

        ones = sb("ones", [P, P])
        x = sb("x", [P, NT, D])
        xn = sb("xn", [P, NT, D])
        xnT = sb("xnT", [P, T])
        stats = sb("stats", [P, NT, 6])
        mv = sb("mv", [P, NT, 2])
        rstd = sb("rstd", [P, NT])
        rt1 = sb("rt1", [P, NT])
        rt2 = sb("rt2", [P, NT])
        ctxT = sb("ctxT", [DC, NC_T * P])
        wa = {n: sb("wa_" + n, [P, D]) for n in ("q", "k", "v")}
        wqkv = sb("wqkv", [P, 3 * D])
        WR = {(f, n): sb(f"wr_{f}_{n}", [P, 4 * P]) for f in ("attn0", "mixer") for n in "qk"}
        wo8 = {f: sb(f"wo_{f}", [P, D]) for f in ("attn0", "mixer")}
        wk_c0, wv_c0 = sb("wk_c0", [P, 512]), sb("wv_c0", [P, 512])
        wk2 = {"cross0": wk_c0[0:DC, :], "cross1": sb("wk_c1", [DC, 1024])[:, :]}
        wq2 = {"cross0": sb("wq_c0", [P, 512]), "cross1": sb("wq_c1", [P, 1024])}
        wv2 = {"cross0": wv_c0[0:DC, :], "cross1": sb("wv_c1", [DC, 1024])[:, :]}
        wo2 = {"cross0": sb("wo_c0", [P, 4, D]), "cross1": sb("wo_c1", [P, 8, D])}
        bias_out = {n: sb("bias_" + n, [P, D]) for n in ("cross0", "mixer", "cross1")}
        K1 = sb("K1", [P, 3, 2, B * SC], F16)
        K2 = sb("K2", [P, 3, 2, B * SC], F16)
        Q12 = sb("Q12", [P, 3, 4, T], F16)
        Q1, Q2 = Q12[:, :, 0:2, :], Q12[:, :, 2:4, :]
        Kr = sb("Kr", [P, 4, T], F16)
        Qr = Q12
        Kh = sb("Kh", [P, 2, B * SC], F16)
        Kl = sb("Kl", [P, 2, B * SC], F16)
        Qh = sb("Qh", [P, 2, T], F16)
        Ql = sb("Ql", [P, 2, T], F16)
        hi = sb("hi", [P, 2, T], F16)
        qn = sb("qn", [P, T], F16)
        V = sb("V", [P, NC_T, 1024])
        V8 = sb("V8", [P, NT, 16, 32])
        Pr = sb("Pr", [P, 3, 1024])
        Psum = sb("Psum", [P, 2, 512])
        mx = sb("mx", [P, 2, NT, 4])
        mrow = sb("mrow", [4, 2, T], F16)
        Zs = sb("Zs", [P, 2, 2 * S])
        zn = sb("zn", [P, 8, T])
        zt = sb("zt", [P, NT, 16, 8])
        rd8 = sb("rd8", [P, 2, 2, 4])
        qg = sb("qg", [P, D])
        gn = sb("gn", [P, 2, H16])
        n2 = sb("n2", [P, NT * H16])
        dot = sb("dot", [P, NT * H16])
        sim = sb("sim", [P, NT])
        simrow = sb("simrow", [1, B, S])
        ext = sb("ext", [1, 4])
        cls_q = sb("cls_q", [1, 2, B, S], F16)
        cls_k = sb("cls_k", [1, 2, B, S], F16)
        negx = sb("negx", [1, B * REG], F16)
        xreg = sb("xreg", [P, B * REG])
        NR = 4 * B * REG
        Qx = sb("Qx", [P, B, 4, 4, REG], F16)
        qxh = sb("qxh", [P, NR], F16)
        qxn = sb("qxn", [P, NR], F16)
        mreg = sb("mreg", [4 * REG, 8])
        PregT = sb("PregT", [P, 16, 4 * REG])
        Zreg = sb("Zreg", [P, NR])
        rreg = sb("rreg", [REG, 8, 4])
        zreg = sb("zreg", [REG, 32, 8])
        wd = {n: sb("wd_" + n, [P, D]) for n in ("q", "k", "v", "g", "o")}
        wbeta = sb("wbeta", [P, H16])
        kqn = sb("kqn", [P, 2, NT * H16])
        beta = sb("beta", [P, NT * H16])
        lng = sb("lng", [P, D])
        lnb = sb("lnb", [P, D])
        wfc, wpj, lnw1, lnb1 = wo2["cross0"], wq2["cross0"], wk_c0, wv_c0
        gam = sb("gam", [P, 8])
        fcT = sb("fcT", [P, 4, P], F16)
        pjT = sb("pjT", [P, 4, P], F16)

        def room(i):
            if i < 8:
                return zn[:, i, :]
            if i < 12:
                return V8[:, i - 8, :, :].rearrange("p h c -> p (h c)")
            return Pr[:, (i - 12) // 2, (i - 12) % 2 * 512:(i - 12) % 2 * 512 + 512]

        Preg = zn[0:4 * REG, 0:4, :].rearrange("p u (b s) -> p (u b) s", b=B)
        ctx_tok = Pr[:, 0, 0:NC_T * DC].rearrange("p (a c) -> p a c", c=DC)

        PS = ctx.enter_context(nc.psum_tensor("PS", [P, 6, 512], F32))
        SC3 = PS[:, 0:3, :]
        AUX = PS[:, 3:6, :]
        SCR, WORK = PS[:, 0:4, :], PS[:, 4:6, :]
        ACC = ctx.enter_context(nc.psum_tensor("ACC", [P, 2, 512], F32))

        prep_jobs = [job for ph in phases for job in ph.order if job[1] in "kq"]
        hi_count = {job: i + 1 for i, job in enumerate(prep_jobs)}
        place_count, n_placed = {}, {}
        for ph in phases:
            for u in range(0 if ph.small else ph.U):
                for kind in "kq":
                    name = f"placed_{kind}{u % 3}"
                    n_placed[name] = n_placed.get(name, 0) + 16 * (6 if kind == "k" else 2)
                    place_count[ph.name, kind, u] = (name, n_placed[name])
        big_units = [(ph, u) for ph in phases if not ph.small for u in range(ph.U)]
        big_index = {(ph.name, u): i for i, (ph, u) in enumerate(big_units)}
        big_chunks = [ph.chunk0 + s for ph in phases if not ph.small for s in range(4 * ph.U)]
        sum_count = {n: (i // 2) * 3 + (1 if i % 2 == 0 else 3) for i, n in enumerate(big_chunks)}
        row_waits, n_rows = {}, {}
        for ph in phases:
            for u in range(ph.U):
                for part in ((0, 1) if u == 0 else (2,)):
                    name = f"rows_first{part}" if u == 0 else f"rows_set{(ph.unit0 + u) % 2}"
                    n_rows[name] = n_rows.get(name, 0) + 16 * ph.hu
                    row_waits[ph.name, u, part] = (name, n_rows[name])

        def turn_tiles(part):
            return range(NT) if part == 2 else range(2 * part, 2 * part + 2)

        def d_half(i, part):
            return room(10).bitcast(F16)[:, part * T:(part + 1) * T] if i == 0 else hi[:, part, :]

        def h_half(t, part):
            return room(8 + t % 2).bitcast(F16)[:, part * 512:(part + 1) * 512]

        def split_h(dve, v, t):
            dve.wait_ge(sem("hT_high"), t + 1)
            v.tensor_tensor(h_half(t, 1), WORK[:, t % 2, :], h_half(t, 0), ALU.subtract).then_inc(sem("hT_split"), 1)

        den_count = {(ph.name, a): ph.chunk0 // 2 + a + 1 for ph in phases for a in range(2 * ph.U)}
        z_count = {(ph.name, a): k * 8 + a + 1 for k, ph in enumerate((A0, F0)) for a in range(8)}

        def wait_free(engine, *job):
            name, count = freed(*job)
            engine.wait_ge(sem(name), count)

        block = ctx.enter_context(nc.Block())

        @block.sync
        def _(sp):
            def load(dst, src, name, n=1):
                sp.dma_start(dst, src).then_inc(sem(name), 16)

            def bcast(v):
                return v.unsqueeze(0).to_broadcast([P, v.shape[0]])

            load(x[:], g["x"].rearrange("b (t p) d -> p (b t) d", p=P), "x_in")
            load(cst[:], cf, "cst_in")
            for n in "qkv":
                load(wa[n][:], g["a_W" + n], "wa_in")
            load(ctx_tok, g["ctx"].rearrange("b (t p) d -> p (b t) d", p=P), "ctx_in")
            load(csth[:], ch, "csth_in")
            load(wo8["attn0"][:], g["a_Wo"], "wo8_in")
            load(wo8["mixer"][:], g["m_Wo"], "wo8_in")
            for f, c in (("cross0", "c0"), ("cross1", "c1")):
                load(wk2[f], g[c + "_Wk"], f + "_w_in")
                load(wq2[f][:], g[c + "_Wq"], f + "_w_in")
                load(wv2[f], g[c + "_Wv"], f + "_w_in")
                load(wo2[f][:], g[c + "_Wo"].rearrange("(u p) n -> p u n", p=P), f + "_w_in")
                load(bias_out[f][:], bcast(g[c + "_bo"]), f + "_w_in")
            load(wqkv[:], g["m_Wqkv"], "wm_in")
            load(qg[:], bcast(g["m_g"][0, 0, :]), "wm_in")
            load(bias_out["mixer"][:], bcast(g["m_bo"]), "wm_in")
            for n in "qkvgo":
                load(wd[n][:], g["d_W" + n], "wd_in")
            load(wbeta[:], g["d_Wbeta"], "wd_in")
            load(lng[:], bcast(g["d_lng"]), "wd_in")
            load(lnb[:], bcast(g["d_lnb"]), "wd_in")
            def rows(ph, u, part):
                wait_free(sp, ph.name, "turn", u, part)
                name, _ = row_waits[ph.name, u, part]
                cols = slice(turn_tiles(part)[0] * P, (turn_tiles(part)[-1] + 1) * P)
                for j in range(ph.hu):
                    dst = Qr[32 * j + 24:32 * j + 25, u % 3, j, cols] if ph.small else \
                        Q2[64 - 64 * j:65 - 64 * j, u % 3, j, cols]
                    sp.dma_start(dst, mrow[j:j + 1, (ph.unit0 + u) % 2, cols]).then_inc(sem(name), 16)

            def place(ph, kind, u):
                if kind == "q":
                    sp.wait_ge(sem("q_low"), big_index[ph.name, u] + 1)
                for i in range(2 if kind == "k" else 0):
                    wait_free(sp, ph.name, kind, u, i)
                r, e = u % 3, big_index[ph.name, u] % 2
                name, _ = place_count[ph.name, kind, u]
                for h in range(2):
                    own, other = slice(64 * h, 64 * h + 64), slice(64 - 64 * h, P - 64 * h)
                    if kind == "k":
                        pairs = ((K1[own, r, h, :], Kh[own, e, :]), (K1[other, r, h, :], Kh[own, e, :]),
                                 (K2[own, r, h, :], Kl[own, e, :]))
                    else:
                        pairs = ((Q1[other, r, h, :], Ql[own, e, :]),)
                    for dst, src in pairs:
                        sp.dma_start(dst, src).then_inc(sem(name), 16)

            sp.wait_ge(sem("k2_set"), 6)
            for ph in phases:
                if ph is F0:
                    sp.wait_ge(sem("x_done"), 2)
                    load(wfc[:], g["f_Wfc"].rearrange("(a p) d -> p a d", p=P), "wf_in")
                    load(wpj[:], g["f_Wpj"], "wf_in")
                    load(lnw1[:], bcast(g["f_lnw"]), "wf_in")
                    load(lnb1[:], bcast(g["f_lnb"]), "wf_in")
                for name, kind, u, i in ph.order:
                    if kind == "turn":
                        rows(ph, u, i)
                    elif not by_name[name].small and (kind, i) in (("k", 1), ("q", 0)):
                        place(by_name[name], kind, u)
            sp.wait_ge(sem("y_done"), 1)
            sp.dma_start(out.rearrange("b (t p) d -> p (b t) d", p=P), x[:]).then_inc(sem("out_done"), 16)
            sp.wait_ge(sem("out_done"), 16)

        @block.gpsimd
        def _(pool):
            done = {}

            def alone(ins, name):
                done[name] = done.get(name, 0) + 1
                ins.then_inc(sem(name), 1)
                pool.wait_ge(sem(name), done[name])

            alone(nc.gpsimd.memset(V8[:], 0.0), "v8_zero")
            alone(nc.gpsimd.memset(V8[:].rearrange("p t h c -> p (t h) c")[:, :, 8:9], 1.0), "v8_set")
            alone(nc.gpsimd.memset(ones[:], 1.0), "ones_set")
            alone(nc.gpsimd.memset(negx[:], 1.0), "ones_set")
            for h in range(2):
                for r in range(3):
                    alone(nc.gpsimd.memset(K2[64 - 64 * h:P - 64 * h, r, h, :].bitcast(F32), 0.0), "k2_zero")
                for r in range(3):
                    alone(nc.gpsimd.memset(K2[64 - 64 * h:65 - 64 * h, r, h, :], 1.0), "k2_set")
            def delta_sums():
                by_tok = lambda r: r.rearrange("p (t d) -> p t d", t=NT)
                pool.wait_ge(sem("wd_in"), 16 * 8)
                pool.wait_ge(sem("d_gate"), 1)
                pool.wait_ge(sem("d_turned"), 4)
                for i, w in enumerate((lng, lnb)):
                    nc.gpsimd.tensor_tensor(by_tok(room(4 + i)), by_tok(room(3)), w[:].unsqueeze(1).to_broadcast([P, NT, D]),
                                            ALU.mult).then_inc(sem("gates_set"), 1)
                for j in range(1, 8):
                    pool.wait_ge(sem("d_prod"), j + 1)
                    before = room(12) if j == 1 else room(0)
                    alone(nc.gpsimd.tensor_tensor(room(0), before, room(12 + j % 2), ALU.add), "d_sum")

            for ph in phases:
                if ph is Y1:
                    delta_sums()
                for c in range(0 if ph.small else 4 * ph.U):
                    n = ph.chunk0 + c
                    a = n // 2
                    if a >= 2 and n % 2 == 0:
                        pool.wait_ge(sem("den_ready"), a - 1)
                    pool.wait_ge(sem("exp_done"), 2 * n + 2)
                    p = Pr[:, n % 3, :].rearrange("p (k hq) -> p k hq", k=2)
                    t = Psum[:, a % 2, :]
                    if n % 2 == 0:
                        alone(nc.gpsimd.tensor_tensor(t, p[:, 0, :], p[:, 1, :], ALU.add), "sums_done")
                    else:
                        alone(nc.gpsimd.tensor_tensor(t, t, p[:, 0, :], ALU.add), "sums_done")
                        alone(nc.gpsimd.tensor_tensor(t, t, p[:, 1, :], ALU.add), "sums_done")

            for t in range(NT):
                pool.wait_ge(sem("h_scaled"), t + 1)
                h = room(2 * t + 1)
                nc.gpsimd.tensor_tensor(h, h, lnb1[:], ALU.add).then_inc(sem("h_norm"), 1)

        @block.tensor
        def _(pe):
            mm = nc.tensor.matmul

            def norm_transpose(n, jobs=()):
                for job in jobs:
                    aux(job)
                for t in range(NT):
                    pe.wait_ge(sem("xn_done"), NT * n + t + 1)
                    last = nc.tensor.transpose(SCR[:, 1, t * P:(t + 1) * P], xn[:, t, :], ident)
                last.then_inc(sem("xnT_ready"), 1)
                pe.wait_ge(sem("xnT_done"), n + 1)
                for job in jobs[-3:]:
                    wait_free(pe, *job)

            def aux(job):
                name, kind, u, i = job
                ph = by_name[name]
                n = aux_index[job]
                dst = AUX[:, n % 3, :]
                if n >= 3:
                    pe.wait_ge(sem(f"aux_free{n % 3}"), n // 3)
                if kind in "kq" and ph.small:
                    classes = ph.name == "mixer"
                    last = mm(dst, WR[ph.name, kind][:, u * P:(u + 1) * P], xnT[:], start=True, stop=not classes)
                    if classes:
                        if u == 0 and kind == "k":
                            pe.wait_ge(sem("cls_done"), 1)
                        rows = cls_k if kind == "k" else cls_q
                        for c, r in enumerate((R_POS, R_NEG)):
                            last = mm(dst, csth[0:1, r:r + P], rows[0:1, c, :, :].rearrange("p b s -> p (b s)"),
                                      start=False, stop=(c == 1))
                elif kind == "k":
                    pe.wait_ge(sem("ctxT_done"), 1)
                    last = mm(dst, wk2[ph.name][:, u * P:(u + 1) * P], ctxT[:, i * SC:(i + 1) * SC], start=True, stop=True)
                elif kind == "q":
                    last = mm(dst, wq2[ph.name][:, u * P:(u + 1) * P], xnT[:], start=True, stop=True)
                elif kind == "v":
                    t, half = divmod(i, ph.heads // 8)
                    last = mm(dst, ctxT[:, t * P:(t + 1) * P], wv2[ph.name][:, half * 512:(half + 1) * 512],
                              start=True, stop=True)
                elif kind == "max":
                    if i == 0:
                        prepared(ph, u)
                    t, b = i // 2, i // 4
                    if ph.small:
                        for e in range(2):
                            j = 2 * (i % 2) + e
                            last = mm(dst[:, e * S:(e + 1) * S], Qr[:, u % 3, j, t * P:(t + 1) * P],
                                      Kr[:, u, b * S:(b + 1) * S], start=True, stop=True)
                    else:
                        last = mm(dst, Q1[:, u % 3, i % 2, t * P:(t + 1) * P],
                                  K1[:, u % 3, i % 2, b * SC:(b + 1) * SC], start=True, stop=True)
                elif kind == "tg":
                    pe.wait_ge(sem("abs_sums"), 2)
                    last = mm(dst[:, 0:2], ones[:], gam[:, 0:2], start=True, stop=True)
                elif kind == "tt":
                    pe.wait_ge(sem("ternary"), i + 1)
                    w = wpj[:] if i else wfc[:].rearrange("p a b -> p (a b)")
                    for a in range(4):
                        last = nc.tensor.transpose(dst[:, a * P:(a + 1) * P], w[:, a * P:(a + 1) * P], ident)
                elif kind == "rs":
                    wait_free(pe, name, "k", u, 0)
                    pe.wait_ge(sem("qx_done"), 1)
                    for b in range(B):
                        last = mm(dst[0:4 * REG, b * S:(b + 1) * S], Qx[:, b, u, :, :].rearrange("p j r -> p (j r)"),
                                  Kr[:, u, b * S:(b + 1) * S], start=True, stop=True)
                elif kind == "rt":
                    pe.wait_ge(sem("reg_exp"), 4)
                    for ub in range(8):
                        for k in range(2):
                            c = (ub * 2 + k) * 4 * REG
                            last = nc.tensor.transpose(dst[:, c:c + 4 * REG], Preg[:, ub, k * P:(k + 1) * P],
                                                       ident[0:4 * REG, 0:4 * REG])
                elif kind == "rv":
                    wait_free(pe, name, "rt", 0, 0)
                    for b in range(B):
                        for k in range(2):
                            for j in range(4):
                                last = mm(dst[32 * j:32 * j + 32, b * REG:(b + 1) * REG], V8[:, 2 * b + k, 4 * u + j, :],
                                          PregT[:, (u * B + b) * 2 + k, j * REG:(j + 1) * REG],
                                          start=(k == 0), stop=(k == 1), tile_position=(0, 32 * j))
                elif kind == "rz":
                    for w in (2 * i, 2 * i + 1):
                        wait_free(pe, name, "rv", w, 0)
                    for ub in range(4 * i, 4 * i + 4):
                        last = nc.tensor.transpose(dst[0:REG, (ub % 4) * P:(ub % 4 + 1) * P],
                                                   Zreg[:, ub * REG:(ub + 1) * REG], ident)
                else:
                    end = 8 if i == 2 else 4 * i + 4
                    for last_max in range(end - 3, end):
                        wait_free(pe, name, "max", u, last_max)
                    for t in turn_tiles(i):
                        last = nc.tensor.transpose(dst[0:ph.hu, t * P:(t + 1) * P],
                                                   mx[:, u % 2, t, 0:ph.hu], ident)
                last.then_inc(sem("aux_ready"), 1)

            def prepared(ph, u):
                if ph.small:
                    wait_free(pe, ph.name, "k", u, 0)
                    wait_free(pe, ph.name, "q", u, 0)
                else:
                    for kind in "kq":
                        name, count = place_count[ph.name, kind, u]
                        pe.wait_ge(sem(name), count)
                    wait_free(pe, ph.name, "q", u, 0)

            def scores(ph, s, half):
                u, c = divmod(s, 4)
                b, k = c // 2, c % 2
                n = ph.chunk0 + s
                m = 2 * n + half
                if m >= 3:
                    pe.wait_ge(sem("exp_done"), m - 2)
                if half == 0 and (c == 0 or (c == 2 and u == 0)):
                    name, count = row_waits[ph.name, u, 2 if u else b]
                    pe.wait_ge(sem(name), count)
                if half == 0 and c == 0:
                    prepared(ph, u)
                dst = SC3[:, m % 3, :]
                if ph.small:
                    last = mm(dst, Kr[:, u, b * S + k * P:b * S + (k + 1) * P],
                              Qr[:, u % 3, 2 * half:2 * half + 2, b * S:(b + 1) * S], start=True, stop=True)
                else:
                    keys = slice(b * SC + (2 * k + half) * P, b * SC + (2 * k + half + 1) * P)
                    for h in range(2):
                        for first, (K_, Q_) in enumerate(((K1, Q1), (K2, Q2))):
                            last = mm(dst[:, h * S:(h + 1) * S], K_[:, u % 3, h, keys],
                                      Q_[:, u % 3, h, b * S:(b + 1) * S], start=(first == 0), stop=(first == 1))
                last.then_inc(sem("scores_ready"), 1)

            def values(ph, s, half):
                u, c = divmod(s, 4)
                b, k = c // 2, c % 2
                n = ph.chunk0 + s
                a = n // 2
                pe.wait_ge(sem("exp_done"), 2 * n + 1 + half)
                if half == 0:
                    if k == 0 and a >= 2:
                        pe.wait_ge(sem("norm_done"), a - 1)
                    if s == 0 and not ph.small:
                        for i in range(3):
                            wait_free(pe, ph.name, "v", 0, NC_T * ph.heads // 8 - 3 + i)
                if ph.small:
                    if half == 0:
                        return
                    if s == 0:
                        pe.wait_ge(sem("v8_done"), 1 if ph is A0 else 2)
                    for j in range(4):
                        last = mm(ACC[32 * j:32 * j + 32, a % 2, 0:S], V8[:, 2 * b + k, 4 * u + j, :],
                                  Pr[:, n % 3, j * S:(j + 1) * S], start=(k == 0), stop=(k == 1),
                                  tile_position=(0, 32 * j))
                else:
                    kk = half
                    kt = 2 * k + kk
                    for h in range(2):
                        last = mm(ACC[64 * h:64 * h + 64, a % 2, 0:S],
                                  V[:, b * 4 + kt, (2 * u + h) * 64:(2 * u + h + 1) * 64],
                                  Pr[:, n % 3, (2 * kk + h) * S:(2 * kk + h + 1) * S],
                                  start=(kt == 0), stop=(kt == 3), tile_position=(0, 64 * h))
                if half == 1:
                    last.then_inc(sem("values_done"), 1)

            def select(ph, a):
                n = ph.chunk0 // 2 + a
                if ph.small:
                    pe.wait_ge(sem("z_copied"), z_count[ph.name, a])
                    for t in range(2):
                        last = nc.tensor.transpose(ACC[:, n % 2, S + t * P:S + (t + 1) * P],
                                                   Zs[:, n % 2, t * P:(t + 1) * P], ident)
                else:
                    pe.wait_ge(sem("sums_done"), sum_count[2 * n + 1])
                    for h in range(2):
                        last = mm(ACC[64 * h:64 * h + 64, n % 2, S:2 * S], ones[:, 0:64],
                                  Psum[:, n % 2, h * S:(h + 1) * S], start=True, stop=True,
                                  tile_position=(0, 64 * h))
                last.then_inc(sem("den_ready"), 1)

            def turn_context():
                pe.wait_ge(sem("ctx_in"), 16)
                for t in range(NC_T):
                    last = nc.tensor.transpose(ACC[0:DC, t // 4, (t % 4) * P:(t % 4 + 1) * P], ctx_tok[:, t, :], ident)
                last.then_inc(sem("ctxT_ready"), 1)

            def run_units(ph):
                for job in ph.head:
                    if ph is A0 and job == ph.head[2]:
                        turn_context()
                    aux(job)
                for slot in ph.slots:
                    jobs = list(slot["aux"])
                    parts = []
                    if slot["main"] is not None:
                        parts += [(scores, slot["main"], 0), (scores, slot["main"], 1)]
                    if slot["pv"] is not None:
                        parts += [(values, slot["pv"], 0), (values, slot["pv"], 1)]
                    while parts or jobs:
                        if parts:
                            f, s, half = parts.pop(0)
                            f(ph, s, half)
                        if jobs:
                            aux(jobs.pop(0))
                    tail = ph.slots.index(slot) - 4 * ph.U if not ph.small else None
                    if tail == 0:
                        for job in ph.order[-3:]:
                            wait_free(pe, *job)
                        pe.wait_ge(sem("exp_done"), 2 * (ph.chunk0 + 4 * ph.U))
                        project_units(ph, range(ph.U // 2))
                    if slot["norm"] is not None:
                        select(ph, slot["norm"])
                    if tail == 1:
                        project_units(ph, range(ph.U // 2, ph.U - 1))
                for job in ph.order[-3:]:
                    wait_free(pe, *job)

            def project_out(ph, w):
                a = (ph.chunk0 + 4 * ph.U) // 2
                pe.wait_ge(sem("norm_done"), a)
                if ph.name == "mixer":
                    pe.wait_ge(sem("regs_merged"), 1)
                if ph.small:
                    for t in range(NT):
                        last = nc.tensor.transpose(SCR[:, 1, t * P:(t + 1) * P],
                                                   zt[:, t, :, :].rearrange("p h d -> p (h d)"), ident)
                    last.then_inc(sem("zT_ready"), 1)
                    pe.wait_ge(sem("zT_done"), 1 if ph.name == "attn0" else 2)
                    for t in range(NT):
                        last = mm(SCR[:, 0, t * P:(t + 1) * P], xnT[:, t * P:(t + 1) * P], w, start=True, stop=True)
                    last.then_inc(sem("out_ready"), 1)
                    return
                project_units(ph, range(ph.U - 1, ph.U)).then_inc(sem("out_ready"), 1)

            def project_units(ph, units):
                pe.wait_ge(sem("norm_done"), ph.chunk0 // 2 + 2 * units[-1] + 2)
                for u in units:
                    for t in range(NT):
                        last = mm(SCR[:, t, 0:P], zn[:, u, t * P:(t + 1) * P], wo2[ph.name][:, u, :],
                                  start=(u == 0), stop=(u == ph.U - 1))
                return last

            def values_small(w):
                for t in range(NT):
                    last = mm(SCR[:, 2, t * P:(t + 1) * P], xnT[:, t * P:(t + 1) * P], w, start=True, stop=True)
                last.then_inc(sem("v8_ready"), 1)

            pe.wait_ge(sem("cst_in"), 16)
            norm_transpose(0)
            pe.wait_ge(sem("wa_in"), 48)
            values_small(wa["v"][:])
            pe.wait_ge(sem("wr_done"), 1)
            pe.wait_ge(sem("cross0_w_in"), 16 * 5)
            run_units(A0)
            pe.wait_ge(sem("wo8_in"), 32)
            project_out(A0, wo8["attn0"][:])

            norm_transpose(1, X0.before)
            pe.wait_ge(sem("ones_set"), 2)
            pe.wait_ge(sem("x_done"), 1)
            run_units(X0)
            project_out(X0, wo2["cross0"])

            pe.wait_ge(sem("cross1_w_in"), 16 * 5)
            pe.wait_ge(sem("x_done"), 2)
            norm_transpose(2, F0.before)
            pe.wait_ge(sem("wm_in"), 48)
            pe.wait_ge(sem("x_done"), 2)
            for t in range(NT):
                last = mm(SCR[:, 0, t * P:(t + 1) * P], xnT[:, t * P:(t + 1) * P], wqkv[:, 0:D], start=True, stop=True)
            last.then_inc(sem("qtok_ready"), 1)
            values_small(wqkv[:, 2 * D:3 * D])
            pe.wait_ge(sem("sim_done"), 1)
            for t in range(NT):
                last = nc.tensor.transpose(ACC[0:1, 0, t * P:(t + 1) * P], sim[:, t:t + 1], ident)
            last.then_inc(sem("simrow_ready"), 1)
            pe.wait_ge(sem("wr_done"), 2)
            pe.wait_ge(sem("xreg_done"), 1)
            pe.wait_ge(sem("csth_in"), 16)
            qx_out = SCR[:, 1, 0:NR].rearrange("p (b u r) -> p b u r", b=B, u=4)
            for u in range(4):
                mm(qx_out[:, :, u, :], WR["mixer", "q"][:, u * P:(u + 1) * P], xreg[:], start=True, stop=False)
                last = mm(qx_out[:, :, u, :], csth[0:1, R_NEG:R_NEG + P], negx[:], start=False, stop=True)
            last.then_inc(sem("qx_ready"), 1)
            run_units(F0)
            project_out(F0, wo8["mixer"][:])

            norm_transpose(3, F0.after)
            pe.wait_ge(sem("wd_in"), 16 * 8)
            pe.wait_ge(sem("x_done"), 3)

            def by_token(dst, w, width):
                for t in range(NT):
                    last = mm(dst[:, t * width:(t + 1) * width], xnT[:, t * P:(t + 1) * P], w, start=True, stop=True)
                last.then_inc(sem("d_proj"), 1)

            by_token(SCR[:, 0, :], wd["k"][:], P)
            by_token(SCR[:, 1, :], wd["q"][:], P)
            by_token(SCR[:, 3, :], wbeta[:], H16)
            by_token(SCR[:, 2, :], wd["v"][:], P)
            by_token(ACC[:, 0, :], wd["g"][:], P)
            for i, (src, dst) in enumerate(((4, WORK[:, 0, :]), (5, WORK[:, 1, :]), (14, ACC[:, 1, :]), (15, SCR[:, 3, :]))):
                pe.wait_ge(sem("d_token"), i + 1)
                for t in range(NT):
                    last = nc.tensor.transpose(dst[:, t * P:(t + 1) * P], room(src)[:, t * P:(t + 1) * P], ident)
                last.then_inc(sem("d_turned"), 1)
            pe.wait_ge(sem("d_split"), 2)
            pe.wait_ge(sem("csth_in"), 16)

            def spread(i, j):
                if j >= 2:
                    pe.wait_ge(sem("d_kfree" if i == 0 else "d_prod"), j - 1)
                if i == 1 and j == 1:
                    pe.wait_ge(sem("d_terms"), 2)
                for part in range(2):
                    last = mm(SCR[:, 2 * i + j % 2, :], csth[:, R_SEL + j * P:R_SEL + (j + 1) * P],
                              d_half(i, part), start=(part == 0), stop=(part == 1))
                last.then_inc(sem("d_spread_k" if i == 0 else "d_spread_q"), 1)

            for j in range(8):
                spread(0, j)
                spread(1, j)
            pe.wait_ge(sem("d_sum"), 7)
            for t in range(NT):
                last = nc.tensor.transpose(WORK[:, 1, t * P:(t + 1) * P], room(0)[:, t * P:(t + 1) * P], ident)
            last.then_inc(sem("d_o_ready"), 1)
            pe.wait_ge(sem("d_y"), 1)
            for t in range(NT):
                last = nc.tensor.transpose(ACC[:, 1, t * P:(t + 1) * P], room(1)[:, t * P:(t + 1) * P], ident)
            last.then_inc(sem("d_yT_ready"), 1)
            pe.wait_ge(sem("d_yT"), 1)
            for t in range(NT):
                last = mm(SCR[:, 0, t * P:(t + 1) * P], room(2)[:, t * P:(t + 1) * P], wd["o"][:], start=True, stop=True)
            last.then_inc(sem("out_ready"), 1)

            norm_transpose(4, Y1.before)
            pe.wait_ge(sem("x_done"), 4)
            run_units(Y1)
            project_out(Y1, wo2["cross1"])

            norm_transpose(5)
            pe.wait_ge(sem("x_split"), 1)
            for i in range(2):
                wait_free(pe, "cross1", "tt", 0, i)
            for t in range(NT):
                for part in range(2):
                    last = mm(SCR[:, t, :], hi[:, part, t * P:(t + 1) * P],
                              fcT[:].rearrange("p a b -> p (a b)"), start=(part == 0), stop=(part == 1))
                last.then_inc(sem("h_ready"), 1)
            def turn_hidden(t):
                pe.wait_ge(sem("h_norm"), t + 1)
                if t >= 2:
                    pe.wait_ge(sem("hT_split"), t - 1)
                for a in range(4):
                    last = nc.tensor.transpose(WORK[:, t % 2, a * P:(a + 1) * P],
                                               room(2 * t + 1)[:, a * P:(a + 1) * P], ident)
                last.then_inc(sem("hT_ready"), 1)

            turn_hidden(0)
            for t in range(NT):
                if t + 1 < NT:
                    turn_hidden(t + 1)
                pe.wait_ge(sem("hT_split"), t + 1)
                for a in range(4):
                    for part in range(2):
                        last = mm(ACC[:, 1, t * P:(t + 1) * P], h_half(t, part)[:, a * P:(a + 1) * P],
                                  pjT[:, a, :], start=(a == 0 and part == 0), stop=(a == 3 and part == 1))
                last.then_inc(sem("h_out" if t < NT - 1 else "out_ready"), 1)

        @block.scalar
        def _(act):
            A = nc.scalar.activation
            wide_sums = [0]

            def inv_root(n, jobs=()):
                for job in jobs[:1]:
                    aux(job)
                act.wait_ge(sem("var_done"), n + 1)
                A(rt1[:], rt2[:], ACT.Ln).then_inc(sem("act_ln"), 1)
                act.wait_ge(sem("act_ln"), n + 1)
                A(rstd[:], rt1[:], ACT.Exp, scale=-0.5).then_inc(sem("root_done"), 1)
                for job in jobs[1:]:
                    aux(job)

            def norm_copy(n):
                act.wait_ge(sem("xnT_ready"), n + 1)
                A(xnT[:], SCR[:, 1, :], ACT.Identity).then_inc(sem("xnT_done"), 1)

            def aux(job):
                name, kind, u, i = job
                ph = by_name[name]
                if kind in ("rs", "rt"):
                    if kind == "rt" or u >= 1:
                        w = u - 1 if kind == "rs" else 3
                        wait_free(act, name, "rs", w, 0)
                        p = Preg[:, 2 * w:2 * w + 2, :]
                        A(p, p, ACT.Exp, scale=ph.scale).then_inc(sem("reg_exp"), 1)
                if kind not in ("turn", "k", "q", "v", "tt"):
                    return
                n = aux_index[job]
                src = AUX[:, n % 3, :]
                act.wait_ge(sem("aux_ready"), n + 1)
                if kind == "turn":
                    gu = ph.unit0 + u
                    if gu >= 2:
                        prev = ph if u >= 2 else phases[phases.index(ph) - 1]
                        pu = u - 2 if u >= 2 else prev.U - 2 + u
                        for part in ((0, 1) if pu == 0 else (2,)):
                            sent, count = row_waits[prev.name, pu, part]
                            act.wait_ge(sem(sent), count)
                    cols = slice(turn_tiles(i)[0] * P, (turn_tiles(i)[-1] + 1) * P)
                    A(mrow[0:ph.hu, gu % 2, cols], src[0:ph.hu, cols], ACT.Identity,
                      scale=-1.0).then_inc(sem(f"aux_free{n % 3}"), 1)
                elif kind == "tt":
                    A((pjT if i else fcT)[:].rearrange("p a b -> p (a b)"), src,
                      ACT.Identity).then_inc(sem(f"aux_free{n % 3}"), 1)
                elif kind == "v":
                    t, half = divmod(i, ph.heads // 8)
                    A(V[:, t, half * 512:(half + 1) * 512], src, ACT.Identity).then_inc(sem(f"aux_free{n % 3}"), 1)
                elif ph.small:
                    before = [j for j in prep_jobs[:hi_count[job] - 1] if j[1] == kind and by_name[j[0]].small]
                    if before:
                        wait_free(act, *before[-1])
                    bias = col(M_BIASK) if kind == "k" else 0.0
                    A(hi[:, "kq".index(kind), :], src, ACT.Identity, bias=bias).then_inc(sem("hi_done"), 1)
                else:
                    bi = big_index[name, u]
                    if bi >= 2:
                        pp, pu = big_units[bi - 2]
                        if kind == "k":
                            placed, count = place_count[pp.name, kind, pu]
                            act.wait_ge(sem(placed), count)
                        else:
                            wait_free(act, pp.name, "q", pu, 0)
                    dst = Kh[:, bi % 2, i * SC:(i + 1) * SC] if kind == "k" else Qh[:, bi % 2, :]
                    A(dst, src, ACT.Identity).then_inc(sem("hi_done"), 1)

            def run_units(ph):
                for job in ph.head:
                    if ph is A0 and job == ph.head[2]:
                        act.wait_ge(sem("ctxT_ready"), 1)
                        A(ctxT[:], ACC[0:DC, :, :].rearrange("p a b -> p (a b)"),
                          ACT.Identity).then_inc(sem("ctxT_done"), 1)
                    aux(job)
                for slot in ph.slots:
                    jobs = list(slot["aux"])
                    for half in range(0 if slot["main"] is None else 2):
                        n = ph.chunk0 + slot["main"]
                        m = 2 * n + half
                        act.wait_ge(sem("scores_ready"), m + 1)
                        if n >= 3 and half == 0:
                            act.wait_ge(sem("values_done"), n - 2)
                            if n - 3 in sum_count:
                                act.wait_ge(sem("sums_done"), sum_count[n - 3])
                        A(Pr[:, n % 3, half * 512:(half + 1) * 512], SC3[:, m % 3, :],
                          ACT.Exp, scale=ph.scale).then_inc(sem("exp_done"), 1)
                        for job in jobs[half:half + 1]:
                            aux(job)
                    for job in jobs[2 if slot["main"] is not None else 0:]:
                        aux(job)
                    if slot["norm"] is not None and not ph.small:
                        a = slot["norm"]
                        n = ph.chunk0 // 2 + a
                        act.wait_ge(sem("den_ready"), den_count[ph.name, a])
                        if n >= 2:
                            act.wait_ge(sem("norm_done"), n - 1)
                        A(Zs[:, n % 2, 0:S], ACC[:, n % 2, S:2 * S], ACT.Ln).then_inc(sem("den_ln"), 1)
                        wide_sums[0] += 1
                        act.wait_ge(sem("den_ln"), wide_sums[0])
                        A(Zs[:, n % 2, S:2 * S], Zs[:, n % 2, 0:S], ACT.Exp, scale=-1.0).then_inc(sem("den_inverted"), 1)

            def project_copy(n):
                act.wait_ge(sem("zT_ready"), n)
                A(xnT[:], SCR[:, 1, :], ACT.Identity).then_inc(sem("zT_done"), 1)

            def values_small(n):
                act.wait_ge(sem("v8_ready"), n + 1)
                act.wait_ge(sem("v8_set"), 1)
                A(V8[:].rearrange("p t h c -> p (t h) c")[:, :, 0:8],
                  SCR[:, 2, :].rearrange("p (a d) -> p a d", d=8), ACT.Identity).then_inc(sem("v8_done"), 1)

            nc.scalar.preload_act_table_set(LN_EXP)
            inv_root(0)
            norm_copy(0)
            values_small(0)
            run_units(A0)

            project_copy(1)
            inv_root(1, X0.before)
            norm_copy(1)
            run_units(X0)

            inv_root(2, F0.before)
            norm_copy(2)
            act.wait_ge(sem("qtok_ready"), 1)
            A(room(1), SCR[:, 0, :], ACT.Square).then_inc(sem("qsq_done"), 1)
            act.wait_ge(sem("norms2"), 1)
            A(n2[:], n2[:], ACT.Sqrt).then_inc(sem("norms"), 1)
            A(gn[:, 0, :], gn[:, 0, :], ACT.Sqrt).then_inc(sem("norms"), 1)
            nc.scalar.preload_act_table_set(LN_EXP)
            values_small(1)
            act.wait_ge(sem("xnT_done"), 3)
            A(xreg[:].rearrange("p (b r) -> p b r", b=B), xnT[:].rearrange("p (b s) -> p b s", b=B)[:, :, 0:REG],
              ACT.Identity).then_inc(sem("xreg_done"), 1)
            act.wait_ge(sem("qx_ready"), 1)
            A(qxh[:], SCR[:, 1, 0:NR], ACT.Identity).then_inc(sem("qxh_done"), 1)
            run_units(F0)

            project_copy(2)

            inv_root(3, F0.after)
            norm_copy(3)
            for i in range(2):
                act.wait_ge(sem("d_proj"), i + 1)
                A(room(i), SCR[:, i, :], ACT.Square).then_inc(sem("d_sq"), 1)
            act.wait_ge(sem("d_proj"), 3)
            A(beta[:], SCR[:, 3, 0:NT * H16], ACT.Exp, scale=-1.0).then_inc(sem("d_ebeta"), 1)
            act.wait_ge(sem("d_n2"), 2)
            A(kqn[:], kqn[:], ACT.Sqrt).then_inc(sem("d_root"), 1)
            nc.scalar.preload_act_table_set(LN_EXP)
            act.wait_ge(sem("d_proj"), 5)
            gate = room(3)
            A(gate, ACC[:, 0, :], ACT.Exp, scale=-1.0).then_inc(sem("d_egate"), 1)
            act.wait_ge(sem("d_egate"), 1)
            A(gate, gate, ACT.Ln, bias=1.0).then_inc(sem("d_egate"), 1)
            act.wait_ge(sem("d_egate"), 2)
            A(gate, gate, ACT.Exp, scale=-1.0).then_inc(sem("d_egate"), 1)
            for i in range(2):
                act.wait_ge(sem("d_turned"), i + 1)
                A(d_half(i, 0), WORK[:, i, :], ACT.Identity).then_inc(sem("d_high"), 1)
            for i, (dst, src) in enumerate(((room(2), ACC[:, 1, :]), (room(1), SCR[:, 3, :]))):
                act.wait_ge(sem("d_turned"), i + 3)
                A(dst, src, ACT.Identity).then_inc(sem("d_terms"), 1)
            for j in range(8):
                act.wait_ge(sem("d_kk"), j + 1)
                A(room(8 + j % 2), room(8 + j % 2), ACT.Identity, bias=1.0).then_inc(sem("d_decay"), 1)
            act.wait_ge(sem("d_var"), 1)
            A(rt1[:], rt2[:], ACT.Ln).then_inc(sem("d_ln"), 1)
            act.wait_ge(sem("d_ln"), 1)
            A(rstd[:], rt1[:], ACT.Exp, scale=-0.5).then_inc(sem("d_rstd"), 1)
            act.wait_ge(sem("d_yT_ready"), 1)
            A(room(2), ACC[:, 1, :], ACT.Identity).then_inc(sem("d_yT"), 1)

            inv_root(4, Y1.before)
            norm_copy(4)
            run_units(Y1)

            inv_root(5)
            act.wait_ge(sem("xnT_ready"), 6)
            A(hi[:, 0, :], SCR[:, 1, :], ACT.Identity).then_inc(sem("xnT_done"), 1)
            for t in range(NT):
                act.wait_ge(sem("h_ready"), t + 1)
                A(room(2 * t), SCR[:, t, :], ACT.Gelu).then_inc(sem("gelu_done"), 1)
            nc.scalar.preload_act_table_set(LN_EXP)
            act.wait_ge(sem("h_var"), 1)
            A(rt1[:], rt2[:], ACT.Ln).then_inc(sem("h_ln"), 1)
            act.wait_ge(sem("h_ln"), 1)
            A(rstd[:], rt1[:], ACT.Exp, scale=-0.5).then_inc(sem("h_rstd"), 1)
            for t in range(NT):
                act.wait_ge(sem("hT_ready"), t + 1)
                if t >= 2:
                    act.wait_ge(sem("h_out"), t - 1)
                A(h_half(t, 0), WORK[:, t % 2, :], ACT.Identity).then_inc(sem("hT_high"), 1)

        @block.vector
        def _(dve):
            v = nc.vector
            chain, wide_sums = [0], [0]

            def then(ins):
                chain[0] += 1
                ins.then_inc(sem("dve_step"), 1)
                dve.wait_ge(sem("dve_step"), chain[0])

            def refine():
                then(v.tensor_tensor(rt1[:], rstd[:], rstd[:], ALU.mult))
                then(v.scalar_tensor_tensor(rt1[:], rt1[:], -0.5, rt2[:], ALU.mult, ALU.mult))
                then(v.scalar_tensor_tensor(rstd[:], rt1[:], 1.5, rstd[:], ALU.add, ALU.mult))

            def variance(src, ready, name):
                for t in range(NT):
                    if ready:
                        dve.wait_ge(sem(ready), t + 1)
                    last = v.bn_stats(stats[:, t, :], src(t))
                then(last)
                for t in range(NT):
                    last = v.bn_aggr(mv[:, t, :], stats[:, t, :])
                then(last)
                v.tensor_scalar(rt2[:], mv[:, :, 1], LN_EPS, None, ALU.add).then_inc(sem(name), 1)

            def layer_norm(n):
                variance(lambda t: x[:, t, :], None, "var_done")
                dve.wait_ge(sem("root_done"), n + 1)
                refine()
                for t in range(NT):
                    v.tensor_scalar(xn[:, t, :], x[:, t, :], mv[:, t, 0:1], rstd[:, t:t + 1],
                                    ALU.subtract, ALU.mult).then_inc(sem("xn_done"), 1)

            def aux(job):
                name, kind, u, i = job
                ph = by_name[name]
                n = aux_index[job]
                src = AUX[:, n % 3, :]
                if kind in ("v", "turn", "tt"):
                    return
                if kind[0] in "rt":
                    dve.wait_ge(sem("aux_ready"), n + 1)
                if kind == "max":
                    dve.wait_ge(sem("aux_ready"), n + 1)
                    t = i // 2
                    if ph.small:
                        e = 2 * (i % 2)
                        last = v.tensor_reduce(mx[:, u % 2, t, e:e + 2], src.rearrange("p (a s) -> p a s", a=2), AX, ALU.max)
                    else:
                        last = v.tensor_reduce(mx[:, u % 2, t, i % 2:i % 2 + 1], src, AX, ALU.max)
                elif kind == "tg":
                    last = v.tensor_scalar(gam[:, 2:4], src[:, 0:2], 0.5 / (D * 512), 0.5e-6, ALU.mult, ALU.add)
                    then(last)
                    last = v.tensor_scalar(gam[:, 4:6], gam[:, 2:4], -1.0, None, ALU.mult)
                elif kind == "rs":
                    m, scores = mreg[:, 2 * u:2 * u + 2], src[0:4 * REG, :].rearrange("p (b s) -> p b s", b=B)
                    then(v.tensor_reduce(m, scores, AX, ALU.max))
                    last = v.tensor_tensor(Preg[:, 2 * u:2 * u + 2, :], scores,
                                           m.unsqueeze(2).to_broadcast([4 * REG, B, S]), ALU.subtract)
                elif kind == "rt":
                    last = v.tensor_copy(PregT[:].rearrange("p a b -> p (a b)"), src[:, 0:16 * 4 * REG])
                elif kind == "rv":
                    last = v.tensor_copy(Zreg[:, u * B * REG:(u + 1) * B * REG], src[:, 0:B * REG])
                elif kind == "rz":
                    z = src[0:REG, :].rearrange("p (a j c) -> p a j c", a=4, j=4)
                    r = rreg[:, 4 * i:4 * i + 4, :]
                    then(v.reciprocal(r, z[:, :, :, 8]))
                    then(v.tensor_scalar(r, r, 0.5, None, ALU.mult))
                    last = v.tensor_tensor(zreg[:, 16 * i:16 * i + 16, :].rearrange("p (a j) d -> p a j d", j=4),
                                           z[:, :, :, 0:8], r.unsqueeze(3).to_broadcast([REG, 4, 4, 8]), ALU.mult)
                else:
                    dve.wait_ge(sem("hi_done"), hi_count[job])
                    if ph.small and kind == "k":
                        last = v.scalar_tensor_tensor(Kr[:, u, :], hi[:, 0, :], col(M_NK), src, ALU.mult, ALU.add)
                    elif ph.small:
                        then(v.scalar_tensor_tensor(qn[:], hi[:, 1, :], col(M_NQ), src, ALU.mult, ALU.add))
                        for j in range(4):
                            last = v.tensor_scalar(Qr[:, u % 3, j, :], qn[:], col(M_BLK + j), None, ALU.mult)
                    else:
                        bi = big_index[name, u]
                        e = bi % 2
                        if kind == "q" and bi >= 2:
                            pp, pu = big_units[bi - 2]
                            placed, count = place_count[pp.name, "q", pu]
                            dve.wait_ge(sem(placed), count)
                        keys = slice(i * SC, (i + 1) * SC)
                        high, low = (Kh[:, e, keys], Kl[:, e, keys]) if kind == "k" else (Qh[:, e, :], Ql[:, e, :])
                        last = v.tensor_tensor(low, src, high, ALU.subtract)
                        if kind == "q":
                            last.then_inc(sem("q_low"), 1)
                            for h in range(2):
                                own = slice(64 * h, 64 * h + 64)
                                for Q_ in (Q1, Q2):
                                    last = v.tensor_copy(Q_[own, u % 3, h, :], high[own, :])
                last.then_inc(sem(f"aux_free{n % 3}"), 1)

            def norm(ph, a, part):
                n = ph.chunk0 // 2 + a
                u, b = divmod(a, 2)
                if part == 0:
                    if n >= 2:
                        dve.wait_ge(sem("norm_done"), n - 1)
                    dve.wait_ge(sem("values_done"), ph.chunk0 + 2 * a + 2)
                    v.tensor_copy(Zs[:, n % 2, 0:S], ACC[:, n % 2, 0:S]).then_inc(sem("z_copied"), 1)
                    return
                if not ph.small:
                    dst, t, r = zn[:, u, b * S:(b + 1) * S], Zs[:, n % 2, 0:S], Zs[:, n % 2, S:2 * S]
                    wide_sums[0] += 1
                    dve.wait_ge(sem("den_inverted"), wide_sums[0])
                    then(v.tensor_tensor(t, ACC[:, n % 2, S:2 * S], r, ALU.mult))
                    then(v.tensor_tensor(dst, ACC[:, n % 2, 0:S], r, ALU.mult))
                    v.scalar_tensor_tensor(dst, t, 2.0, dst, ALU.subtract, ALU.mult).then_inc(sem("norm_done"), 1)
                    return
                dve.wait_ge(sem("den_ready"), den_count[ph.name, a])
                z = ACC[:, n % 2, S:2 * S].rearrange("p (t j c) -> p t j c", t=2, j=4)
                r = rd8[:, n % 2, :, :]
                then(v.reciprocal(r, z[:, :, :, 8]))
                last = v.tensor_tensor(zt[:, 2 * b:2 * b + 2, 4 * u:4 * u + 4, :], z[:, :, :, 0:8],
                                       r.unsqueeze(3).to_broadcast([P, 2, 4, 8]), ALU.mult)
                last.then_inc(sem("norm_done"), 1)

            def ternary(s):
                w = {0: wfc[:].rearrange("p a b -> p (a b)"), 1: wpj[:]}
                if s in (1, 2):
                    if s == 1:
                        dve.wait_ge(sem("wf_in"), 64)
                    v.tensor_reduce(gam[:, s - 1:s], w[s - 1], AX, ALU.add,
                                    apply_absolute_value=True).then_inc(sem("abs_sums"), 1)
                elif s in (10, 14):
                    i = (s - 10) // 4
                    if i == 0:
                        wait_free(dve, "cross1", "tg", 0, 0)
                    else:
                        dve.wait_ge(sem("ternary"), 1)
                    then(v.tensor_scalar(room(8), w[i], gam[:, 4 + i:5 + i], None, ALU.is_lt))
                    v.scalar_tensor_tensor(w[i], w[i], gam[:, 2 + i:3 + i], room(8), ALU.is_gt,
                                           ALU.subtract).then_inc(sem("ternary"), 1)

            def run_units(ph):
                for job in ph.head:
                    aux(job)
                for slot in ph.slots:
                    for job in slot["aux"]:
                        aux(job)
                    if ph is Y1:
                        ternary(ph.slots.index(slot))
                    if slot["norm"] is not None:
                        norm(ph, slot["norm"], 1)
                    if slot["copy"] is not None:
                        norm(ph, slot["copy"], 0)

            def residual(n, bias=None, also=None, negative=False):
                if bias is not None:
                    then(v.tensor_tensor(x[:], x[:], bias[:].unsqueeze(1).to_broadcast([P, NT, D]), ALU.add))
                if also is not None:
                    then(v.tensor_tensor(x[:], x[:], also[:], ALU.add))
                dve.wait_ge(sem("out_ready"), n + 1)
                src = SCR[:, :, 0:D] if negative else (ACC[:, 1, :] if n == 5 else SCR[:, 0, :]).rearrange(
                    "p (t d) -> p t d", d=D)
                last = v.tensor_tensor(x[:], x[:], src, ALU.subtract if negative else ALU.add)
                last.then_inc(sem("x_done" if n < 5 else "y_done"), 1)
                if n < 5:
                    dve.wait_ge(sem("x_done"), n + 1)

            def repeat(f, srcs):
                for which, src in srcs:
                    w = WR[f, which][:].rearrange("p (h r d) -> p h r d", h=16, r=4)
                    v.memset(w[:, :, 3, :], 0.0)
                    for r in range(3):
                        last = v.tensor_copy(w[:, :, r, :], src.rearrange("p (h d) -> p h d", h=16))
                last.then_inc(sem("wr_done"), 1)

            dve.wait_ge(sem("x_in"), 16)
            layer_norm(0)
            dve.wait_ge(sem("cst_in"), 16)
            dve.wait_ge(sem("wa_in"), 48)
            repeat("attn0", (("q", wa["q"][:]), ("k", wa["k"][:])))
            run_units(A0)
            residual(0, also=xn)

            layer_norm(1)
            run_units(X0)
            dve.wait_ge(sem("cross0_w_in"), 16 * 5)
            residual(1, bias=bias_out["cross0"], negative=True)

            layer_norm(2)
            dve.wait_ge(sem("wm_in"), 48)
            repeat("mixer", (("q", wqkv[:, 0:D]), ("k", wqkv[:, D:2 * D])))
            then(v.tensor_tensor(room(2)[:, 0:D], qg[:], qg[:], ALU.mult))
            then(v.tensor_reduce(gn[:, 0, :], room(2)[:, 0:D].rearrange("p (h d) -> p h d", d=8), AX, ALU.add))
            dve.wait_ge(sem("qsq_done"), 1)
            v.tensor_reduce(n2[:], room(1).rearrange("p (a d) -> p a d", d=8), AX, ALU.add).then_inc(sem("norms2"), 1)
            then(v.tensor_tensor(room(0).rearrange("p (t c) -> p t c", t=NT), SCR[:, 0, :].rearrange("p (t c) -> p t c", t=NT),
                                 qg[:].unsqueeze(1).to_broadcast([P, NT, D]), ALU.mult))
            then(v.tensor_reduce(dot[:], room(0).rearrange("p (a d) -> p a d", d=8), AX, ALU.add))
            dve.wait_ge(sem("norms"), 2)
            then(v.reciprocal(n2[:], n2[:]))
            then(v.reciprocal(gn[:, 1, :], gn[:, 0, :]))
            then(v.tensor_tensor(dot[:], dot[:], n2[:], ALU.mult))
            dot3 = dot[:].rearrange("p (t h) -> p t h", t=NT)
            then(v.tensor_tensor(dot3, dot3, gn[:, 1, :].unsqueeze(1).to_broadcast([P, NT, H16]), ALU.mult))
            then(v.tensor_reduce(sim[:], dot3, AX, ALU.add))
            v.tensor_scalar(sim[:], sim[:], 1.0 / H16, None, ALU.mult).then_inc(sem("sim_done"), 1)
            dve.wait_ge(sem("simrow_ready"), 1)
            sims = ACC[0:1, 0, :].rearrange("p (b s) -> p b s", b=B)
            for i, op in enumerate((ALU.min, ALU.max)):
                last = v.tensor_reduce(ext[:, i:i + 1], sims[:, :, REG:S], mybir.AxisListType.XY, op)
            then(last)
            then(v.tensor_tensor(ext[:, 2:3], ext[:, 1:2], ext[:, 0:1], ALU.subtract))
            then(v.reciprocal(ext[:, 3:4], ext[:, 2:3]))
            then(v.tensor_scalar(simrow[:], sims, ext[:, 0:1], ext[:, 3:4], ALU.subtract, ALU.mult))
            pos = cls_q[:, 0, :, :]
            then(v.tensor_scalar(pos, simrow[:], 0.9, None, ALU.is_gt))
            v.tensor_scalar(cls_q[:, 1, :, :], pos, -1.0, 1.0, ALU.mult, ALU.add)
            v.tensor_scalar(cls_k[:, 0, :, :], pos, BIG, -BIG, ALU.mult, ALU.add)
            then(v.tensor_scalar(cls_k[:, 1, :, :], pos, -BIG, None, ALU.mult))
            v.memset(cls_q[:, 0, :, 0:REG], 1.0)
            v.memset(cls_q[:, 1, :, 0:REG], 0.0)
            then(v.memset(cls_k[:, 0, :, 0:REG], 0.0))
            v.memset(cls_k[:, 1, :, 0:REG], 0.0).then_inc(sem("cls_done"), 1)
            dve.wait_ge(sem("qxh_done"), 1)
            then(v.scalar_tensor_tensor(qxn[:], qxh[:], col(M_NQ), SCR[:, 1, 0:NR], ALU.mult, ALU.add))
            for j in range(4):
                last = v.tensor_scalar(Qx[:, :, :, j, :].rearrange("p b u r -> p (b u) r"),
                                       qxn[:].rearrange("p (a r) -> p a r", r=REG), col(M_BLK + j), None, ALU.mult)
            last.then_inc(sem("qx_done"), 1)
            run_units(F0)
            dve.wait_ge(sem("norm_done"), F0.chunk0 // 2 + 8)
            for i in range(2):
                wait_free(dve, "mixer", "rz", 0, i)
            for b in range(B):
                z = zt[0:REG, 2 * b, :, :].rearrange("p (u j) d -> p u (j d)", u=4)
                last = v.scalar_tensor_tensor(z, z, 0.5, zreg[:].rearrange(
                    "p (u b j) d -> p u b (j d)", u=4, b=B)[:, :, b, :], ALU.mult, ALU.add)
            last.then_inc(sem("regs_merged"), 1)
            residual(2, bias=bias_out["mixer"])

            layer_norm(3)
            dve.wait_ge(sem("wd_in"), 16 * 8)
            heads = lambda r: r.rearrange("p (a d) -> p a d", d=8)
            over = lambda r: r.unsqueeze(2).to_broadcast([P, NT * H16, 8])
            for i in range(2):
                dve.wait_ge(sem("d_sq"), i + 1)
                v.tensor_reduce(kqn[:, i, :], heads(room(i)), AX, ALU.add).then_inc(sem("d_n2"), 1)
            dve.wait_ge(sem("d_ebeta"), 1)
            then(v.tensor_scalar(beta[:], beta[:], 1.0, None, ALU.add))
            then(v.reciprocal(beta[:], beta[:]))
            dve.wait_ge(sem("d_root"), 1)
            then(v.tensor_scalar(kqn[:], kqn[:], 1e-12, None, ALU.max))
            then(v.reciprocal(kqn[:], kqn[:]))
            for i in range(2):
                last = v.tensor_tensor(heads(room(4 + i)), heads(SCR[:, i, :]), over(kqn[:, i, :]), ALU.mult)
                last.then_inc(sem("d_token"), 1)
            dve.wait_ge(sem("d_token"), 1)
            v.scalar_tensor_tensor(heads(room(14)), heads(room(4)), -1.0, over(beta[:]), ALU.mult, ALU.mult)\
                .then_inc(sem("d_token"), 1)
            dve.wait_ge(sem("d_proj"), 4)
            v.tensor_tensor(heads(room(15)), heads(SCR[:, 2, :]), over(beta[:]), ALU.mult).then_inc(sem("d_token"), 1)
            for i in range(2):
                dve.wait_ge(sem("d_high"), i + 1)
                v.tensor_tensor(d_half(i, 1), WORK[:, i, :], d_half(i, 0), ALU.subtract).then_inc(sem("d_split"), 1)
            gate, kb, vb = room(3), room(2), room(1)
            dve.wait_ge(sem("d_egate"), 3)
            v.tensor_tensor(gate, gate, ACC[:, 0, :], ALU.mult).then_inc(sem("d_gate"), 1)

            def recur(j):
                dve.wait_ge(sem("d_decay"), j + 1)
                if j >= 1:
                    dve.wait_ge(sem("d_prod"), j)
                for b in range(B):
                    ts = slice(b * S, (b + 1) * S)
                    last = v.tensor_tensor_scan(room(11)[:, ts], room(8 + j % 2)[:, ts], room(6 + j % 2)[:, ts],
                                                0.0, ALU.mult, ALU.add)
                    if b == 0:
                        last.then_inc(sem("d_scan"), 1)
                last.then_inc(sem("d_scan"), 1)
                dve.wait_ge(sem("d_scan"), 2 * j + 2)
                if j >= 2:
                    dve.wait_ge(sem("d_sum"), max(1, j - 2))
                dve.wait_ge(sem("d_spread_q"), j + 1)
                v.tensor_tensor(room(12 + j % 2), room(11), SCR[:, 2 + j % 2, :], ALU.mult).then_inc(sem("d_prod"), 1)

            dve.wait_ge(sem("d_terms"), 2)
            for j in range(8):
                dve.wait_ge(sem("d_spread_k"), j + 1)
                v.tensor_tensor(room(8 + j % 2), SCR[:, j % 2, :], kb, ALU.mult).then_inc(sem("d_kk"), 1)
                v.tensor_tensor(room(6 + j % 2), SCR[:, j % 2, :], vb, ALU.mult).then_inc(sem("d_kfree"), 1)
                if j >= 1:
                    dve.wait_ge(sem("d_kfree"), j)
                    recur(j - 1)
            dve.wait_ge(sem("d_kfree"), 8)
            recur(7)
            dve.wait_ge(sem("d_o_ready"), 1)
            variance(lambda t: WORK[:, 1, t * P:(t + 1) * P], None, "d_var")
            dve.wait_ge(sem("d_rstd"), 1)
            refine()
            y = room(1)
            y3 = y.rearrange("p (t d) -> p t d", t=NT)
            for t in range(NT):
                last = v.tensor_scalar(y[:, t * P:(t + 1) * P], WORK[:, 1, t * P:(t + 1) * P], mv[:, t, 0:1],
                                       rstd[:, t:t + 1], ALU.subtract, ALU.mult)
            then(last)
            dve.wait_ge(sem("gates_set"), 2)
            then(v.tensor_tensor(y, y, room(4), ALU.mult))
            v.tensor_tensor(y, y, room(5), ALU.add).then_inc(sem("d_y"), 1)
            residual(3)

            layer_norm(4)
            run_units(Y1)
            dve.wait_ge(sem("cross1_w_in"), 16 * 5)
            residual(4, bias=bias_out["cross1"], negative=True)

            layer_norm(5)
            dve.wait_ge(sem("xnT_done"), 6)
            v.tensor_tensor(hi[:, 1, :], SCR[:, 1, :], hi[:, 0, :], ALU.subtract).then_inc(sem("x_split"), 1)
            variance(lambda t: room(2 * t), "gelu_done", "h_var")
            dve.wait_ge(sem("h_rstd"), 1)
            refine()
            for t in range(NT):
                h = room(2 * t + 1)
                then(v.tensor_scalar(h, room(2 * t), mv[:, t, 0:1], rstd[:, t:t + 1], ALU.subtract, ALU.mult))
                v.tensor_tensor(h, h, lnw1[:], ALU.mult).then_inc(sem("h_scaled"), 1)
                if t >= 2:
                    split_h(dve, v, t - 2)
            for t in (NT - 2, NT - 1):
                split_h(dve, v, t)
            residual(5)


NAMES = {
    "x": "x", "ctx": "ctx_768",
    "a_Wq": "L0_attn_Wq", "a_Wk": "L0_attn_Wk", "a_Wv": "L0_attn_Wv", "a_Wo": "L0_attn_Wout",
    "c0_Wq": "L0_xattn_Wq", "c0_Wk": "L0_xattn_Wk", "c0_Wv": "L0_xattn_Wv", "c0_Wo": "L0_xattn_Wout",
    "c0_bo": "L0_xattn_bout",
    "m_g": "L0_ffn_g_info", "m_Wqkv": "L0_ffn_W_qkv", "m_Wo": "L0_ffn_W_proj", "m_bo": "L0_ffn_b_proj",
    "d_Wq": "L1_attn_Wq", "d_Wk": "L1_attn_Wk", "d_Wv": "L1_attn_Wv", "d_Wbeta": "L1_attn_Wbeta",
    "d_Wg": "L1_attn_Wg", "d_Wo": "L1_attn_Wout", "d_lng": "L1_attn_ln_g", "d_lnb": "L1_attn_ln_b",
    "c1_Wq": "L1_xattn_Wq", "c1_Wk": "L1_xattn_Wk", "c1_Wv": "L1_xattn_Wv", "c1_Wo": "L1_xattn_Wo",
    "c1_bo": "L1_xattn_bo",
    "f_Wfc": "L1_ffn_W_fc", "f_lnw": "L1_ffn_ln_w", "f_lnb": "L1_ffn_ln_b", "f_Wpj": "L1_ffn_W_proj",
}


def kernel(**inputs):
    import numpy as _np
    import concourse.bacc as _bacc
    from concourse import mybir as _mybir
    from concourse.bass_utils import run_bass_kernel_spmd as _run

    nc = _bacc.Bacc("TRN2", target_bir_lowering=False, num_devices=1)
    arrays, aps = {}, {}
    for name in INPUTS:
        a = _np.ascontiguousarray(inputs[NAMES[name]])
        arrays[f"in_{name}_dram"] = a
        aps[name] = nc.dram_tensor(f"in_{name}_dram", a.shape, _mybir.dt.from_np(a.dtype), kind="ExternalInput").ap()
    consts = []
    for name, a in zip(("const32", "const16"), constants()):
        arrays[f"in_{name}_dram"] = a
        consts.append(nc.dram_tensor(f"in_{name}_dram", a.shape, _mybir.dt.from_np(a.dtype), kind="ExternalInput").ap())
    out = nc.dram_tensor("out_0_dram", (B, S, D), _mybir.dt.float32, kind="ExternalOutput").ap()
    decoder(nc, aps, *consts, out)
    r = _run(nc, [arrays], core_ids=[0])
    return r.results[0]["out_0_dram"]
```
